# Optimizing a Trainium2 kernel written in Bass

```python
import numpy as np
import jax
import jax.numpy as jnp

def _softmax(x, axis=-1):
    return jax.nn.softmax(x, axis=axis)

def _gelu(x):
    return jax.nn.gelu(x, approximate=True)

def _silu(x):
    return jax.nn.silu(x)

def _sigmoid(x):
    return jax.nn.sigmoid(x)

def _layernorm(x, axis=-1, eps=1e-05):
    m = jnp.mean(x, axis=axis, keepdims=True)
    v = jnp.var(x, axis=axis, keepdims=True)
    return (x - m) / jnp.sqrt(v + eps)

def _scatter_add(tgt, idx, src, axis=0):
    return tgt.at[idx].add(src)

def _segment_sum(src, seg, n):
    return jax.ops.segment_sum(src, seg, n)
kernel_name = 'mk_seq_preln_d1_jaxref_r8_8ba3ef'

def setup_inputs(seed: int=0):
    np.random.seed(seed)
    _w = jnp.asarray

    def _L0_attn_setup():
        import jax, jax.numpy as jnp
        import numpy as np
        B, S, IN_DIM, D_MODEL, NUM_HEADS = (4, 256, 128, 128, 16)
        HEAD_DIM = D_MODEL // NUM_HEADS
        CAUSAL = True
        NEG = -9000000000000000.0

        def _xavier(key, shape):
            fan_out, fan_in = shape
            limit = (6.0 / (fan_in + fan_out)) ** 0.5
            return jax.random.uniform(key, shape, jnp.float32, -limit, limit)
        key = jax.random.key(seed)
        ks = jax.random.split(key, 5)
        x = jax.random.normal(ks[0], (B, S, IN_DIM), jnp.float32)
        Wq = _xavier(ks[1], (D_MODEL, IN_DIM))
        Wk = _xavier(ks[2], (D_MODEL, IN_DIM))
        Wv = _xavier(ks[3], (D_MODEL, IN_DIM))
        Wo = _xavier(ks[4], (D_MODEL, D_MODEL))
        bq = jnp.zeros((D_MODEL,), jnp.float32)
        bk = jnp.zeros((D_MODEL,), jnp.float32)
        bv = jnp.zeros((D_MODEL,), jnp.float32)
        bo = jnp.zeros((D_MODEL,), jnp.float32)
        return {'x': x, 'Wq': Wq, 'bq': bq, 'Wk': Wk, 'bk': bk, 'Wv': Wv, 'bv': bv, 'Wo': Wo, 'bo': bo}
    _L0_attn_in = _L0_attn_setup()

    def _L0_ffn_setup():
        import jax, jax.numpy as jnp
        import numpy as np
        D_MODEL, FF_DIM = (128, 256)
        N_SHARED, N_ROUTED, TOP_K = (1, 8, 2)
        BATCH, SEQ = (2, 256)
        key = jax.random.key(seed)
        ks = jax.random.split(key, 8)
        init = lambda k, shape: jax.random.normal(k, shape, jnp.float32) * 0.02
        x = jax.random.normal(ks[0], (BATCH, SEQ, D_MODEL), jnp.float32)
        Wg = init(ks[1], (D_MODEL, N_ROUTED))
        Ws1 = init(ks[2], (D_MODEL, FF_DIM))
        Ws3 = init(ks[3], (D_MODEL, FF_DIM))
        Ws2 = init(ks[4], (FF_DIM, D_MODEL))
        We1 = init(ks[5], (N_ROUTED, D_MODEL, FF_DIM))
        We3 = init(ks[6], (N_ROUTED, D_MODEL, FF_DIM))
        We2 = init(ks[7], (N_ROUTED, FF_DIM, D_MODEL))
        return {'x': x, 'Wg': Wg, 'Ws1': Ws1, 'Ws3': Ws3, 'Ws2': Ws2, 'We1': We1, 'We3': We3, 'We2': We2}
    _L0_ffn_in = _L0_ffn_setup()
    _d = {'L0_attn_x': _L0_attn_in['x'], 'L0_attn_Wq': _L0_attn_in['Wq'], 'L0_attn_bq': _L0_attn_in['bq'], 'L0_attn_Wk': _L0_attn_in['Wk'], 'L0_attn_bk': _L0_attn_in['bk'], 'L0_attn_Wv': _L0_attn_in['Wv'], 'L0_attn_bv': _L0_attn_in['bv'], 'L0_attn_Wo': _L0_attn_in['Wo'], 'L0_attn_bo': _L0_attn_in['bo'], 'L0_ffn_Wg': _L0_ffn_in['Wg'], 'L0_ffn_Ws1': _L0_ffn_in['Ws1'], 'L0_ffn_Ws3': _L0_ffn_in['Ws3'], 'L0_ffn_Ws2': _L0_ffn_in['Ws2'], 'L0_ffn_We1': _L0_ffn_in['We1'], 'L0_ffn_We3': _L0_ffn_in['We3'], 'L0_ffn_We2': _L0_ffn_in['We2']}
    _x0 = _d['L0_attn_x']
    _d['L0_attn_x'] = jax.random.normal(jax.random.fold_in(jax.random.key(seed), 1), (4, 1024, 128), dtype=_x0.dtype)
    del _x0
    return _d

def reference(L0_attn_x, L0_attn_Wq, L0_attn_bq, L0_attn_Wk, L0_attn_bk, L0_attn_Wv, L0_attn_bv, L0_attn_Wo, L0_attn_bo, L0_ffn_Wg, L0_ffn_Ws1, L0_ffn_Ws3, L0_ffn_Ws2, L0_ffn_We1, L0_ffn_We3, L0_ffn_We2):

    def _L0_attn_ref(x, Wq, bq, Wk, bk, Wv, bv, Wo, bo):
        import jax, jax.numpy as jnp
        import numpy as np
        B, S, IN_DIM, D_MODEL, NUM_HEADS = (4, 256, 128, 128, 16)
        HEAD_DIM = D_MODEL // NUM_HEADS
        CAUSAL = True
        NEG = -9000000000000000.0

        def _xavier(key, shape):
            fan_out, fan_in = shape
            limit = (6.0 / (fan_in + fan_out)) ** 0.5
            return jax.random.uniform(key, shape, jnp.float32, -limit, limit)
        batch, seq, _ = x.shape
        q = x @ Wq.T + bq
        k = x @ Wk.T + bk
        v = x @ Wv.T + bv

        def split(t):
            return t.reshape(batch, seq, NUM_HEADS, HEAD_DIM).transpose(0, 2, 1, 3)
        q, k, v = (split(q), split(k), split(v))
        scores = jnp.einsum('bhqd,bhkd->bhqk', q, k) / jnp.sqrt(jnp.float32(HEAD_DIM))
        if CAUSAL:
            mask = jnp.tril(jnp.ones((seq, seq), bool))
            scores = jnp.where(mask, scores, jnp.float32(NEG))
        attn = jax.nn.softmax(scores, axis=-1)
        out = jnp.einsum('bhqk,bhkd->bhqd', attn, v)
        out = out.transpose(0, 2, 1, 3).reshape(batch, seq, D_MODEL)
        return out @ Wo.T + bo

    def _L0_ffn_ref(x, Wg, Ws1, Ws3, Ws2, We1, We3, We2):
        import jax, jax.numpy as jnp
        import numpy as np
        D_MODEL, FF_DIM = (128, 256)
        N_SHARED, N_ROUTED, TOP_K = (1, 8, 2)
        BATCH, SEQ = (2, 256)
        B, S, d = x.shape
        E = Wg.shape[1]
        xf = x.reshape(-1, d)
        T = xf.shape[0]
        gates = jax.nn.sigmoid(xf @ Wg)
        vals, idx = jax.lax.top_k(gates, TOP_K)
        vals = vals / vals.sum(axis=-1, keepdims=True)
        w = jnp.zeros((T, E), x.dtype).at[jnp.arange(T)[:, None], idx].add(vals)
        shared = jax.nn.silu(xf @ Ws1) * (xf @ Ws3) @ Ws2
        h = jax.nn.silu(jnp.einsum('td,edf->tef', xf, We1)) * jnp.einsum('td,edf->tef', xf, We3)
        routed = jnp.einsum('tef,efd,te->td', h, We2, w)
        out = (shared + routed) / (N_SHARED + TOP_K)
        return out.reshape(B, S, d)
    x = L0_attn_x
    x = x + _L0_attn_ref(_layernorm(x, axis=-1), L0_attn_Wq, L0_attn_bq, L0_attn_Wk, L0_attn_bk, L0_attn_Wv, L0_attn_bv, L0_attn_Wo, L0_attn_bo)
    x = x + _L0_ffn_ref(_layernorm(x, axis=-1), L0_ffn_Wg, L0_ffn_Ws1, L0_ffn_Ws3, L0_ffn_Ws2, L0_ffn_We1, L0_ffn_We3, L0_ffn_We2)
    return x

_drawn_inputs = setup_inputs


def setup_inputs(seed=0):
    import zlib

    import numpy as np

    out = dict(_drawn_inputs(seed))
    spreads = {'L0_attn_bq': (0.0, 0.664),
     'L0_attn_bk': (0.0, 0.8),
     'L0_attn_bv': (0.0, 0.1),
     'L0_attn_bo': (0.0, 0.1)}
    factors = {'L0_ffn_Wg': 8.0,
     'L0_ffn_Ws1': 8.0,
     'L0_ffn_Ws3': 8.0,
     'L0_ffn_Ws2': 8.0,
     'L0_ffn_We1': 8.0,
     'L0_ffn_We3': 8.0,
     'L0_ffn_We2': 8.0}
    for name, (base, spread) in spreads.items():
        noise = np.random.default_rng([zlib.crc32(name.encode()), seed]).standard_normal(out[name].shape)
        drawn = base * np.exp(spread * noise) if base else spread * noise
        out[name] = jnp.asarray(drawn.astype(out[name].dtype))
    for name, factor in factors.items():
        out[name] = (out[name] * factor).astype(out[name].dtype)
    return out
```

```python
from contextlib import ExitStack

import concourse.bass as bass
from concourse import mybir

F32 = mybir.dt.float32
F32R = mybir.dt.float32r
BF16 = mybir.dt.bfloat16
ACT = mybir.ActivationFunctionType
ALU = mybir.AluOpType
AX = mybir.AxisListType.X

P = 128
D = 128
B, S = 4, 1024
H, DH = 16, 8
GH = 4
GB = H // GH
NG = B * GB
ROWS = P // GH
PARTS = 3 * DH
T = B * S // P
TB = S // P
HALF = S // 2
SC = 4
FF = 256
NE = 8
UNITS = NE + 1
EPS = 1e-5
MASKED = -1.0e30
SCALE = float(DH) ** -0.5

TILES = [
    [(0, 0, 512), (0, 512, 512)],
    [(7, 0, 128), (1, 128, 384), (1, 512, 512)],
    [(6, 0, 256), (2, 256, 256), (2, 512, 512)],
    [(5, 0, 384), (3, 384, 128), (3, 512, 512)],
]
DIAGONALS = [[0], [0, 128], [0, 256], [0, 384], [0, 512]]
NTYPE = 5
STEPS = 4 * GH + GH // 2
TYPE_END = [4, 8, 12, 16, 18]


def query_of(j, c):
    return c + (S - P * (8 - j) if j > 4 else 0)


def step_pieces(st):
    if st < 16:
        t, h = divmod(st, GH)
        return [(h, j, c, w, query_of(j, c)) for j, c, w in TILES[t]]
    h = 2 * (st - 16)
    return [(h, 4, 512, 512, 512), (h + 1, 4, 0, 512, 512)]


def values_chunks():
    cuts = {512: (256, 256)}
    order = [[0, 1], [1, 0, 2], [1, 0, 2], [1, 0, 2]]
    out = []
    for t, pieces in enumerate(TILES):
        for j, c, w in [pieces[i] for i in order[t]]:
            for part in cuts.get(w, (w,)):
                out.append((t, j, c, part, query_of(j, c)))
                c += part
    return out + [(4, 4, c, 256, 512 + c) for c in (0, 256)]


def max_segments():
    out = []
    for i in range(S // ROWS):
        n = ROWS * (i + 1)
        if n <= 512:
            out.append((i, 0, n, i, True))
        else:
            out.append((i, 0, n // 2, i, False))
            out.append((i, n // 2, n // 2, i + 16, True))
    return out


SEGMENTS = max_segments()
NSEG = len(SEGMENTS)
CHUNKS = values_chunks()
LAG = 4
AHEAD = 2
MAX_AT = 7
LOWER_LAST = max(i for i, (t, j, c, w, q) in enumerate(CHUNKS) if q < HALF)


def segments_by_chunk():
    cost = [65 + s[2] / 0.96 for s in SEGMENTS]
    total, at, out = sum(cost), 0.0, [[] for _ in range(STEPS)]
    for n, c in enumerate(cost):
        u = MAX_AT + min(int(at / total * STEPS), STEPS - 1)
        out[u % STEPS].append((2 if u < STEPS else 1, n))
        at += c
    return out


SEGS_BY_CHUNK = segments_by_chunk()


def layer_kernel(nc, x, Wq, bq, Wk, bk, Wv, bv, Wo, bo, Wg, Ws1, Ws3, Ws2, We1, We3, We2, out):
    q_parts = nc.dram_tensor("q_parts", (B, H, PARTS + 2, S), F32).ap()
    k_parts = nc.dram_tensor("k_parts", (B, H, PARTS, S), F32).ap()
    heads_out = nc.dram_tensor("heads_out", (NG, P, S), F32).ap()
    x_tiles = x.rearrange("b (n p) d -> p (b n) d", p=P)
    out_tiles = out.rearrange("b (n p) d -> p (b n) d", p=P)
    with ExitStack() as ctx:
        def sb(name, shape, dt=F32, where=ctx):
            return where.enter_context(nc.sbuf_tensor(name, shape, dt))

        ident = sb("ident", [P, P])
        x_all = sb("x_all", [P, T, D])
        woT = sb("woT", [P, D])
        row_consts = sb("row_consts", [P, 2, D])
        wg = sb("wg", [P, NE])
        neg_half = sb("neg_half", [P, TB])
        with ExitStack() as attn:
            keep = dict(
                ident=ident, x_all=x_all, woT=woT, row_consts=row_consts, neg_half=neg_half, wg=wg,
                ident_bf=sb("ident_bf", [P, P], BF16, attn),
                mask_bf=sb("mask_bf", [P, ROWS], BF16, attn),
                v_all=sb("v_all", [P, NG, TB, GH * DH], F32, attn),
                q_diag=[sb(f"q_diag{i}", [P, S // ROWS, GH, ROWS], F32R, attn) for i in range(3)],
                k_rows=[sb(f"k_rows{i}", [P, S], F32R, attn) for i in range(3)],
                v_one=[sb(f"v_one{i}", [P, TB, GH, ROWS], F32, attn) for i in range(3)],
            )
            prepare(nc, keep, x_tiles, Wq, bq, Wk, bk, Wv, bv, Wo, bo, Wg, q_parts, k_parts)
            attention(nc, keep, q_parts, k_parts, heads_out)
        feed_forward(nc, keep, heads_out, Ws1, Ws3, Ws2, We1, We3, We2, out_tiles)


def prepare(nc, keep, x_tiles, Wq, bq, Wk, bk, Wv, bv, Wo, bo, Wg, q_parts, k_parts):
    ident, x_all = keep["ident"], keep["x_all"]
    with ExitStack() as ctx:
        def sb(name, shape, dt=F32):
            return ctx.enter_context(nc.sbuf_tensor(name, shape, dt))

        def pair(name, shape, dt=F32):
            return [sb(f"{name}{s}", shape, dt) for s in range(2)]

        def sem(name):
            return ctx.enter_context(nc.semaphore(name))

        def sems(name):
            return [sem(f"{name}{s}") for s in range(2)]

        w_raw = sb("w_raw", [P, 4, D])
        w_hi = sb("w_hi", [P, 3, D], F32R)
        w_lo = sb("w_lo", [P, 3, D], F32R)
        bias_cols = sb("bias_cols", [P, 2])
        zeros = sb("zeros", [P, S])
        ones = sb("ones", [8, S])
        stats = sb("stats", [P, TB, 6])
        mean_var = sb("mean_var", [P, TB, 2])
        var_eps = sb("var_eps", [P, TB])
        rstd = sb("rstd", [P, TB])
        xn = pair("xn", [P, SC, D])
        xh = pair("xh", [P, SC * P], F32R)
        xl = pair("xl", [P, SC * P], F32R)
        qf, kf = pair("qf", [P, HALF]), pair("kf", [P, HALF])
        qh, kh = pair("qh", [P, HALF], F32R), pair("kh", [P, HALF], F32R)
        ql, kl = pair("ql", [P, HALF], F32R), pair("kl", [P, HALF], F32R)
        ps = ctx.enter_context(nc.psum_tensor("ps_prep", [P, 8, 512], F32))

        x_in, w_in, b_in, mat_in = sem("x_in"), sem("w_in"), sem("b_in"), sem("mat_in")
        consts, ident_ready, wT_done, w_hi_done = sem("consts"), sem("ident_ready"), sem("wT_done"), sem("w_hi_done")
        w_ready, fills, pool_fills = sem("w_ready"), sem("fills"), sem("pool_fills")
        stats_step, mv_done, eps_done, rstd_done = sem("stats_step"), sem("mv_done"), sem("eps_done"), sem("rstd_done")
        xn_done, xT_done, xh_done, xl_done = sems("xn_done"), sems("xT_done"), sems("xh_done"), sems("xl_done")
        q_done, k_done, v_done = sems("q_done"), sems("k_done"), sems("v_done")
        qf_done, kf_done, qh_done, kh_done = sems("qf_done"), sems("kf_done"), sems("qh_done"), sems("kh_done")
        ql_done, kl_done, v_out = sems("ql_done"), sems("kl_done"), sems("v_out")
        stored, rows_out = sems("stored"), sem("rows_out")
        passed = sem("passed0")
        block = ctx.enter_context(nc.Block())
        FILLS = 12

        @block.sync
        def _(sp):
            sp.dma_start(x_all[:, 0:TB, :], x_tiles[:, 0:TB, :]).then_inc(x_in, 16)
            for n, w in enumerate((Wq, Wk, Wv, Wo)):
                sp.dma_start(w_raw[:, n, :], w).then_inc(w_in, 16)
            for n, b in enumerate((bq, bk)):
                sp.dma_start(bias_cols[:, n:n + 1], b.rearrange("(p a) -> p a", a=1)).then_inc(b_in, 16)
            for n, b in enumerate((bv, bo)):
                sp.dma_start(keep["row_consts"][:, n, :], b.rearrange("(a n) -> a n", a=1).to_broadcast([P, D])).then_inc(b_in, 16)
            sp.dma_start(keep["wg"][:], Wg).then_inc(b_in, 16)
            sp.wait_ge(x_in, 16)
            for b in range(1, B):
                sp.dma_start(x_all[:, TB * b:TB * b + TB, :], x_tiles[:, TB * b:TB * b + TB, :]).then_inc(x_in, 16)
                sp.wait_ge(x_in, 16 * (b + 1))
            sp.wait_ge(pool_fills, 2)
            sp.dma_start(q_parts.rearrange("b h r c -> (b h) r c")[:, PARTS:PARTS + 2, :], zeros[:]).then_inc(rows_out, 16)
            sp.wait_ge(pool_fills, FILLS)
            for i in range(3):
                for h in range(GH):
                    r = ROWS * h + PARTS
                    sp.dma_start(keep["k_rows"][i][r:r + 2, :].bitcast(F32), ones[0:2, :]).then_inc(rows_out, 16)
            with sp.Fori(0, B) as b:
                for s in range(2):
                    cols = slice(HALF * s, HALF * s + HALF)
                    qd = q_parts[bass.ds(b, 1), :, :, cols].rearrange("b h r c -> (b h) r c")
                    kd = k_parts[bass.ds(b, 1), :, :, cols].rearrange("b h r c -> (b h) r c")
                    sp.wait_ge(qh_done[s], b + 1)
                    sp.dma_start(qd[:, 0:DH, :], qh[s][:].bitcast(F32)).then_inc(stored[s], 16)
                    sp.dma_start(qd[:, 2 * DH:3 * DH, :], qh[s][:].bitcast(F32)).then_inc(stored[s], 16)
                    sp.wait_ge(kh_done[s], b + 1)
                    sp.dma_start(kd[:, 0:DH, :], kh[s][:].bitcast(F32)).then_inc(stored[s], 16)
                    sp.dma_start(kd[:, DH:2 * DH, :], kh[s][:].bitcast(F32)).then_inc(stored[s], 16)
                    sp.wait_ge(ql_done[s], b + 1)
                    sp.dma_start(qd[:, DH:2 * DH, :], ql[s][:].bitcast(F32)).then_inc(stored[s], 16)
                    sp.wait_ge(kl_done[s], b + 1)
                    sp.dma_start(kd[:, 2 * DH:3 * DH, :], kl[s][:].bitcast(F32)).then_inc(stored[s], 16)
            for s in range(2):
                sp.wait_ge(stored[s], 16 * 6 * B)
            sp.wait_ge(rows_out, 16 * (1 + 3 * GH))

        @block.gpsimd
        def _(pool):
            mask, identb = keep["mask_bf"], keep["ident_bf"]
            nc.gpsimd.memset(ident[:], 0.0).then_inc(consts, 1)
            nc.gpsimd.memset(identb[:], 0.0).then_inc(consts, 1)
            nc.gpsimd.memset(mask[:], 0.0).then_inc(consts, 1)
            pool.wait_ge(consts, 3)
            for m in (ident, identb):
                nc.gpsimd.affine_select(out=m[:], in_=m[:], compare_op=ALU.not_equal, fill=1.0, base=0,
                                        pattern=[[-1, P]], channel_multiplier=1).then_inc(ident_ready, 1)
            pool.wait_ge(ident_ready, 2)
            for h in range(GH):
                m = mask[ROWS * h:ROWS * h + ROWS, :]
                nc.gpsimd.affine_select(out=m, in_=m, compare_op=ALU.is_ge, fill=MASKED, base=0,
                                        pattern=[[-1, ROWS]], channel_multiplier=1).then_inc(ident_ready, 1)
                pool.wait_ge(ident_ready, 3 + h)
            nc.gpsimd.memset(keep["neg_half"][:], -0.5).then_inc(consts, 1)
            nc.gpsimd.memset(zeros[:], 0.0).then_inc(pool_fills, 1)
            nc.gpsimd.memset(ones[:], 1.0).then_inc(pool_fills, 1)
            for i in range(3):
                nc.gpsimd.memset(keep["v_one"][i][:], 0.0).then_inc(pool_fills, 1)
                nc.gpsimd.memset(keep["k_rows"][i][:].bitcast(F32), 0.0).then_inc(pool_fills, 1)
            pool.wait_ge(pool_fills, 8)
            for i in range(3):
                nc.gpsimd.memset(keep["v_one"][i][:, :, :, DH:DH + 1], 1.0).then_inc(pool_fills, 1)
            nc.gpsimd.memset(keep["q_diag"][2][:].bitcast(F32), 0.0).then_inc(pool_fills, 1)
            with pool.Fori(0, B) as b:
                pool.wait_ge(mv_done, b + 1)
                pool.sem_inc(passed, 1)
                nc.gpsimd.tensor_scalar(var_eps[:], mean_var[:, :, 1], EPS, 0.0, ALU.add, ALU.add).then_inc(eps_done, 1)
                pool.wait_ge(eps_done, b + 1)
                nc.gpsimd.tensor_tensor(rstd[:], var_eps[:], keep["neg_half"][:], ALU.pow).then_inc(rstd_done, 1)

        @block.vector
        def _(dve):
            w_psum = ps[:, 0, :].rearrange("p (n d) -> p n d", n=4)
            dve.wait_ge(w_hi_done, 2)
            nc.vector.tensor_tensor(w_lo[:], w_psum[:, 0:3, :], w_hi[:].bitcast(F32), ALU.subtract).then_inc(w_ready, 1)
            for i in range(2):
                nc.vector.memset(keep["q_diag"][i][:].bitcast(F32), 0.0).then_inc(fills, 1)
            dve.wait_ge(b_in, 16 * 5)
            with dve.Fori(0, B) as b:
                dve.wait_ge(x_in, 16 * b + 16)
                dve.sem_inc(passed, 1)
                for t in range(TB):
                    nc.vector.bn_stats(stats[:, t, :], x_all[:, bass.ds(TB * b + t, 1), :].rearrange("p a d -> p (a d)")).then_inc(stats_step, 1)
                for t in range(TB):
                    dve.wait_ge(stats_step, TB * b + t + 1)
                    dve.sem_inc(passed, 1)
                    ins = nc.vector.bn_aggr(mean_var[:, t, :], stats[:, t, :])
                ins.then_inc(mv_done, 1)
                dve.wait_ge(rstd_done, b + 1)
                for s in range(2):
                    dve.wait_ge(xT_done[s], b)
                    for t in range(SC):
                        n = SC * s + t
                        ins = nc.vector.tensor_scalar(xn[s][:, t, :], x_all[:, bass.ds(TB * b + n, 1), :].rearrange("p a d -> p (a d)"),
                                                      mean_var[:, n, 0:1], rstd[:, n:n + 1], ALU.subtract, ALU.mult)
                    ins.then_inc(xn_done[s], 1)
                for s in range(2):
                    dve.wait_ge(xh_done[s], b + 1)
                    nc.vector.tensor_tensor(xl[s][:], ps[:, s, :], xh[s][:].bitcast(F32), ALU.subtract).then_inc(xl_done[s], 1)
                for s in range(2):
                    dve.wait_ge(qh_done[s], b + 1)
                    dve.wait_ge(stored[s], 96 * b)
                    nc.vector.tensor_tensor(ql[s][:], qf[s][:], qh[s][:].bitcast(F32), ALU.subtract).then_inc(ql_done[s], 1)
                    dve.wait_ge(kh_done[s], b + 1)
                    nc.vector.tensor_tensor(kl[s][:], kf[s][:], kh[s][:].bitcast(F32), ALU.subtract).then_inc(kl_done[s], 1)
                    dve.wait_ge(v_done[s], b + 1)
                    src = ps[:, 6 + s, :].rearrange("p (j g c) -> p j g c", j=SC, g=GB)
                    bias = keep["row_consts"][:, 0:1, :].rearrange("p a (g c) -> p a g c", g=GB).to_broadcast([P, SC, GB, GH * DH])
                    dst = keep["v_all"][:, bass.ds(GB * b, GB), SC * s:SC * s + SC, :].rearrange("p g j c -> p j g c")
                    nc.vector.tensor_tensor(dst, src, bias, ALU.add).then_inc(v_out[s], 1)

        @block.scalar
        def _(act):
            w_psum = ps[:, 0, :].rearrange("p (n d) -> p n d", n=4)
            act.wait_ge(wT_done, 1)
            nc.scalar.activation(w_hi[:], w_psum[:, 0:3, :], ACT.Copy).then_inc(w_hi_done, 1)
            nc.scalar.activation(keep["woT"][:], w_psum[:, 3, :], ACT.Copy).then_inc(w_hi_done, 1)
            act.wait_ge(b_in, 16 * 5)
            with act.Fori(0, B) as b:
                for s in range(2):
                    act.wait_ge(xT_done[s], b + 1)
                    act.wait_ge(v_done[s], b)
                    nc.scalar.activation(xh[s][:], ps[:, s, :], ACT.Copy).then_inc(xh_done[s], 1)
                for s in range(2):
                    for full, high, f_done, h_done, mm_done, l_done, col in (
                            (qf, qh, qf_done, qh_done, q_done, ql_done, 0), (kf, kh, kf_done, kh_done, k_done, kl_done, 1)):
                        act.wait_ge(mm_done[s], b + 1)
                        act.wait_ge(l_done[s], b)
                        nc.scalar.activation(full[s][:], ps[:, 2 + 2 * col + s, :], ACT.Identity,
                                             bias=bias_cols[:, col:col + 1]).then_inc(f_done[s], 1)
                        act.wait_ge(f_done[s], b + 1)
                        act.wait_ge(stored[s], 96 * b)
                        nc.scalar.activation(high[s][:], full[s][:], ACT.Copy).then_inc(h_done[s], 1)

        @block.tensor
        def _(pe):
            pe.wait_ge(w_in, 64)
            pe.wait_ge(ident_ready, 1)
            for n in range(4):
                ins = nc.tensor.transpose(ps[:, 0, D * n:D * n + D], w_raw[:, n, :], ident[:])
            ins.then_inc(wT_done, 1)
            pe.wait_ge(w_ready, 1)
            with pe.Fori(0, B) as b:
                for s in range(2):
                    pe.wait_ge(xn_done[s], b + 1)
                    pe.wait_ge(xl_done[s], b)
                    for t in range(SC):
                        ins = nc.tensor.transpose(ps[:, s, P * t:P * t + P], xn[s][:, t, :], ident[:])
                    ins.then_inc(xT_done[s], 1)
                for s in range(2):
                    pe.wait_ge(xl_done[s], b + 1)
                    for col, mm_done, f_done in ((0, q_done, qf_done), (1, k_done, kf_done)):
                        pe.wait_ge(f_done[s], b)
                        o = ps[:, 2 + 2 * col + s, :]
                        nc.tensor.matmul(o, w_hi[:, col, :], xh[s][:], start=True, stop=False)
                        nc.tensor.matmul(o, w_hi[:, col, :], xl[s][:], start=False, stop=False)
                        nc.tensor.matmul(o, w_lo[:, col, :], xh[s][:], start=False, stop=True).then_inc(mm_done[s], 1)
                    pe.wait_ge(v_out[s], b)
                    for t in range(SC):
                        o, c = ps[:, 6 + s, P * t:P * t + P], slice(P * t, P * t + P)
                        nc.tensor.matmul(o, xh[s][:, c], w_hi[:, 2, :], start=True, stop=False)
                        nc.tensor.matmul(o, xl[s][:, c], w_hi[:, 2, :], start=False, stop=False)
                        ins = nc.tensor.matmul(o, xh[s][:, c], w_lo[:, 2, :], start=False, stop=True)
                    ins.then_inc(v_done[s], 1)


def attention(nc, keep, q_parts, k_parts, heads_out):
    q_diag, k_rows, v_one = keep["q_diag"], keep["k_rows"], keep["v_one"]
    q_flat = q_parts.rearrange("b h r c -> (b h) r c")
    k_flat = k_parts.rearrange("b h r c -> (b h) r c")
    with ExitStack() as ctx:
        def sb(name, shape, dt=F32):
            return ctx.enter_context(nc.sbuf_tensor(name, shape, dt))

        def sem(name):
            return ctx.enter_context(nc.semaphore(name))

        def sems(name):
            return [sem(f"{name}{s}") for s in range(3)]

        probs = [sb(f"probs{i}", [P, GH, S]) for i in range(3)]
        heads = [sb(f"heads{i}", [P, S]) for i in range(3)]
        partial = sb("partial", [P, 48])
        row_max = sb("row_max", [P, 32])
        neg_max = sb("neg_max", [32, 2, P], F32R)
        neg_full = sb("neg_full", [32, P])
        ps_scores = ctx.enter_context(nc.psum_tensor("ps_scores", [P, 2, 1024], F32))
        ps_max = ctx.enter_context(nc.psum_tensor("ps_max", [P, 2, 512], F32))
        ps_out = ctx.enter_context(nc.psum_tensor("ps_out", [P, 2, 512], F32))

        qk_in, max_in, heads_free = sems("qk_in"), sems("max_in"), sems("heads_free")
        scores_done, exp_done, mask_done = sem("scores_done"), sem("exp_done"), sem("mask_done")
        seg_done, seg_read, max_done, maxT_done = sem("seg_done"), sem("seg_read"), sem("max_done"), sem("maxT_done")
        neg_step, neg_done, v_ready = sem("neg_step"), sem("neg_done"), sem("v_ready")
        lower_done = sem("lower_done")
        lower_free, upper_free = sem("lower_free"), sem("upper_free")
        probs_free = sems("probs_free")
        passed = sem("passed1")
        block = ctx.enter_context(nc.Block())
        QK_IN, MAX_IN = 16 * 2 * GH, 16 * 2 * GH
        ITERS = (NG - 4) // 3
        PEELED = range(3 * ITERS, NG)


        @block.sync
        def _(sp):
            def load(n, slot):
                for h in range(GH):
                    r = ROWS * h
                    sp.dma_start(q_diag[slot][r:r + PARTS + 2, :, h, :].bitcast(F32),
                                 q_flat[bass.ds(n * GH + h, 1), :, :].rearrange("a r (i c) -> (a r) i c", c=ROWS)).then_inc(qk_in[slot], 16)
                    sp.dma_start(k_rows[slot][r:r + PARTS, :].bitcast(F32),
                                 k_flat[bass.ds(n * GH + h, 1), :, :].rearrange("a r c -> (a r) c")).then_inc(qk_in[slot], 16)

            def put_max(m, slot):
                sp.wait_ge(neg_done, m + 1)
                for h in range(GH):
                    for part in range(2):
                        r = ROWS * h + PARTS + part
                        sp.dma_start(q_diag[slot][r:r + 1, :, h, :].bitcast(F32),
                                     neg_max[:, part, ROWS * h:ROWS * h + ROWS].bitcast(F32)).then_inc(max_in[slot], 16)

            def group(n, k, loads, following):
                if loads:
                    sp.wait_ge(scores_done, STEPS * n + 1)
                    load(n + 2, (k + 2) % 3)
                if following:
                    put_max(n + 1, (k + 1) % 3)
                sp.wait_ge(lower_free, n + 2)
                sp.wait_ge(upper_free, n + 2)
                sp.dma_start(heads_out[bass.ds(n, 1), :, :].rearrange("a p c -> (a p) c"), heads[k][:]).then_inc(heads_free[k], 16)

            for k in range(3):
                sp.sem_inc(heads_free[k], 16)
            load(0, 0)
            load(1, 1)
            put_max(0, 0)
            with sp.Fori(0, ITERS) as it:
                for k in range(3):
                    group(3 * it + k, k, True, True)
            for n in PEELED:
                group(n, n % 3, n + 2 < NG, n + 1 < NG)
            for k in range(3):
                sp.wait_ge(heads_free[k], 16 * (1 + len(range(k, NG, 3))))

        @block.gpsimd
        def _(pool):
            def group(n, k):
                for st in range(STEPS):
                    t = st // GH
                    buf = probs[(5 * k + t) % 3]
                    slot = st % GH if t < 4 else st - 16
                    pool.wait_ge(exp_done, STEPS * n + st + 1)
                    pool.sem_inc(passed, 1)
                    gap, count = max(DIAGONALS[t][-1], P), len(DIAGONALS[t])
                    view = buf[:, slot, 0:gap * count].rearrange("p (a c) -> p a c", a=count)[:, :, 0:P]
                    nc.gpsimd.affine_select(out=view, in_=view, compare_op=ALU.is_ge, fill=0.0, base=0,
                                            pattern=[[0, count], [1, P]], channel_multiplier=-1).then_inc(mask_done, 1)
                    if st == 1:
                        src = keep["v_all"][:, bass.ds(n, 1), :, :].rearrange("p a j (h d) -> p (a j) h d", h=GH)
                        nc.gpsimd.tensor_copy(v_one[k][:, :, :, 0:DH], src).then_inc(v_ready, 1)

            with pool.Fori(0, ITERS) as it:
                for k in range(3):
                    group(3 * it + k, k)
            for n in PEELED:
                group(n, n % 3)

        @block.scalar
        def _(act):
            def exp_tile(n, it, k, st):
                t = st // GH
                tau = 5 * k + t
                slot = st % GH if t < 4 else st - 16
                if st in (0, 4, 8, 12, 16):
                    act.wait_ge(probs_free[tau % 3], 5 * it + tau // 3 + 1)
                act.wait_ge(scores_done, STEPS * n + st + 1)
                nc.scalar.activation(probs[tau % 3][:, slot, :], ps_scores[:, st % 2, :], ACT.Exp, scale=SCALE).then_inc(exp_done, 1)

            def copy_out(n, it, k, half, free):
                if half == 1:
                    tau = 5 * k + 4
                    act.wait_ge(probs_free[tau % 3], 5 * it + tau // 3 + 2)
                if half == 0:
                    act.wait_ge(lower_done, n + 1)
                    act.wait_ge(heads_free[k], 16 * it + 16)
                nc.scalar.activation(heads[k][:, HALF * half:HALF * half + HALF], ps_out[:, half, :], ACT.Copy).then_inc(free, 1)

            def group(n, it, k, following):
                for st in range(LAG + AHEAD, STEPS + LAG + AHEAD):
                    if st < STEPS:
                        exp_tile(n, it, k, st)
                    elif following:
                        exp_tile(n + 1, it + (k == 2), (k + 1) % 3, st - STEPS)
                    if st == STEPS + 2:
                        copy_out(n, it, k, 0, lower_free)
                    if st == STEPS + LAG:
                        copy_out(n, it, k, 1, upper_free)

            act.sem_inc(lower_free, 1)
            act.sem_inc(upper_free, 1)
            for st in range(LAG + AHEAD):
                exp_tile(0, 0, 0, st)
            with act.Fori(0, ITERS) as it:
                for k in range(3):
                    group(3 * it + k, it, k, True)
            for n in PEELED:
                group(n, n // 3, n % 3, n + 1 < NG)

        @block.vector
        def _(dve):
            def reduce_segment(m, s):
                _, _, n, col, _ = SEGMENTS[s]
                dve.wait_ge(seg_done, NSEG * m + s + 1)
                dst = row_max[:, col:col + 1] if col < 16 else partial[:, col:col + 1]
                nc.vector.reduce_max(dst, ps_max[:, s % 2, 0:n], AX).then_inc(seg_read, 1)
                if s == NSEG - 1:
                    dve.wait_ge(seg_read, NSEG * m + NSEG)
                    nc.vector.tensor_tensor(row_max[:, 16:32], partial[:, 16:32], partial[:, 32:48], ALU.max).then_inc(max_done, 1)

            def negate(m, put_before):
                if put_before is not None:
                    dve.wait_ge(*put_before)
                dve.wait_ge(maxT_done, m + 1)
                nc.vector.tensor_scalar(neg_full[:], ps_max[0:32, 0, 0:P], -1.0, None, ALU.mult).then_inc(neg_step, 1)
                dve.wait_ge(neg_step, 2 * m + 1)
                nc.vector.tensor_copy(neg_max[:, 0, :], neg_full[:]).then_inc(neg_step, 1)
                dve.wait_ge(neg_step, 2 * m + 2)
                nc.vector.tensor_tensor(neg_max[:, 1, :], neg_full[:], neg_max[:, 0, :].bitcast(F32), ALU.subtract).then_inc(neg_done, 1)

            def group(n, it, k, last):
                for u in range(STEPS):
                    if u == MAX_AT:
                        negate(n + 1, (max_in[k], MAX_IN * (it + 1)))
                    for dm, s in SEGS_BY_CHUNK[u]:
                        if dm <= last:
                            reduce_segment(n + dm, s)

            for s in range(NSEG):
                reduce_segment(0, s)
            negate(0, None)
            for u in range(MAX_AT, STEPS):
                for _, s in SEGS_BY_CHUNK[u]:
                    reduce_segment(1, s)
            with dve.Fori(0, ITERS) as it:
                for k in range(3):
                    group(3 * it + k, it, k, 2)
            for n in PEELED:
                if n + 1 < NG:
                    group(n, n // 3, n % 3, NG - 1 - n)

        @block.tensor
        def _(pe):
            def scores(st, slot):
                for h, j, c, w, q in step_pieces(st):
                    ins = nc.tensor.matmul(ps_scores[:, st % 2, c:c + w], k_rows[slot][:, P * j:P * j + P],
                                           q_diag[slot][:, q // ROWS:(q + w) // ROWS, h, :], start=True, stop=True)
                ins.then_inc(scores_done, 1)

            def segment(m, s, slot, first=False):
                i, k0, n, _, diagonal = SEGMENTS[s]
                if s == 0 and not first:
                    pe.wait_ge(neg_step, 2 * m - 1)
                if not (first and s < 2):
                    pe.wait_ge(seg_read, NSEG * m + s - 1)
                o = ps_max[:, s % 2, 0:n]
                ins = nc.tensor.matmul(o, q_diag[slot][:, i, :, :].rearrange("p h r -> p (h r)"), k_rows[slot][:, k0:k0 + n],
                                       start=True, stop=not diagonal)
                if diagonal:
                    ins = nc.tensor.matmul(ps_max[:, s % 2, n - ROWS:n], keep["ident_bf"][:], keep["mask_bf"][:],
                                           start=False, stop=True)
                ins.then_inc(seg_done, 1)

            def transpose_max(m):
                pe.wait_ge(max_done, m + 1)
                nc.tensor.transpose(ps_max[0:32, 0, 0:P], row_max[:], keep["ident"][:]).then_inc(maxT_done, 1)

            def values(n, k, u):
                t, j, c, w, q = CHUNKS[u]
                tau = 5 * k + t
                if u == 0:
                    pe.wait_ge(v_ready, n + 1)
                    pe.wait_ge(lower_free, n + 1)
                if u == 2:
                    pe.wait_ge(upper_free, n + 1)
                if u == 0 or CHUNKS[u - 1][0] != t:
                    pe.wait_ge(mask_done, STEPS * n + TYPE_END[t])
                for h in range(GH):
                    slot, c0 = (h, c) if t < 4 else (h // 2, c + HALF * (1 - h % 2))
                    ins = nc.tensor.matmul(ps_out[ROWS * h:ROWS * h + ROWS, q // HALF, q % HALF:q % HALF + w], v_one[k][:, j, h, :],
                                           probs[tau % 3][:, slot, c0:c0 + w], start=(u in (0, 2)), stop=(u in (LOWER_LAST, STEPS - 1)))
                if u == STEPS - 1 or CHUNKS[u + 1][0] != t:
                    ins.then_inc(probs_free[tau % 3], 1)
                elif u == LOWER_LAST:
                    ins.then_inc(lower_done, 1)

            def group(n, it, k, last):
                for u in range(STEPS):
                    st = u + LAG
                    segs = [(dm, s) for dm, s in SEGS_BY_CHUNK[u] if dm <= last]
                    if u == MAX_AT and last > 1:
                        pe.wait_ge(qk_in[(k + 2) % 3], QK_IN * (it + 1 + (k > 0)))
                    cut = [0, len(segs) // 3, 2 * len(segs) // 3, len(segs)]
                    if u == MAX_AT and last > 0:
                        cut[1] = cut[2] = 0
                        transpose_max(n + 1)
                    for dm, s in segs[:cut[1]]:
                        segment(n + dm, s, (k + dm) % 3)
                    if st + AHEAD < STEPS or last > 0:
                        pe.wait_ge(exp_done, STEPS * n + st + 1)
                        if st + AHEAD < STEPS:
                            scores(st + AHEAD, k)
                        else:
                            if st + AHEAD == STEPS:
                                pe.wait_ge(max_in[(k + 1) % 3], MAX_IN * (it + 1 + (k == 2)))
                            scores(st + AHEAD - STEPS, (k + 1) % 3)
                    for dm, s in segs[cut[1]:cut[2]]:
                        segment(n + dm, s, (k + dm) % 3)
                    values(n, k, u)
                    for dm, s in segs[cut[2]:]:
                        segment(n + dm, s, (k + dm) % 3)

            for k in range(3):
                pe.sem_inc(probs_free[k], 1)
            pe.wait_ge(qk_in[0], QK_IN)
            for s in range(NSEG):
                segment(0, s, 0, True)
            transpose_max(0)
            pe.wait_ge(qk_in[1], QK_IN)
            for u in range(MAX_AT, STEPS):
                for _, s in SEGS_BY_CHUNK[u]:
                    segment(1, s, 1)
            pe.wait_ge(max_in[0], MAX_IN)
            for st in range(AHEAD):
                scores(st, 0)
            for st in range(LAG):
                pe.wait_ge(exp_done, st + 1)
                scores(st + AHEAD, 0)
            with pe.Fori(0, ITERS) as it:
                for k in range(3):
                    group(3 * it + k, it, k, 2)
            for n in PEELED:
                group(n, n // 3, n % 3, NG - 1 - n)


def feed_forward(nc, keep, heads_out, Ws1, Ws3, Ws2, We1, We3, We2, out_tiles):
    with ExitStack() as ctx:
        def sb(name, shape, dt=F32):
            return ctx.enter_context(nc.sbuf_tensor(name, shape, dt))

        ff = dict(
            w13_hi=sb("w13_hi", [P, UNITS, 2 * FF], F32R),
            w13_lo=sb("w13_lo", [P, UNITS, 2 * FF], F32R),
            w2=sb("w2", [P, UNITS, 2, D]),
            xT_all=sb("xT_all", [P, T, P]),
            weights=sb("weights", [P, T, UNITS]),
        )
        route(nc, keep, ff, heads_out, Ws1, Ws3, Ws2, We1, We3, We2)
        experts(nc, keep, ff, out_tiles)


def route(nc, keep, ff, heads_out, Ws1, Ws3, Ws2, We1, We3, We2):
    ident, x_all = keep["ident"], keep["x_all"]
    with ExitStack() as ctx:
        def sb(name, shape, dt=F32):
            return ctx.enter_context(nc.sbuf_tensor(name, shape, dt))

        def pair(name, shape, dt=F32):
            return [sb(f"{name}{s}", shape, dt) for s in range(2)]

        def sem(name):
            return ctx.enter_context(nc.semaphore(name))

        def sems(name):
            return [sem(f"{name}{s}") for s in range(2)]

        w13 = sb("w13", [P, UNITS, 2 * FF])
        heads = pair("heads_in", [P, GB, HALF])
        rec = pair("rec", [P, H])
        o_nat = pair("o_nat", [P, SC, D])
        oT = pair("oT", [P, SC * P])
        stats = pair("stats2", [P, SC, 6])
        mean_var = pair("mean_var2", [P, SC, 2])
        var_eps = pair("var_eps2", [P, SC])
        rstd = pair("rstd2", [P, SC])
        xn = pair("xn2", [P, SC, D])
        xT = pair("xT2", [P, SC * P])
        gates = sb("gates", [P, T, NE])
        lower = sb("lower", [P, NE, NE])
        above, ties = sb("above", [P, T, NE, NE]), sb("ties", [P, T, NE, NE])
        rank = sb("rank", [P, T, NE])
        total = sb("total", [P, T])
        ps = ctx.enter_context(nc.psum_tensor("ps_route", [P, 8, 512], F32))

        w_in, lower_step, bias_added = sem("ffw_in"), sem("lower_step"), sem("bias_added")
        heads_in, tr_done, o_done, rec_done = sems("heads_in"), sems("tr_done"), sems("o_done"), sem("rec_done")
        oT_done, oT_out, y_done, x1_done = sems("oT_done"), sems("oT_out"), sems("y_done"), sems("x1_done")
        stats_step, mv_done, eps_done, rstd_done = sems("stats_step2"), sems("mv_done2"), sems("eps_done2"), sems("rstd_done2")
        xn_done, xT_done, xT_out, logit_done, gate_exp = sems("xn_done2"), sems("xT_done2"), sems("xT_out2"), sems("logit_done"), sems("gate_exp")
        passed = sem("passed2")
        split_hi, split_lo, chain = sem("split_hi"), sem("split_lo"), sem("chain")
        block = ctx.enter_context(nc.Block())

        @block.sync
        def _(sp):
            with sp.Fori(0, B) as b:
                for s in range(2):
                    sp.wait_ge(oT_done[s], b)
                    sp.dma_start(heads[s][:], heads_out[bass.ds(GB * b, GB), :, HALF * s:HALF * s + HALF].rearrange("g p c -> p g c")).then_inc(heads_in[s], 16)

        @block.gpsimd
        def _(pool):
            nc.gpsimd.memset(lower[:], 1.0).then_inc(lower_step, 1)
            pool.wait_ge(lower_step, 1)
            nc.gpsimd.affine_select(out=lower[:], in_=lower[:], compare_op=ALU.is_gt, fill=0.0, base=0,
                                    pattern=[[1, NE], [-1, NE]], channel_multiplier=0).then_inc(lower_step, 1)
            nc.gpsimd.memset(ff["weights"][:, :, NE:UNITS], 1.0).then_inc(lower_step, 1)
            with pool.Fori(0, B) as b:
                rows = x_all[:, bass.ds(TB * b, TB), :]
                nc.gpsimd.tensor_tensor(rows, rows, keep["row_consts"][:, 1:2, :].to_broadcast([P, TB, D]), ALU.add).then_inc(bias_added, 1)
                for s in range(2):
                    pool.wait_ge(mv_done[s], b + 1)
                    pool.sem_inc(passed, 1)
                    nc.gpsimd.tensor_scalar(var_eps[s][:], mean_var[s][:, :, 1], EPS, 0.0, ALU.add, ALU.add).then_inc(eps_done[s], 1)
                    pool.wait_ge(eps_done[s], b + 1)
                    nc.gpsimd.tensor_tensor(rstd[s][:], var_eps[s][:], keep["neg_half"][:, 0:SC], ALU.pow).then_inc(rstd_done[s], 1)

        @block.vector
        def _(dve):
            with dve.Fori(0, B) as b:
                for s in range(2):
                    for t in range(SC):
                        n = SC * s + t
                        view = ps[:, t % 2, :].rearrange("p (h r) -> p h r", r=ROWS)
                        dve.wait_ge(tr_done[t % 2], 4 * b + 2 * s + t // 2 + 1)
                        nc.vector.reciprocal(rec[t % 2][:], view[:, :, DH]).then_inc(rec_done, 1)
                        dve.wait_ge(rec_done, TB * b + n + 1)
                        if t == 0:
                            dve.wait_ge(oT_done[s], b)
                        nc.vector.tensor_tensor(o_nat[s][:, t, :].rearrange("p (h d) -> p h d", d=DH), view[:, :, 0:DH],
                                                rec[t % 2][:].rearrange("p (h a) -> p h a", a=1).to_broadcast([P, H, DH]), ALU.mult).then_inc(o_done[t % 2], 1)
                for s in range(2):
                    dve.wait_ge(y_done[s], b + 1)
                    dve.wait_ge(bias_added, b + 1)
                    rows = x_all[:, bass.ds(TB * b + SC * s, SC), :]
                    nc.vector.tensor_tensor(rows, ps[:, 4 + s, :].rearrange("p (t d) -> p t d", t=SC), rows, ALU.add).then_inc(x1_done[s], 1)
                    dve.wait_ge(x1_done[s], b + 1)
                    dve.sem_inc(passed, 1)
                    for t in range(SC):
                        ins = nc.vector.bn_stats(stats[s][:, t, :], x_all[:, bass.ds(TB * b + SC * s + t, 1), :].rearrange("p a d -> p (a d)")).then_inc(stats_step[s], 1)
                    for t in range(SC):
                        dve.wait_ge(stats_step[s], SC * b + t + 1)
                        dve.sem_inc(passed, 1)
                        ins = nc.vector.bn_aggr(mean_var[s][:, t, :], stats[s][:, t, :])
                    ins.then_inc(mv_done[s], 1)
                for s in range(2):
                    dve.wait_ge(rstd_done[s], b + 1)
                    dve.wait_ge(xT_done[s], b)
                    for t in range(SC):
                        ins = nc.vector.tensor_scalar(xn[s][:, t, :], x_all[:, bass.ds(TB * b + SC * s + t, 1), :].rearrange("p a d -> p (a d)"),
                                                      mean_var[s][:, t, 0:1], rstd[s][:, t:t + 1], ALU.subtract, ALU.mult)
                    ins.then_inc(xn_done[s], 1)
            for u in range(UNITS):
                dve.wait_ge(split_hi, u + 1)
                nc.vector.tensor_tensor(ff["w13_lo"][:, u, :], w13[:, u, :], ff["w13_hi"][:, u, :].bitcast(F32), ALU.subtract).then_inc(split_lo, 1)

            done = [0]

            def then(ins):
                ins.then_inc(chain, 1)
                done[0] += 1
                dve.wait_ge(chain, done[0])

            for s in range(2):
                dve.wait_ge(gate_exp[s], B)
            dve.wait_ge(lower_step, 3)
            then(nc.vector.tensor_scalar(gates[:], gates[:], 1.0, None, ALU.add))
            then(nc.vector.reciprocal(gates[:], gates[:]))
            mine = gates[:].rearrange("p t (e a) -> p t e a", a=1).to_broadcast([P, T, NE, NE])
            other = gates[:].rearrange("p t (a e) -> p t a e", a=1).to_broadcast([P, T, NE, NE])
            then(nc.vector.tensor_tensor(ties[:], other, mine, ALU.is_ge))
            then(nc.vector.tensor_tensor(above[:], other, mine, ALU.is_gt))
            then(nc.vector.tensor_tensor(ties[:].rearrange("p t e j -> p t (e j)"), ties[:].rearrange("p t e j -> p t (e j)"),
                                         lower[:].rearrange("p e (j a) -> p a (e j)", a=1).to_broadcast([P, T, NE * NE]), ALU.mult))
            then(nc.vector.tensor_tensor(ties[:], ties[:], above[:], ALU.max))
            then(nc.vector.reduce_sum(rank[:], ties[:], AX))
            then(nc.vector.tensor_scalar(rank[:], rank[:], 1.5, None, ALU.is_lt))
            then(nc.vector.tensor_tensor(gates[:], gates[:], rank[:], ALU.mult))
            then(nc.vector.reduce_sum(total[:], gates[:], AX))
            then(nc.vector.reciprocal(total[:], total[:]))
            then(nc.vector.tensor_tensor(ff["weights"][:, :, 0:NE], gates[:],
                                         total[:].rearrange("p (t a) -> p t a", a=1).to_broadcast([P, T, NE]), ALU.mult))

        @block.scalar
        def _(act):
            for u in range(UNITS):
                w1, w3, w2 = (We1[u], We3[u], We2[u]) if u < NE else (Ws1, Ws3, Ws2)
                act.dma_start(w13[:, u, 0:FF], w1).then_inc(w_in, 16)
                act.dma_start(w13[:, u, FF:2 * FF], w3).then_inc(w_in, 16)
                act.dma_start(ff["w2"][:, u, :, :], w2.rearrange("(c p) d -> p c d", p=P)).then_inc(w_in, 16)
            with act.Fori(0, B) as b:
                for s in range(2):
                    act.wait_ge(oT_done[s], b + 1)
                    act.wait_ge(y_done[s], b)
                    nc.scalar.activation(oT[s][:], ps[:, 2 + s, :], ACT.Copy).then_inc(oT_out[s], 1)
                for s in range(2):
                    act.wait_ge(xT_done[s], b + 1)
                    act.wait_ge(logit_done[s], b)
                    nc.scalar.activation(ff["xT_all"][:, bass.ds(TB * b + SC * s, SC), :], ps[:, 6 + s, :].rearrange("p (t d) -> p t d", t=SC), ACT.Copy)
                    nc.scalar.activation(xT[s][:], ps[:, 6 + s, :], ACT.Copy).then_inc(xT_out[s], 1)
                for s in range(2):
                    act.wait_ge(logit_done[s], b + 1)
                    nc.scalar.activation(gates[:, bass.ds(TB * b + SC * s, SC), :], ps[:, 2 + s, 0:SC * NE].rearrange("p (t e) -> p t e", t=SC),
                                         ACT.Exp, scale=-1.0).then_inc(gate_exp[s], 1)
            act.wait_ge(w_in, 16 * 3 * UNITS)
            for u in range(UNITS):
                nc.scalar.activation(ff["w13_hi"][:, u, :], w13[:, u, :], ACT.Copy).then_inc(split_hi, 1)

        @block.tensor
        def _(pe):
            with pe.Fori(0, B) as b:
                for s in range(2):
                    pe.wait_ge(heads_in[s], 16 * b + 16)
                    for t in range(SC):
                        pe.wait_ge(o_done[t % 2], 4 * b + 2 * s + t // 2)
                        for g in range(GB):
                            ins = nc.tensor.transpose(ps[:, t % 2, P * g:P * g + P], heads[s][:, g, P * t:P * t + P], ident[:])
                        ins.then_inc(tr_done[t % 2], 1)
                for s in range(2):
                    pe.wait_ge(gate_exp[s], b)
                    for k in range(2):
                        pe.wait_ge(o_done[k], 4 * b + 2 * s + 2)
                    for t in range(SC):
                        ins = nc.tensor.transpose(ps[:, 2 + s, P * t:P * t + P], o_nat[s][:, t, :], ident[:])
                    ins.then_inc(oT_done[s], 1)
                for s in range(2):
                    pe.wait_ge(oT_out[s], b + 1)
                    pe.wait_ge(x1_done[s], b)
                    for t in range(SC):
                        ins = nc.tensor.matmul(ps[:, 4 + s, P * t:P * t + P], oT[s][:, P * t:P * t + P], keep["woT"][:], start=True, stop=True)
                    ins.then_inc(y_done[s], 1)
                for s in range(2):
                    pe.wait_ge(xn_done[s], b + 1)
                    pe.wait_ge(xT_out[s], b)
                    for t in range(SC):
                        ins = nc.tensor.transpose(ps[:, 6 + s, P * t:P * t + P], xn[s][:, t, :], ident[:])
                    ins.then_inc(xT_done[s], 1)
                for s in range(2):
                    pe.wait_ge(xT_out[s], b + 1)
                    for t in range(SC):
                        ins = nc.tensor.matmul(ps[:, 2 + s, NE * t:NE * t + NE], xT[s][:, P * t:P * t + P], keep["wg"][:], start=True, stop=True)
                    ins.then_inc(logit_done[s], 1)


def experts(nc, keep, ff, out_tiles):
    ident, x_all = keep["ident"], keep["x_all"]
    with ExitStack() as ctx:
        def sb(name, shape, dt=F32):
            return ctx.enter_context(nc.sbuf_tensor(name, shape, dt))

        def sem(name):
            return ctx.enter_context(nc.semaphore(name))

        def sems(name, n=2):
            return [sem(f"{name}{s}") for s in range(n)]

        ND = 3
        xh = [sb(f"x_hi{s}", [P, P], F32R) for s in range(2)]
        xl = [sb(f"x_lo{s}", [P, P], F32R) for s in range(2)]
        wt = [sb(f"wt{s}", [P, UNITS]) for s in range(2)]
        act_out = [sb(f"act_out{i}", [P, FF]) for i in range(ND)]
        hid = [sb(f"hid{i}", [P, FF]) for i in range(ND)]
        hidT = [sb(f"hidT{i}", [P, FF]) for i in range(ND)]
        y = [sb(f"y{s}", [P, D]) for s in range(2)]
        ps_up = ctx.enter_context(nc.psum_tensor("ps_up", [P, ND, 512], F32))
        ps_hT = ctx.enter_context(nc.psum_tensor("ps_hT", [P, 2, 512], F32))
        ps_y = ctx.enter_context(nc.psum_tensor("ps_y", [P, 2, 512], F32))

        xh_done, xl_done, wt_done = sems("xh_done3"), sems("xl_done3"), sems("wt_done")
        up_done, act_done, hid_done, hT_done = sems("up_done", ND), sems("act_done", ND), sems("hid_done", ND), sems("hT_done", 2)
        hT_out, down_done, y_out, y_stored = sems("hT_out", ND), sems("down_done", ND), sems("y_out3"), sems("y_stored")
        block = ctx.enter_context(nc.Block())
        N2 = 2 * UNITS
        PER = N2 // ND


        @block.sync
        def _(sp):
            with sp.Fori(0, T // 2) as it:
                for s in range(2):
                    sp.wait_ge(y_out[s], it + 1)
                    sp.dma_start(out_tiles[:, bass.ds(2 * it + s, 1), :].rearrange("p a d -> p (a d)"), y[s][:]).then_inc(y_stored[s], 16)
            for s in range(2):
                sp.wait_ge(y_stored[s], 16 * (T // 2))

        @block.vector
        def _(dve):
            def finish(it, s):
                last = UNITS * s + UNITS - 1
                dve.wait_ge(down_done[last % ND], PER * it + last // ND + 1)
                dve.wait_ge(y_stored[s], 16 * it)
                nc.vector.scalar_tensor_tensor(out=y[s][:], in0=ps_y[:, s, 0:D], scalar=1.0 / 3.0,
                                               in1=x_all[:, bass.ds(2 * it + s, 1), :].rearrange("p a d -> p (a d)"),
                                               op0=ALU.mult, op1=ALU.add).then_inc(y_out[s], 1)

            with dve.Fori(0, T // 2) as it:
                for s in range(2):
                    row = ff["xT_all"][:, bass.ds(2 * it + s, 1), :].rearrange("p a d -> p (a d)")
                    dve.wait_ge(xh_done[s], it + 1)
                    nc.vector.tensor_tensor(xl[s][:], row, xh[s][:].bitcast(F32), ALU.subtract).then_inc(xl_done[s], 1)
                    nc.vector.tensor_copy(wt[s][:], ff["weights"][:, bass.ds(2 * it + s, 1), :].rearrange("p a d -> p (a d)")).then_inc(wt_done[s], 1)
                for v in range(N2):
                    s, e, i = v // UNITS, v % UNITS, v % ND
                    if e == 0:
                        dve.wait_ge(wt_done[s], it + 1)
                    dve.wait_ge(act_done[i], PER * it + v // ND + 1)
                    if v < ND:
                        dve.wait_ge(hT_done[(N2 - ND + v) % 2], UNITS * it)
                    else:
                        dve.wait_ge(hT_done[(v - ND) % 2], UNITS * it + (v - ND) // 2 + 1)
                    nc.vector.scalar_tensor_tensor(out=hid[i][:], in0=ps_up[:, i, FF:2 * FF], scalar=wt[s][:, e:e + 1], in1=act_out[i][:],
                                                   op0=ALU.mult, op1=ALU.mult).then_inc(hid_done[i], 1)
                    if v == UNITS + 2:
                        finish(it, 0)
                finish(it, 1)

        @block.scalar
        def _(act):
            with act.Fori(0, T // 2) as it:
                for s in range(2):
                    act.wait_ge(up_done[(N2 - 1) % ND], PER * it)
                    act.wait_ge(xl_done[s], it)
                    nc.scalar.activation(xh[s][:], ff["xT_all"][:, bass.ds(2 * it + s, 1), :].rearrange("p a d -> p (a d)"), ACT.Copy).then_inc(xh_done[s], 1)
                for v in range(N2 + 1):
                    if v < N2:
                        i = v % ND
                        act.wait_ge(up_done[i], PER * it + v // ND + 1)
                        act.wait_ge(hid_done[i], PER * it + v // ND)
                        nc.scalar.activation(act_out[i][:], ps_up[:, i, 0:FF], ACT.Silu).then_inc(act_done[i], 1)
                    if v > 0:
                        w = v - 1
                        i = w % ND
                        act.wait_ge(hT_done[w % 2], UNITS * it + w // 2 + 1)
                        act.wait_ge(down_done[i], PER * it + w // ND)
                        nc.scalar.activation(hidT[i][:], ps_hT[:, w % 2, 0:FF], ACT.Copy).then_inc(hT_out[i], 1)

        @block.tensor
        def _(pe):
            with pe.Fori(0, T // 2) as it:
                for v in range(N2 + 2):
                    if v < N2:
                        s, e, i = v // UNITS, v % UNITS, v % ND
                        if e == 0:
                            pe.wait_ge(xl_done[s], it + 1)
                        pe.wait_ge(hid_done[i], PER * it + v // ND)
                        o = ps_up[:, i, :]
                        nc.tensor.matmul(o, xh[s][:], ff["w13_hi"][:, e, :], start=True, stop=False)
                        nc.tensor.matmul(o, xl[s][:], ff["w13_hi"][:, e, :], start=False, stop=False)
                        nc.tensor.matmul(o, xh[s][:], ff["w13_lo"][:, e, :], start=False, stop=True).then_inc(up_done[i], 1)
                    if 0 < v <= N2:
                        w = v - 1
                        i = w % ND
                        pe.wait_ge(hid_done[i], PER * it + w // ND + 1)
                        if w < 2:
                            pe.wait_ge(hT_out[(N2 - 2 + w) % ND], PER * it)
                        else:
                            pe.wait_ge(hT_out[(w - 2) % ND], PER * it + (w - 2) // ND + 1)
                        nc.tensor.transpose(ps_hT[:, w % 2, 0:P], hid[i][:, 0:P], ident[:])
                        nc.tensor.transpose(ps_hT[:, w % 2, P:2 * P], hid[i][:, P:2 * P], ident[:]).then_inc(hT_done[w % 2], 1)
                    if v > 1:
                        w = v - 2
                        s, e, i = w // UNITS, w % UNITS, w % ND
                        pe.wait_ge(hT_out[i], PER * it + w // ND + 1)
                        if e == 0:
                            pe.wait_ge(y_out[s], it)
                        for c in range(2):
                            ins = nc.tensor.matmul(ps_y[:, s, 0:D], hidT[i][:, P * c:P * c + P], ff["w2"][:, e, c, :],
                                                   start=(e == 0 and c == 0), stop=(e == UNITS - 1 and c == 1))
                        ins.then_inc(down_done[i], 1)


_INS = ["L0_attn_x", "L0_attn_Wq", "L0_attn_bq", "L0_attn_Wk", "L0_attn_bk", "L0_attn_Wv", "L0_attn_bv", "L0_attn_Wo",
        "L0_attn_bo", "L0_ffn_Wg", "L0_ffn_Ws1", "L0_ffn_Ws3", "L0_ffn_Ws2", "L0_ffn_We1", "L0_ffn_We3", "L0_ffn_We2"]


def kernel(**inputs):
    import numpy as np
    import concourse.bacc as bacc
    from concourse.bass_utils import run_bass_kernel_spmd

    nc = bacc.Bacc("TRN2", target_bir_lowering=False, num_devices=1)
    arrays, args = {}, []
    for name in _INS:
        a = np.ascontiguousarray(inputs[name])
        arrays[f"in_{name}"] = a
        args.append(nc.dram_tensor(f"in_{name}", a.shape, mybir.dt.from_np(a.dtype), kind="ExternalInput").ap())
    out = nc.dram_tensor("out_x", (B, S, D), F32, kind="ExternalOutput").ap()
    layer_kernel(nc, *args, out)
    r = run_bass_kernel_spmd(nc, [arrays], core_ids=[0])
    return r.results[0]["out_x"]
```

```python
from contextlib import ExitStack

import concourse.bass as bass
from concourse import mybir

F32 = mybir.dt.float32
F32R = mybir.dt.float32r
BF16 = mybir.dt.bfloat16
U32 = mybir.dt.uint32
I32 = mybir.dt.int32
ACT = mybir.ActivationFunctionType
ALU = mybir.AluOpType
AX = mybir.AxisListType.X

P = 128
D = 128
B, S = 4, 1024
H, DH = 16, 8
GH = 4
GB = H // GH
NG = B * GB
ROWS = P // GH
PARTS = 3 * DH
T = B * S // P
TB = S // P
HALF = S // 2
SC = 4
FF = 256
NE = 8
UNITS = NE + 1
EPS = 1e-5
TOP = 2
SLOTS = 72
BATCH = 3
ROW = D + NE
MASKED = -1.0e30
SCALE = float(DH) ** -0.5

TILES = [
    [(0, 0, 512), (0, 512, 512)],
    [(7, 0, 128), (1, 128, 384), (1, 512, 512)],
    [(6, 0, 256), (2, 256, 256), (2, 512, 512)],
    [(5, 0, 384), (3, 384, 128), (3, 512, 512)],
]
DIAGONALS = [[0], [0, 128], [0, 256], [0, 384], [0, 512]]
NTYPE = 5
STEPS = 4 * GH + GH // 2
TYPE_END = [4, 8, 12, 16, 18]


def query_of(j, c):
    return c + (S - P * (8 - j) if j > 4 else 0)


def half_pieces(hs):
    st, half = divmod(hs, 2)
    if st < 16:
        t, h = divmod(st, GH)
        return [(h, j, c % HALF, w, query_of(j, c)) for j, c, w in TILES[t] if c // HALF == half]
    return [(2 * (st - 16) + 1 - half, 4, 0, 512, 512)]


def values_chunks():
    cuts = {512: (256, 256)}
    order = [[0, 1], [1, 0, 2], [1, 0, 2], [1, 0, 2]]
    out = []
    for t, pieces in enumerate(TILES):
        for j, c, w in [pieces[i] for i in order[t]]:
            for part in cuts.get(w, (w,)):
                out.append((t, j, c, part, query_of(j, c)))
                c += part
    return out + [(4, 4, c, 256, 512 + c) for c in (0, 256)]


def max_segments():
    out = []
    for i in range(S // ROWS):
        n = ROWS * (i + 1)
        if n <= 512:
            out.append((i, 0, n, i, True))
        else:
            out.append((i, 0, n // 2, i, False))
            out.append((i, n // 2, n // 2, i + 16, True))
    return out


SEGMENTS = max_segments()
NSEG = len(SEGMENTS)
CHUNKS = values_chunks()
LAG = 4
HALVES = 2 * STEPS
AHEAD = 3
MAX_AT = 7
LOWER_LAST = max(i for i, (t, j, c, w, q) in enumerate(CHUNKS) if q < HALF)


def segments_by_chunk():
    cost = [65 + s[2] / 0.96 for s in SEGMENTS]
    total, at, out = sum(cost), 0.0, [[] for _ in range(STEPS)]
    for n, c in enumerate(cost):
        u = MAX_AT + min(int(at / total * STEPS), STEPS - 1)
        out[u % STEPS].append((2 if u < STEPS else 1, n))
        at += c
    return out


SEGS_BY_CHUNK = segments_by_chunk()


def layer_kernel(nc, x, Wq, bq, Wk, bk, Wv, bv, Wo, bo, Wg, Ws1, Ws3, Ws2, We1, We3, We2, out):
    q_parts = nc.dram_tensor("q_parts", (B, H, PARTS + 2, S), F32).ap()
    k_parts = nc.dram_tensor("k_parts", (B, H, PARTS, S), F32).ap()
    heads_out = nc.dram_tensor("heads_out", (B * H, DH + 1, S), F32).ap()
    inverse = nc.dram_tensor("inverse", (B * H, S), F32).ap()
    x_tiles = x.rearrange("b (n p) d -> p (b n) d", p=P)
    out_tiles = out.rearrange("b (n p) d -> p (b n) d", p=P)
    with ExitStack() as ctx:
        def sb(name, shape, dt=F32, where=ctx):
            return where.enter_context(nc.sbuf_tensor(name, shape, dt))

        ident = sb("ident", [P, P])
        x_all = sb("x_all", [P, T, D])
        woT = sb("woT", [P, D])
        row_consts = sb("row_consts", [P, 2, D])
        wg = sb("wg", [P, NE])
        neg_half = sb("neg_half", [P, TB])
        w13_hi = sb("w13_hi", [P, UNITS, 2 * FF], F32R)
        w13_lo = sb("w13_lo", [P, UNITS, 2 * FF], F32R)
        w2 = sb("w2", [P, UNITS, 2, D])
        with ExitStack() as attn:
            keep = dict(
                ident=ident, x_all=x_all, woT=woT, row_consts=row_consts, neg_half=neg_half, wg=wg,
                w13_hi=w13_hi, w13_lo=w13_lo, w2=w2,
                ident_bf=sb("ident_bf", [P, P], BF16, attn),
                mask_bf=sb("mask_bf", [P, ROWS], BF16, attn),
                v_all=sb("v_all", [P, NG, TB, GH * DH], F32, attn),
                q_diag=[sb(f"q_diag{i}", [P, S // ROWS, GH, ROWS], F32R, attn) for i in range(3)],
                k_rows=[sb(f"k_rows{i}", [P, S], F32R, attn) for i in range(3)],
                v_one=[sb(f"v_one{i}", [P, TB, GH, ROWS], F32, attn) for i in range(3)],
            )
            prepare(nc, keep, x_tiles, Wq, bq, Wk, bk, Wv, bv, Wo, bo, Wg, Ws1, Ws3, Ws2, We1, We3, We2, q_parts, k_parts)
            attention(nc, keep, q_parts, k_parts, heads_out, inverse, Ws1, Ws3, We1, We3)
        feed_forward(nc, keep, heads_out, inverse, out_tiles)


def prepare(nc, keep, x_tiles, Wq, bq, Wk, bk, Wv, bv, Wo, bo, Wg, Ws1, Ws3, Ws2, We1, We3, We2, q_parts, k_parts):
    ident, x_all = keep["ident"], keep["x_all"]
    semaphores = []
    with ExitStack() as ctx:
        def sb(name, shape, dt=F32):
            return ctx.enter_context(nc.sbuf_tensor(name, shape, dt))

        def pair(name, shape, dt=F32):
            return [sb(f"{name}{s}", shape, dt) for s in range(2)]

        def sem(name):
            semaphores.append(nc.alloc_semaphore(name))
            return semaphores[-1]

        def sems(name):
            return [sem(f"{name}{s}") for s in range(2)]

        w_raw = sb("w_raw", [P, 4, D])
        w_hi = sb("w_hi", [P, 3, D], F32R)
        w_lo = sb("w_lo", [P, 3, D], F32R)
        bias_cols = sb("bias_cols", [P, 2])
        zeros = sb("zeros", [P, S])
        ones = sb("ones", [8, S])
        stats = sb("stats", [P, TB, 6])
        mean_var = sb("mean_var", [P, TB, 2])
        var_eps = sb("var_eps", [P, TB])
        rstd = sb("rstd", [P, TB])
        xn = pair("xn", [P, SC, D])
        xh = pair("xh", [P, SC * P], F32R)
        xl = pair("xl", [P, SC * P], F32R)
        qf, kf = pair("qf", [P, HALF]), pair("kf", [P, HALF])
        qh, kh = pair("qh", [P, HALF], F32R), pair("kh", [P, HALF], F32R)
        ql, kl = pair("ql", [P, HALF], F32R), pair("kl", [P, HALF], F32R)
        ps = ctx.enter_context(nc.psum_tensor("ps_prep", [P, 8, 512], F32))

        x_in, w_in, b_in, mat_in = sem("x_in"), sem("w_in"), sem("b_in"), sem("mat_in")
        consts, ident_ready, wT_done, w_hi_done = sem("consts"), sem("ident_ready"), sem("wT_done"), sem("w_hi_done")
        w_ready, fills, pool_fills = sem("w_ready"), sem("fills"), sem("pool_fills")
        stats_step, mv_done, eps_done, rstd_done = sem("stats_step"), sem("mv_done"), sem("eps_done"), sem("rstd_done")
        xn_done, xT_done, xh_done, xl_done = sems("xn_done"), sems("xT_done"), sems("xh_done"), sems("xl_done")
        q_done, k_done, v_done = sems("q_done"), sems("k_done"), sems("v_done")
        qf_done, kf_done, qh_done, kh_done = sems("qf_done"), sems("kf_done"), sems("qh_done"), sems("kh_done")
        ql_done, kl_done, v_out = sems("ql_done"), sems("kl_done"), sems("v_out")
        stored, rows_out = sems("stored"), sem("rows_out")
        w2_in = sem("w2_in")
        passed, bias_added = sem("passed0"), sem("bias_added")
        block = ctx.enter_context(nc.Block())
        FILLS = 12

        @block.sync
        def _(sp):
            sp.dma_start(x_all[:, 0:TB, :], x_tiles[:, 0:TB, :]).then_inc(x_in, 16)
            for n, w in enumerate((Wq, Wk, Wv, Wo)):
                sp.dma_start(w_raw[:, n, :], w).then_inc(w_in, 16)
            for n, b in enumerate((bq, bk)):
                sp.dma_start(bias_cols[:, n:n + 1], b.rearrange("(p a) -> p a", a=1)).then_inc(b_in, 16)
            for n, b in enumerate((bv, bo)):
                sp.dma_start(keep["row_consts"][:, n, :], b.rearrange("(a n) -> a n", a=1).to_broadcast([P, D])).then_inc(b_in, 16)
            sp.dma_start(keep["wg"][:], Wg).then_inc(b_in, 16)
            sp.wait_ge(x_in, 16)
            for b in range(1, B):
                sp.dma_start(x_all[:, TB * b:TB * b + TB, :], x_tiles[:, TB * b:TB * b + TB, :]).then_inc(x_in, 16)
                sp.wait_ge(x_in, 16 * (b + 1))
            sp.wait_ge(pool_fills, 2)
            sp.dma_start(q_parts.rearrange("b h r c -> (b h) r c")[:, PARTS:PARTS + 2, :], zeros[:]).then_inc(rows_out, 16)
            sp.wait_ge(pool_fills, FILLS)
            for i in range(3):
                for h in range(GH):
                    r = ROWS * h + PARTS
                    sp.dma_start(keep["k_rows"][i][r:r + 2, :].bitcast(F32), ones[0:2, :]).then_inc(rows_out, 16)
            with sp.Fori(0, B) as b:
                for s in range(2):
                    cols = slice(HALF * s, HALF * s + HALF)
                    qd = q_parts[bass.ds(b, 1), :, :, cols].rearrange("b h r c -> (b h) r c")
                    kd = k_parts[bass.ds(b, 1), :, :, cols].rearrange("b h r c -> (b h) r c")
                    sp.wait_ge(qh_done[s], b + 1)
                    sp.dma_start(qd[:, 0:DH, :], qh[s][:].bitcast(F32)).then_inc(stored[s], 16)
                    sp.dma_start(qd[:, 2 * DH:3 * DH, :], qh[s][:].bitcast(F32)).then_inc(stored[s], 16)
                    sp.wait_ge(kh_done[s], b + 1)
                    sp.dma_start(kd[:, 0:DH, :], kh[s][:].bitcast(F32)).then_inc(stored[s], 16)
                    sp.dma_start(kd[:, DH:2 * DH, :], kh[s][:].bitcast(F32)).then_inc(stored[s], 16)
                    sp.wait_ge(ql_done[s], b + 1)
                    sp.dma_start(qd[:, DH:2 * DH, :], ql[s][:].bitcast(F32)).then_inc(stored[s], 16)
                    sp.wait_ge(kl_done[s], b + 1)
                    sp.dma_start(kd[:, 2 * DH:3 * DH, :], kl[s][:].bitcast(F32)).then_inc(stored[s], 16)
            for s in range(2):
                sp.wait_ge(stored[s], 16 * 6 * B)
            sp.wait_ge(rows_out, 16 * (1 + 3 * GH))

        @block.gpsimd
        def _(pool):
            mask, identb = keep["mask_bf"], keep["ident_bf"]
            nc.gpsimd.memset(ident[:], 0.0).then_inc(consts, 1)
            nc.gpsimd.memset(identb[:], 0.0).then_inc(consts, 1)
            nc.gpsimd.memset(mask[:], 0.0).then_inc(consts, 1)
            pool.wait_ge(consts, 3)
            for m in (ident, identb):
                nc.gpsimd.affine_select(out=m[:], in_=m[:], compare_op=ALU.not_equal, fill=1.0, base=0,
                                        pattern=[[-1, P]], channel_multiplier=1).then_inc(ident_ready, 1)
            pool.wait_ge(ident_ready, 2)
            for h in range(GH):
                m = mask[ROWS * h:ROWS * h + ROWS, :]
                nc.gpsimd.affine_select(out=m, in_=m, compare_op=ALU.is_ge, fill=MASKED, base=0,
                                        pattern=[[-1, ROWS]], channel_multiplier=1).then_inc(ident_ready, 1)
                pool.wait_ge(ident_ready, 3 + h)
            nc.gpsimd.memset(keep["neg_half"][:], -0.5).then_inc(consts, 1)
            nc.gpsimd.memset(zeros[:], 0.0).then_inc(pool_fills, 1)
            nc.gpsimd.memset(ones[:], 1.0).then_inc(pool_fills, 1)
            for i in range(3):
                nc.gpsimd.memset(keep["v_one"][i][:], 0.0).then_inc(pool_fills, 1)
                nc.gpsimd.memset(keep["k_rows"][i][:].bitcast(F32), 0.0).then_inc(pool_fills, 1)
            pool.wait_ge(pool_fills, 8)
            for i in range(3):
                nc.gpsimd.memset(keep["v_one"][i][:, :, :, DH:DH + 1], 1.0).then_inc(pool_fills, 1)
            nc.gpsimd.memset(keep["q_diag"][2][:].bitcast(F32), 0.0).then_inc(pool_fills, 1)
            with pool.Fori(0, B) as b:
                pool.wait_ge(mv_done, b + 1)
                pool.sem_inc(passed, 1)
                nc.gpsimd.tensor_scalar(var_eps[:], mean_var[:, :, 1], EPS, 0.0, ALU.add, ALU.add).then_inc(eps_done, 1)
                pool.wait_ge(eps_done, b + 1)
                nc.gpsimd.tensor_tensor(rstd[:], var_eps[:], keep["neg_half"][:], ALU.pow).then_inc(rstd_done, 1)
            pool.wait_ge(w2_in, 16 * UNITS)
            for s in range(2):
                pool.wait_ge(xn_done[s], B)
            for b in range(B):
                rows = x_all[:, TB * b:TB * b + TB, :]
                nc.gpsimd.tensor_tensor(rows, rows, keep["row_consts"][:, 1:2, :].to_broadcast([P, TB, D]), ALU.add).then_inc(bias_added, 1)

        @block.vector
        def _(dve):
            w_psum = ps[:, 0, :].rearrange("p (n d) -> p n d", n=4)
            dve.wait_ge(w_hi_done, 2)
            nc.vector.tensor_tensor(w_lo[:], w_psum[:, 0:3, :], w_hi[:].bitcast(F32), ALU.subtract).then_inc(w_ready, 1)
            for i in range(2):
                nc.vector.memset(keep["q_diag"][i][:].bitcast(F32), 0.0).then_inc(fills, 1)
            dve.wait_ge(b_in, 16 * 5)
            with dve.Fori(0, B) as b:
                dve.wait_ge(x_in, 16 * b + 16)
                dve.sem_inc(passed, 1)
                for t in range(TB):
                    nc.vector.bn_stats(stats[:, t, :], x_all[:, bass.ds(TB * b + t, 1), :].rearrange("p a d -> p (a d)")).then_inc(stats_step, 1)
                for t in range(TB):
                    dve.wait_ge(stats_step, TB * b + t + 1)
                    dve.sem_inc(passed, 1)
                    ins = nc.vector.bn_aggr(mean_var[:, t, :], stats[:, t, :])
                ins.then_inc(mv_done, 1)
                dve.wait_ge(rstd_done, b + 1)
                for s in range(2):
                    dve.wait_ge(xT_done[s], b)
                    for t in range(SC):
                        n = SC * s + t
                        ins = nc.vector.tensor_scalar(xn[s][:, t, :], x_all[:, bass.ds(TB * b + n, 1), :].rearrange("p a d -> p (a d)"),
                                                      mean_var[:, n, 0:1], rstd[:, n:n + 1], ALU.subtract, ALU.mult)
                    ins.then_inc(xn_done[s], 1)
                for s in range(2):
                    dve.wait_ge(xh_done[s], b + 1)
                    nc.vector.tensor_tensor(xl[s][:], ps[:, s, :], xh[s][:].bitcast(F32), ALU.subtract).then_inc(xl_done[s], 1)
                for s in range(2):
                    dve.wait_ge(qh_done[s], b + 1)
                    dve.wait_ge(stored[s], 96 * b)
                    nc.vector.tensor_tensor(ql[s][:], qf[s][:], qh[s][:].bitcast(F32), ALU.subtract).then_inc(ql_done[s], 1)
                    dve.wait_ge(kh_done[s], b + 1)
                    nc.vector.tensor_tensor(kl[s][:], kf[s][:], kh[s][:].bitcast(F32), ALU.subtract).then_inc(kl_done[s], 1)
                    dve.wait_ge(v_done[s], b + 1)
                    src = ps[:, 6 + s, :].rearrange("p (j g c) -> p j g c", j=SC, g=GB)
                    bias = keep["row_consts"][:, 0:1, :].rearrange("p a (g c) -> p a g c", g=GB).to_broadcast([P, SC, GB, GH * DH])
                    dst = keep["v_all"][:, bass.ds(GB * b, GB), SC * s:SC * s + SC, :].rearrange("p g j c -> p j g c")
                    nc.vector.tensor_tensor(dst, src, bias, ALU.add).then_inc(v_out[s], 1)

        @block.scalar
        def _(act):
            for u in range(UNITS):
                w2 = We2[u] if u < NE else Ws2
                act.dma_start(keep["w2"][:, u, :, :], w2.rearrange("(c p) d -> p c d", p=P)).then_inc(w2_in, 16)
            w_psum = ps[:, 0, :].rearrange("p (n d) -> p n d", n=4)
            act.wait_ge(wT_done, 1)
            nc.scalar.activation(w_hi[:], w_psum[:, 0:3, :], ACT.Copy).then_inc(w_hi_done, 1)
            nc.scalar.activation(keep["woT"][:], w_psum[:, 3, :], ACT.Copy).then_inc(w_hi_done, 1)
            act.wait_ge(b_in, 16 * 5)
            with act.Fori(0, B) as b:
                for s in range(2):
                    act.wait_ge(xT_done[s], b + 1)
                    act.wait_ge(v_done[s], b)
                    nc.scalar.activation(xh[s][:], ps[:, s, :], ACT.Copy).then_inc(xh_done[s], 1)
                for s in range(2):
                    for full, high, f_done, h_done, mm_done, l_done, col in (
                            (qf, qh, qf_done, qh_done, q_done, ql_done, 0), (kf, kh, kf_done, kh_done, k_done, kl_done, 1)):
                        act.wait_ge(mm_done[s], b + 1)
                        act.wait_ge(l_done[s], b)
                        nc.scalar.activation(full[s][:], ps[:, 2 + 2 * col + s, :], ACT.Identity,
                                             bias=bias_cols[:, col:col + 1]).then_inc(f_done[s], 1)
                        act.wait_ge(f_done[s], b + 1)
                        act.wait_ge(stored[s], 96 * b)
                        nc.scalar.activation(high[s][:], full[s][:], ACT.Copy).then_inc(h_done[s], 1)

        @block.tensor
        def _(pe):
            pe.wait_ge(w_in, 64)
            pe.wait_ge(ident_ready, 1)
            for n in range(4):
                ins = nc.tensor.transpose(ps[:, 0, D * n:D * n + D], w_raw[:, n, :], ident[:])
            ins.then_inc(wT_done, 1)
            pe.wait_ge(w_ready, 1)
            with pe.Fori(0, B) as b:
                for s in range(2):
                    pe.wait_ge(xn_done[s], b + 1)
                    pe.wait_ge(xl_done[s], b)
                    for t in range(SC):
                        ins = nc.tensor.transpose(ps[:, s, P * t:P * t + P], xn[s][:, t, :], ident[:])
                    ins.then_inc(xT_done[s], 1)
                for s in range(2):
                    pe.wait_ge(xl_done[s], b + 1)
                    for col, mm_done, f_done in ((0, q_done, qf_done), (1, k_done, kf_done)):
                        pe.wait_ge(f_done[s], b)
                        o = ps[:, 2 + 2 * col + s, :]
                        nc.tensor.matmul(o, w_hi[:, col, :], xh[s][:], start=True, stop=False)
                        nc.tensor.matmul(o, w_hi[:, col, :], xl[s][:], start=False, stop=False)
                        nc.tensor.matmul(o, w_lo[:, col, :], xh[s][:], start=False, stop=True).then_inc(mm_done[s], 1)
                    pe.wait_ge(v_out[s], b)
                    for t in range(SC):
                        o, c = ps[:, 6 + s, P * t:P * t + P], slice(P * t, P * t + P)
                        nc.tensor.matmul(o, xh[s][:, c], w_hi[:, 2, :], start=True, stop=False)
                        nc.tensor.matmul(o, xl[s][:, c], w_hi[:, 2, :], start=False, stop=False)
                        ins = nc.tensor.matmul(o, xh[s][:, c], w_lo[:, 2, :], start=False, stop=True)
                    ins.then_inc(v_done[s], 1)
    nc.clear_and_free_semaphores(semaphores)
    nc.all_engine_barrier()


def attention(nc, keep, q_parts, k_parts, heads_out, inverse, Ws1, Ws3, We1, We3):
    q_diag, k_rows, v_one = keep["q_diag"], keep["k_rows"], keep["v_one"]
    q_flat = q_parts.rearrange("b h r c -> (b h) r c")
    k_flat = k_parts.rearrange("b h r c -> (b h) r c")
    with ExitStack() as ctx:
        def sb(name, shape, dt=F32):
            return ctx.enter_context(nc.sbuf_tensor(name, shape, dt))

        def sem(name):
            return ctx.enter_context(nc.semaphore(name))

        def sems(name):
            return [sem(f"{name}{s}") for s in range(3)]

        probs = [sb(f"probs{i}", [P, GH, S]) for i in range(3)]
        heads = sb("heads", [P, S])
        sums = sb("sums", [P, B - 1, P])
        partial = sb("partial", [P, 48])
        row_max = sb("row_max", [P, 32])
        neg_max = sb("neg_max", [32, 2, P], F32R)
        neg_full = sb("neg_full", [32, P])
        def raw_up(u):
            return probs[2][:, u // 2, HALF * (u % 2):HALF * (u % 2) + 2 * FF] if u < NE else probs[1][:, 0, 0:2 * FF]

        ps_scores = ctx.enter_context(nc.psum_tensor("ps_scores", [P, 3, 512], F32))
        ps_max = ctx.enter_context(nc.psum_tensor("ps_max", [P, 3, 512], F32))
        ps_out = ctx.enter_context(nc.psum_tensor("ps_out", [P, 2, 512], F32))

        qk_in, max_in, heads_free = sems("qk_in"), sems("max_in"), sem("heads_free")
        scores_done, exp_done, mask_done = sem("scores_done"), sem("exp_done"), sem("mask_done")
        seg_done, seg_read, max_done, maxT_done = sem("seg_done"), sem("seg_read"), sem("max_done"), sem("maxT_done")
        neg_step, neg_done, v_ready = sem("neg_step"), sem("neg_done"), sem("v_ready")
        lower_done = sem("lower_done")
        lower_free, upper_free = sem("lower_free"), sem("upper_free")
        probs_free = sems("probs_free")
        sums_in, sums_done = sem("sums_in"), sem("sums_done")
        passed, ffw_hi, ffw_lo, ffw_in = sem("passed1"), sem("ffw_hi"), sem("ffw_lo"), sem("ffw_in")
        block = ctx.enter_context(nc.Block())
        FIRST = 2 * LAG + AHEAD
        QK_IN, MAX_IN = 16 * 2 * GH, 16 * 2 * GH
        ITERS = (NG - 4) // 3
        PEELED = range(3 * ITERS, NG)


        @block.sync
        def _(sp):
            def load(n, slot):
                for h in range(GH):
                    r = ROWS * h
                    sp.dma_start(q_diag[slot][r:r + PARTS + 2, :, h, :].bitcast(F32),
                                 q_flat[bass.ds(n * GH + h, 1), :, :].rearrange("a r (i c) -> (a r) i c", c=ROWS)).then_inc(qk_in[slot], 16)
                    sp.dma_start(k_rows[slot][r:r + PARTS, :].bitcast(F32),
                                 k_flat[bass.ds(n * GH + h, 1), :, :].rearrange("a r c -> (a r) c")).then_inc(qk_in[slot], 16)

            def put_max(m, slot):
                sp.wait_ge(neg_done, m + 1)
                for h in range(GH):
                    for part in range(2):
                        r = ROWS * h + PARTS + part
                        sp.dma_start(q_diag[slot][r:r + 1, :, h, :].bitcast(F32),
                                     neg_max[:, part, ROWS * h:ROWS * h + ROWS].bitcast(F32)).then_inc(max_in[slot], 16)

            def group(n, k, loads, following):
                if loads:
                    sp.wait_ge(scores_done, HALVES * n + 1)
                    load(n + 2, (k + 2) % 3)
                if following:
                    put_max(n + 1, (k + 1) % 3)
                sp.wait_ge(lower_free, n + 2)
                sp.wait_ge(upper_free, n + 2)
                for h in range(GH):
                    sp.dma_start(heads_out[bass.ds(GH * n + h, 1), :, :].rearrange("a r c -> (a r) c"),
                                 heads[ROWS * h:ROWS * h + DH + 1, :]).then_inc(heads_free, 16)

            sp.sem_inc(heads_free, 16 * GH)
            load(0, 0)
            load(1, 1)
            put_max(0, 0)
            with sp.Fori(0, ITERS) as it:
                for k in range(3):
                    group(3 * it + k, k, True, True)
            for n in PEELED:
                if n == NG - 3:
                    sp.wait_ge(heads_free, 16 * GH * n)
                    for b in range(B - 1):
                        sp.dma_start(sums[:, b, :], sums_of(heads_out, b)).then_inc(sums_in, 16)
                if n == NG - 1:
                    sp.wait_ge(sums_done, 1)
                    for b in range(B - 1):
                        sp.dma_start(inverse_of(inverse, b), sums[:, b, :]).then_inc(sums_in, 16)
                group(n, n % 3, n + 2 < NG, n + 1 < NG)
            sp.wait_ge(heads_free, 16 * GH * (NG + 1))
            sp.wait_ge(sums_in, 16 * 2 * (B - 1))

        @block.gpsimd
        def _(pool):
            def group(n, k):
                for st in range(STEPS):
                    t = st // GH
                    buf = probs[(5 * k + t) % 3]
                    slot = st % GH if t < 4 else st - 16
                    pool.wait_ge(exp_done, HALVES * n + 2 * st + 2)
                    pool.sem_inc(passed, 1)
                    gap, count = max(DIAGONALS[t][-1], P), len(DIAGONALS[t])
                    view = buf[:, slot, 0:gap * count].rearrange("p (a c) -> p a c", a=count)[:, :, 0:P]
                    nc.gpsimd.affine_select(out=view, in_=view, compare_op=ALU.is_ge, fill=0.0, base=0,
                                            pattern=[[0, count], [1, P]], channel_multiplier=-1).then_inc(mask_done, 1)
                    if st == 1:
                        src = keep["v_all"][:, bass.ds(n, 1), :, :].rearrange("p a j (h d) -> p (a j) h d", h=GH)
                        nc.gpsimd.tensor_copy(v_one[k][:, :, :, 0:DH], src).then_inc(v_ready, 1)

            for u in range(UNITS):
                pool.wait_ge(ffw_hi, u + 1)
                nc.gpsimd.tensor_tensor(keep["w13_lo"][:, u, :], raw_up(u), keep["w13_hi"][:, u, :].bitcast(F32), ALU.subtract).then_inc(ffw_lo, 1)
            with pool.Fori(0, ITERS) as it:
                for k in range(3):
                    group(3 * it + k, k)
            for n in PEELED:
                group(n, n % 3)

        @block.scalar
        def _(act):
            def exp_half(n, it, k, hs):
                st, half = divmod(hs, 2)
                t = st // GH
                tau = 5 * k + t
                slot = st % GH if t < 4 else st - 16
                if hs % (2 * GH) == 0:
                    act.wait_ge(probs_free[tau % 3], 5 * it + tau // 3 + 1)
                act.wait_ge(scores_done, HALVES * n + hs + 1)
                nc.scalar.activation(probs[tau % 3][:, slot, HALF * half:HALF * half + HALF], ps_scores[:, hs % 3, :],
                                     ACT.Exp, scale=SCALE).then_inc(exp_done, 1)

            def copy_out(n, it, k, half, free):
                if half == 1:
                    tau = 5 * k + 4
                    act.wait_ge(probs_free[tau % 3], 5 * it + tau // 3 + 2)
                if half == 0:
                    act.wait_ge(lower_done, n + 1)
                    act.wait_ge(heads_free, 16 * GH * (n + 1))
                nc.scalar.activation(heads[:, HALF * half:HALF * half + HALF], ps_out[:, half, :], ACT.Copy).then_inc(free, 1)

            def group(n, it, k, following):
                for hs in range(FIRST, HALVES + FIRST):
                    if hs < HALVES:
                        exp_half(n, it, k, hs)
                    elif following:
                        exp_half(n + 1, it + (k == 2), (k + 1) % 3, hs - HALVES)
                    if hs == HALVES + 5:
                        copy_out(n, it, k, 0, lower_free)
                    if hs == HALVES + 2 * LAG + 1:
                        copy_out(n, it, k, 1, upper_free)

            act.sem_inc(lower_free, 1)
            act.sem_inc(upper_free, 1)

            for u in range(UNITS):
                for n, w in enumerate((We1[u], We3[u]) if u < NE else (Ws1, Ws3)):
                    act.dma_start(raw_up(u)[:, FF * n:FF * n + FF], w).then_inc(ffw_in, 16)
            act.wait_ge(ffw_in, 32 * UNITS)
            for u in range(UNITS):
                nc.scalar.activation(keep["w13_hi"][:, u, :], raw_up(u), ACT.Copy).then_inc(ffw_hi, 1)
            act.wait_ge(ffw_lo, UNITS)
            for hs in range(FIRST):
                exp_half(0, 0, 0, hs)
            with act.Fori(0, ITERS) as it:
                for k in range(3):
                    group(3 * it + k, it, k, True)
            for n in PEELED:
                group(n, n // 3, n % 3, n + 1 < NG)

        @block.vector
        def _(dve):
            def reduce_segment(m, s):
                _, _, n, col, _ = SEGMENTS[s]
                dve.wait_ge(seg_done, NSEG * m + s + 1)
                dst = row_max[:, col:col + 1] if col < 16 else partial[:, col:col + 1]
                nc.vector.reduce_max(dst, ps_max[:, s % 3, 0:n], AX).then_inc(seg_read, 1)
                if s == NSEG - 1:
                    dve.wait_ge(seg_read, NSEG * m + NSEG)
                    nc.vector.tensor_tensor(row_max[:, 16:32], partial[:, 16:32], partial[:, 32:48], ALU.max).then_inc(max_done, 1)

            def negate(m, put_before):
                if put_before is not None:
                    dve.wait_ge(*put_before)
                dve.wait_ge(maxT_done, m + 1)
                nc.vector.tensor_scalar(neg_full[:], ps_max[0:32, 2, 0:P], -1.0, None, ALU.mult).then_inc(neg_step, 1)
                dve.wait_ge(neg_step, 2 * m + 1)
                nc.vector.tensor_copy(neg_max[:, 0, :], neg_full[:]).then_inc(neg_step, 1)
                dve.wait_ge(neg_step, 2 * m + 2)
                nc.vector.tensor_tensor(neg_max[:, 1, :], neg_full[:], neg_max[:, 0, :].bitcast(F32), ALU.subtract).then_inc(neg_done, 1)

            def group(n, it, k, last):
                for u in range(STEPS):
                    if u == MAX_AT:
                        negate(n + 1, (max_in[k], MAX_IN * (it + 1)))
                    for dm, s in SEGS_BY_CHUNK[u]:
                        if dm <= last:
                            reduce_segment(n + dm, s)

            for s in range(NSEG):
                reduce_segment(0, s)
            negate(0, None)
            for u in range(MAX_AT, STEPS):
                for _, s in SEGS_BY_CHUNK[u]:
                    reduce_segment(1, s)
            with dve.Fori(0, ITERS) as it:
                for k in range(3):
                    group(3 * it + k, it, k, 2)
            for n in PEELED:
                if n + 1 < NG:
                    group(n, n // 3, n % 3, NG - 1 - n)
            dve.wait_ge(sums_in, 16 * (B - 1))
            nc.vector.reciprocal(sums[:], sums[:]).then_inc(sums_done, 1)

        @block.tensor
        def _(pe):
            def scores(hs, slot):
                for h, j, c, w, q in half_pieces(hs):
                    ins = nc.tensor.matmul(ps_scores[:, hs % 3, c:c + w], k_rows[slot][:, P * j:P * j + P],
                                           q_diag[slot][:, q // ROWS:(q + w) // ROWS, h, :], start=True, stop=True)
                ins.then_inc(scores_done, 1)

            def segment(m, s, slot, first=False):
                i, k0, n, _, diagonal = SEGMENTS[s]
                if s == 2 and not first:
                    pe.wait_ge(neg_step, 2 * m - 1)
                if not (first and s < 3):
                    pe.wait_ge(seg_read, NSEG * m + s - 2)
                o = ps_max[:, s % 3, 0:n]
                ins = nc.tensor.matmul(o, q_diag[slot][:, i, :, :].rearrange("p h r -> p (h r)"), k_rows[slot][:, k0:k0 + n],
                                       start=True, stop=not diagonal)
                if diagonal:
                    ins = nc.tensor.matmul(ps_max[:, s % 3, n - ROWS:n], keep["ident_bf"][:], keep["mask_bf"][:],
                                           start=False, stop=True)
                ins.then_inc(seg_done, 1)

            def transpose_max(m):
                pe.wait_ge(max_done, m + 1)
                nc.tensor.transpose(ps_max[0:32, 2, 0:P], row_max[:], keep["ident"][:]).then_inc(maxT_done, 1)

            def values(n, k, u):
                t, j, c, w, q = CHUNKS[u]
                tau = 5 * k + t
                if u == 0:
                    pe.wait_ge(v_ready, n + 1)
                    pe.wait_ge(lower_free, n + 1)
                if u == 2:
                    pe.wait_ge(upper_free, n + 1)
                if u == 0 or CHUNKS[u - 1][0] != t:
                    pe.wait_ge(mask_done, STEPS * n + TYPE_END[t])
                for h in range(GH):
                    slot, c0 = (h, c) if t < 4 else (h // 2, c + HALF * (1 - h % 2))
                    ins = nc.tensor.matmul(ps_out[ROWS * h:ROWS * h + ROWS, q // HALF, q % HALF:q % HALF + w], v_one[k][:, j, h, :],
                                           probs[tau % 3][:, slot, c0:c0 + w], start=(u in (0, 2)), stop=(u in (LOWER_LAST, STEPS - 1)))
                if u == STEPS - 1 or CHUNKS[u + 1][0] != t:
                    ins.then_inc(probs_free[tau % 3], 1)
                elif u == LOWER_LAST:
                    ins.then_inc(lower_done, 1)

            def group(n, it, k, last):
                for u in range(STEPS):
                    st = u + LAG
                    segs = [(dm, s) for dm, s in SEGS_BY_CHUNK[u] if dm <= last]
                    if u == MAX_AT and last > 1:
                        pe.wait_ge(qk_in[(k + 2) % 3], QK_IN * (it + 1 + (k > 0)))
                    cut = [0, (len(segs) + 1) // 4, (len(segs) + 1) // 2, 3 * (len(segs) + 1) // 4, len(segs)]
                    if u == MAX_AT and last > 0:
                        cut[1] = 0
                        transpose_max(n + 1)
                    for part in range(4):
                        for dm, s in segs[cut[part]:cut[part + 1]]:
                            segment(n + dm, s, (k + dm) % 3)
                        if part == 1:
                            values(n, k, u)
                        if part in (0, 2):
                            hs = 2 * st + part // 2
                            if hs + AHEAD < HALVES or last > 0:
                                pe.wait_ge(exp_done, HALVES * n + hs + 1)
                                if hs + AHEAD == HALVES:
                                    pe.wait_ge(max_in[(k + 1) % 3], MAX_IN * (it + 1 + (k == 2)))
                                scores((hs + AHEAD) % HALVES, (k + (hs + AHEAD >= HALVES)) % 3)

            for k in range(3):
                pe.sem_inc(probs_free[k], 1)
            pe.wait_ge(qk_in[0], QK_IN)
            for s in range(NSEG):
                segment(0, s, 0, True)
            transpose_max(0)
            pe.wait_ge(qk_in[1], QK_IN)
            early = [s for u in range(MAX_AT, STEPS) for _, s in SEGS_BY_CHUNK[u]]
            cut = len(early) // 2
            for s in early[:cut]:
                segment(1, s, 1)
            pe.wait_ge(max_in[0], MAX_IN)
            for hs in range(AHEAD):
                scores(hs, 0)
            for hs in range(2 * LAG):
                for s in early[cut + hs * (len(early) - cut) // (2 * LAG):cut + (hs + 1) * (len(early) - cut) // (2 * LAG)]:
                    segment(1, s, 1)
                pe.wait_ge(exp_done, hs + 1)
                scores(hs + AHEAD, 0)
            with pe.Fori(0, ITERS) as it:
                for k in range(3):
                    group(3 * it + k, it, k, 2)
            for n in PEELED:
                group(n, n // 3, n % 3, NG - 1 - n)


def feed_forward(nc, keep, heads_out, inverse, out_tiles):
    x_rows = nc.dram_tensor("x_rows", (B * S + 1, ROW), F32).ap()
    y_rows = nc.dram_tensor("y_rows", (SLOTS * P, D), F32).ap()
    with ExitStack() as ctx:
        def sb(name, shape, dt=F32):
            return ctx.enter_context(nc.sbuf_tensor(name, shape, dt))

        gathers = [ctx.enter_context(nc.semaphore(f"gathered{i}")) for i in range(4)]
        ff = dict(
            row_gathers=gathers[:2], output_gathers=gathers[2:],
            x_hi=sb("x_hi_all", [P, B, S], F32R),
            x_lo=sb("x_lo_all", [P, B, S], F32R),
            position=sb("position", [P, TOP, T], U32),
            place=sb("place", [P, NE, T]),
            chosen=[sb(f"chosen{k}", [P, T, NE]) for k in range(TOP)],
            slot_expert=sb("slot_expert", [P, SLOTS + BATCH], I32),
            slot_onehot=sb("slot_onehot", [P, SLOTS, NE]),
            slot_start=sb("slot_start", [P, 2, SLOTS + BATCH]),
            table=sb("table", [P, 2, P + 2], BF16),
            iota=sb("iota_tokens", [P, P], BF16),
            slot_index=sb("slot_index", [P, SLOTS + BATCH]),
        )
        route(nc, keep, ff, heads_out, inverse, x_rows)
        experts(nc, keep, ff, x_rows, y_rows)
        combine(nc, keep, ff, y_rows, out_tiles)


def sums_of(heads_out, b):
    return heads_out[H * b:H * b + H, DH:DH + 1, :].rearrange("h a (q c) -> h (a q) c", c=P)


def inverse_of(inverse, b):
    return inverse[H * b:H * b + H, :].rearrange("h (q c) -> (h q) c", c=P)


def route(nc, keep, ff, heads_out, inverse, x_rows):
    ident, x_all = keep["ident"], keep["x_all"]
    with ExitStack() as ctx:
        def sb(name, shape, dt=F32):
            return ctx.enter_context(nc.sbuf_tensor(name, shape, dt))

        def pair(name, shape, dt=F32):
            return [sb(f"{name}{s}", shape, dt) for s in range(2)]

        def sem(name):
            return ctx.enter_context(nc.semaphore(name))

        def sems(name):
            return [sem(f"{name}{s}") for s in range(2)]

        o_raw = pair("o_raw", [P, HALF])
        over_sums = pair("over_sums", [P, HALF])
        last_sums = sb("last_sums", [P, P])
        oT = pair("oT", [P, HALF])
        stats = sb("stats2", [P, T, 6])
        mean_var = sb("mean_var2", [P, T, 2])
        var_eps = sb("var_eps2", [P, T])
        rstd = sb("rstd2", [P, T])
        xn = pair("xn2", [P, SC, D])
        xT = pair("xT2", [P, HALF])
        gates = sb("gates", [P, T, NE])
        zero_row = sb("zero_row", [1, ROW])
        upper = sb("upper", [P, P], BF16)
        ones = sb("ones_bf", [P, P], BF16)
        same_expert = sb("same_expert", [P, P], BF16)
        descending = sb("descending", [P, NE])
        numbers = sb("numbers", [P, NE])
        earlier = sb("earlier", [P, NE, NE])
        tile_counts = sb("tile_counts", [P, T])
        run_tokens = sb("run_tokens", [P, NE, T])
        slot_numbers = sb("slot_numbers", [P, SLOTS + BATCH])
        best, second, total = sb("best", [P, T]), sb("second", [P, T]), sb("total", [P, T])
        pick = sb("pick", [P, T])
        equal = sb("equal", [P, T, NE])
        chosen = ff["chosen"]
        rest = sb("rest", [P, T, NE])
        both = sb("both", [P, T, NE])
        weights = sb("weights", [P, T, NE])
        member = sb("member", [P, NE, T], BF16)
        member_step = sb("member_step", [P, NE * T], BF16)
        counts = sb("counts", [P, 2, P], BF16)
        n_expert = sb("n_expert", [P, NE])
        over = sb("over", [P, NE, T])
        n_tiles = sb("n_tiles", [P, NE])
        before = sb("before", [P, NE, NE])
        base, end = sb("base", [P, NE]), sb("end", [P, NE])
        starts = sb("starts", [P, 2, NE * T])
        starts_step = sb("starts_step", [P, 2, NE * T])
        diagonal = sb("diagonal", [P, 2, P])
        steps_diagonal = sb("steps_diagonal", [P, 2, 2, P])
        start_column = sb("start_column", [P, 2])
        step_columns = sb("step_columns", [P, 2, 2])
        past = sb("past", [P, SLOTS + BATCH, NE - 1])
        expert_f = sb("expert_f", [P, SLOTS + BATCH])
        ps = ctx.enter_context(nc.psum_tensor("ps_route", [P, 8, 512], F32))

        o_in, o_done, y_done, x1_done = sems("o_in"), sems("o_done"), sems("y_done"), sems("x1_done")
        stats_step, mv_done, eps_done, rstd_done = sem("stats_step2"), sem("mv_done2"), sem("eps_done2"), sem("rstd_done2")
        xn_done, xT_done, xT_out, logit_done, gate_exp = sems("xn_done2"), sems("xT_done2"), sems("xT_out2"), sems("logit_done"), sems("gate_exp")
        sums_in, sums_done = sem("sums_in"), sem("sums_done")
        xh_done, xl_done, xn_free = sems("xh_done2"), sems("xl_done2"), sems("xn_free2")
        const_step, chain, row_zero, rows_out, weights_done = sem("const_step"), sem("chain"), sem("row_zero"), sem("rows_out2"), sem("weights_done")
        member_done, counted, counts_out, scanned = sem("member_done"), sem("counted"), sem("counts_out"), sem("scanned")
        block = ctx.enter_context(nc.Block())
        CONSTS = 16

        @block.sync
        def _(sp):
            def load_heads(b, s):
                cols = slice(HALF * s, HALF * s + HALF)
                sp.wait_ge(o_done[s], b + 1)
                sp.dma_start(o_raw[s][:], heads_out[bass.ds(H * b, H), 0:DH, cols]).then_inc(o_in[s], 16)
                sp.dma_start(over_sums[s][:], inverse[bass.ds(H * b, H), cols].rearrange("h (a c) -> h a c", a=1).to_broadcast([H, DH, HALF])).then_inc(o_in[s], 16)

            sp.dma_start(last_sums[:], sums_of(heads_out, B - 1)).then_inc(sums_in, 16)
            for s in range(2):
                load_heads(0, s)
            sp.wait_ge(sums_done, 1)
            sp.dma_start(inverse_of(inverse, B - 1), last_sums[:]).then_inc(sums_in, 16)
            sp.wait_ge(sums_in, 32)
            with sp.Fori(1, B) as b:
                for s in range(2):
                    load_heads(b, s)
            sp.wait_ge(row_zero, 1)
            sp.dma_start(x_rows[B * S:B * S + 1, :], zero_row[:]).then_inc(rows_out, 16)
            for s in range(2):
                sp.sem_inc(xn_free[s], 16)
            with sp.Fori(0, B) as b:
                for s in range(2):
                    sp.wait_ge(xn_done[s], b + 1)
                    sp.dma_start(x_rows[bass.ds(S * b + HALF * s, HALF), 0:D].rearrange("(t p) d -> p t d", p=P), xn[s][:]).then_inc(xn_free[s], 16)
            sp.wait_ge(weights_done, 1)
            sp.dma_start(x_rows[0:B * S, D:ROW].rearrange("(t p) e -> p t e", p=P), weights[:]).then_inc(rows_out, 16)
            sp.wait_ge(rows_out, 32)
            for s in range(2):
                sp.wait_ge(xn_free[s], 16 * (B + 1))

        @block.gpsimd
        def _(pool):
            nc.gpsimd.memset(zero_row[:], 0.0).then_inc(row_zero, 1)
            for m in (upper, ones, same_expert, earlier):
                nc.gpsimd.memset(m[:], 1.0).then_inc(const_step, 1)
            for m, pattern, p_step in ((descending, [[-1, NE]], 0), (numbers, [[1, NE]], 0), (tile_counts, [[P, T]], 0),
                                       (run_tokens, [[0, NE], [P, T]], 0), (slot_numbers, [[1, SLOTS + BATCH]], 0),
                                       (ff["iota"], [[1, P]], 0), (ff["slot_index"], [[P, SLOTS + BATCH]], 1)):
                nc.gpsimd.iota(m[:], pattern=pattern, base=NE if m is descending else 0, channel_multiplier=p_step,
                               allow_small_or_imprecise_dtypes=True).then_inc(const_step, 1)
            pool.wait_ge(const_step, 11)
            nc.gpsimd.affine_select(out=upper[:], in_=upper[:], compare_op=ALU.is_ge, fill=0.0, base=0,
                                    pattern=[[1, P]], channel_multiplier=-1).then_inc(const_step, 1)
            nc.gpsimd.affine_select(out=earlier[:], in_=earlier[:], compare_op=ALU.is_gt, fill=0.0, base=0,
                                    pattern=[[1, NE], [-1, NE]], channel_multiplier=0).then_inc(const_step, 1)
            nc.gpsimd.affine_select(out=same_expert[:], in_=same_expert[:], compare_op=ALU.is_gt, fill=0.0, base=0,
                                    pattern=[[1, P]], channel_multiplier=-1).then_inc(const_step, 1)
            pool.wait_ge(const_step, 14)
            nc.gpsimd.affine_select(out=same_expert[:], in_=same_expert[:], compare_op=ALU.is_ge, fill=0.0, base=0,
                                    pattern=[[-T, P // T], [0, T]], channel_multiplier=1).then_inc(const_step, 1)
            nc.gpsimd.tensor_copy(starts[:, 1, :], run_tokens[:].rearrange("p e t -> p (e t)")).then_inc(const_step, 1)
            for c in range(2 * B):
                pool.wait_ge(mv_done, c + 1)
                nc.gpsimd.tensor_scalar(var_eps[:, SC * c:SC * c + SC], mean_var[:, SC * c:SC * c + SC, 1], EPS, 0.0, ALU.add, ALU.add).then_inc(eps_done, 1)
                pool.wait_ge(eps_done, c + 1)
                nc.gpsimd.tensor_tensor(rstd[:, SC * c:SC * c + SC], var_eps[:, SC * c:SC * c + SC], keep["neg_half"][:, 0:SC], ALU.pow).then_inc(rstd_done, 1)

        @block.vector
        def _(dve):
            def tokens_of(c):
                return x_all[:, SC * c:SC * c + SC, :]

            def divide(c):
                b, s = divmod(c, 2)
                dve.wait_ge(o_in[s], 32 * b + 32)
                dve.wait_ge(y_done[s], b + 1)
                nc.vector.tensor_tensor(oT[s][:], o_raw[s][:], over_sums[s][:], ALU.mult).then_inc(o_done[s], 1)

            def statistics(c):
                b, s = divmod(c, 2)
                dve.wait_ge(y_done[s], b + 2)
                nc.vector.tensor_tensor(tokens_of(c), ps[:, s, :].rearrange("p (t d) -> p t d", t=SC), tokens_of(c), ALU.add).then_inc(x1_done[s], 1)
                dve.wait_ge(x1_done[s], b + 2)
                for t in range(SC):
                    nc.vector.bn_stats(stats[:, SC * c + t, :], x_all[:, SC * c + t, :]).then_inc(stats_step, 1)
                dve.wait_ge(stats_step, SC * c + SC)
                for t in range(SC):
                    ins = nc.vector.bn_aggr(mean_var[:, SC * c + t, :], stats[:, SC * c + t, :])
                ins.then_inc(mv_done, 1)

            def normalise(c):
                b, s = divmod(c, 2)
                dve.wait_ge(rstd_done, c + 1)
                dve.wait_ge(xn_free[s], 16 * b + 16)
                dve.wait_ge(xT_done[s], b + 1)
                for t in range(SC):
                    n = SC * c + t
                    ins = nc.vector.tensor_scalar(xn[s][:, t, :], x_all[:, n, :], mean_var[:, n, 0:1], rstd[:, n:n + 1], ALU.subtract, ALU.mult)
                ins.then_inc(xn_done[s], 1)

            def low_part(c):
                b, s = divmod(c, 2)
                dve.wait_ge(xT_out[s], b + 1)
                nc.vector.tensor_tensor(ff["x_lo"][:, b, HALF * s:HALF * s + HALF], ps[:, 2 + s, :],
                                        ff["x_hi"][:, b, HALF * s:HALF * s + HALF].bitcast(F32), ALU.subtract).then_inc(xl_done[s], 1)

            for s in range(2):
                dve.sem_inc(o_done[s], 1)
            dve.wait_ge(sums_in, 16)
            nc.vector.reciprocal(last_sums[:], last_sums[:]).then_inc(sums_done, 1)
            divide(0)
            for c in range(2 * B):
                if c + 1 < 2 * B:
                    divide(c + 1)
                statistics(c)
            for c in range(2 * B + 1):
                if c < 2 * B:
                    normalise(c)
                if c > 0:
                    low_part(c - 1)

            done = [0]

            def then(ins):
                ins.then_inc(chain, 1)
                done[0] += 1
                dve.wait_ge(chain, done[0])

            def over_experts(ap):
                return ap.rearrange("p (t a) -> p t a", a=1).to_broadcast([P, T, NE])

            def over_tiles(ap):
                return ap.rearrange("p (a e) -> p a e", a=1).to_broadcast([P, T, NE])

            for s in range(2):
                dve.wait_ge(gate_exp[s], B + 1)
            dve.wait_ge(const_step, CONSTS)
            then(nc.vector.tensor_scalar(gates[:], gates[:], 1.0, None, ALU.add))
            then(nc.vector.reciprocal(gates[:], gates[:]))
            for k, (source, greatest) in enumerate(((gates, best), (rest, second))):
                then(nc.vector.reduce_max(greatest[:], source[:], AX))
                then(nc.vector.tensor_tensor(equal[:], source[:], over_experts(greatest[:]), ALU.is_equal))
                then(nc.vector.tensor_tensor(equal[:], equal[:], over_tiles(descending[:]), ALU.mult))
                then(nc.vector.reduce_max(pick[:], equal[:], AX))
                then(nc.vector.tensor_tensor(chosen[k][:], over_tiles(descending[:]), over_experts(pick[:]), ALU.is_equal))
                if k == 0:
                    then(nc.vector.scalar_tensor_tensor(out=rest[:], in0=chosen[0][:], scalar=-4.0, in1=gates[:], op0=ALU.mult, op1=ALU.add))
            then(nc.vector.tensor_tensor(both[:], chosen[0][:], chosen[1][:], ALU.add))
            then(nc.vector.tensor_copy(member[:], both[:].rearrange("p t e -> p e t")))
            flat = member[:].rearrange("p e t -> p (e t)")
            nc.vector.tensor_copy(member_step[:, 0:1], flat[:, 0:1])
            then(nc.vector.tensor_tensor(member_step[:, 1:NE * T], flat[:, 1:NE * T], flat[:, 0:NE * T - 1], ALU.subtract))
            nc.vector.sem_inc(member_done, 1)
            then(nc.vector.tensor_tensor(total[:], best[:], second[:], ALU.add))
            then(nc.vector.tensor_scalar(total[:], total[:], float(1 + TOP), None, ALU.mult))
            then(nc.vector.reciprocal(total[:], total[:]))
            then(nc.vector.tensor_tensor(weights[:], gates[:], both[:], ALU.mult))
            then(nc.vector.tensor_tensor(weights[:], weights[:], over_experts(total[:]), ALU.mult))
            nc.vector.sem_inc(weights_done, 1)
            inclusive = ps[:, 4, 0:NE * T]
            run_counts = ps[:, 4, NE * T:2 * NE * T].rearrange("p (e t) -> p e t", e=NE)
            dve.wait_ge(counted, 1)
            then(nc.vector.tensor_copy(counts[:], ps[:, 5, 0:2 * P].rearrange("p (h r) -> p h r", h=2)))
            nc.vector.sem_inc(counts_out, 1)
            then(nc.vector.tensor_copy(ff["table"][:, :, 0:P], ps[:, 6, 0:2 * P].rearrange("p (h r) -> p h r", h=2)))
            then(nc.vector.reduce_sum(n_expert[:], run_counts, AX))
            then(nc.vector.tensor_tensor(over[:], n_expert[:].rearrange("p (e a) -> p e a", a=1).to_broadcast([P, NE, T]),
                                         tile_counts[:].rearrange("p (a t) -> p a t", a=1).to_broadcast([P, NE, T]), ALU.is_gt))
            then(nc.vector.reduce_sum(n_tiles[:], over[:], AX))
            then(nc.vector.tensor_tensor(before[:], earlier[:], n_tiles[:].rearrange("p (a e) -> p a e", a=1).to_broadcast([P, NE, NE]), ALU.mult))
            then(nc.vector.reduce_sum(base[:], before[:], AX))
            then(nc.vector.tensor_tensor(end[:], base[:], n_tiles[:], ALU.add))
            dve.wait_ge(scanned, 1)
            then(nc.vector.scalar_tensor_tensor(out=starts[:, 0, :].rearrange("p (e t) -> p e t", e=NE),
                                                in0=base[:].rearrange("p (e a) -> p e a", a=1).to_broadcast([P, NE, T]), scalar=float(P),
                                                in1=ps[:, 7, 0:NE * T].rearrange("p (e t) -> p e t", e=NE), op0=ALU.mult, op1=ALU.add))
            eye2 = ident[:].rearrange("p (a c) -> p a c", a=1).to_broadcast([P, 2, P])
            eye4 = ident[:].rearrange("p (a b c) -> p a b c", a=1, b=1).to_broadcast([P, 2, 2, P])
            then(nc.vector.tensor_tensor(diagonal[:], starts[:, 0, :].rearrange("p (h r) -> p h r", h=2), eye2, ALU.mult))
            then(nc.vector.reduce_sum(start_column[:], diagonal[:], AX))
            nc.vector.tensor_copy(starts_step[:, :, 0:1], starts[:, :, 0:1])
            then(nc.vector.tensor_tensor(starts_step[:, :, 1:NE * T], starts[:, :, 1:NE * T], starts[:, :, 0:NE * T - 1], ALU.subtract))
            then(nc.vector.tensor_tensor(steps_diagonal[:], starts_step[:].rearrange("p k (h r) -> p k h r", h=2), eye4, ALU.mult))
            then(nc.vector.reduce_sum(step_columns[:], steps_diagonal[:], AX))
            then(nc.vector.tensor_copy(ff["table"][:, :, P:P + 2], step_columns[:].rearrange("p k h -> p h k")))
            then(nc.vector.tensor_tensor(ff["place"][:].rearrange("p e t -> p (e t)"), inclusive, starts[:, 0, :], ALU.add))
            then(nc.vector.scalar_tensor_tensor(out=ff["slot_start"][:],
                                                in0=slot_numbers[:].rearrange("p (a j) -> p a j", a=1).to_broadcast([P, 2, SLOTS + BATCH]), scalar=-float(P),
                                                in1=start_column[:].rearrange("p (h a) -> p h a", a=1).to_broadcast([P, 2, SLOTS + BATCH]),
                                                op0=ALU.mult, op1=ALU.add))
            then(nc.vector.tensor_tensor(past[:], end[:, 0:NE - 1].rearrange("p (a e) -> p a e", a=1).to_broadcast([P, SLOTS + BATCH, NE - 1]),
                                         slot_numbers[:].rearrange("p (j a) -> p j a", a=1).to_broadcast([P, SLOTS + BATCH, NE - 1]), ALU.is_le))
            then(nc.vector.reduce_sum(expert_f[:], past[:], AX))
            then(nc.vector.tensor_copy(ff["slot_expert"][:], expert_f[:]))
            then(nc.vector.tensor_tensor(ff["slot_onehot"][:], expert_f[:, 0:SLOTS].rearrange("p (j a) -> p j a", a=1).to_broadcast([P, SLOTS, NE]),
                                         numbers[:].rearrange("p (a e) -> p a e", a=1).to_broadcast([P, SLOTS, NE]), ALU.is_equal))

        @block.scalar
        def _(act):
            for s in range(2):
                act.sem_inc(gate_exp[s], 1)
            with act.Fori(0, B) as b:
                for s in range(2):
                    cols = slice(HALF * s, HALF * s + HALF)
                    act.wait_ge(xT_done[s], b + 2)
                    act.wait_ge(logit_done[s], b + 1)
                    nc.scalar.activation(ff["x_hi"][:, bass.ds(b, 1), cols].rearrange("p a c -> p (a c)"), ps[:, 2 + s, :], ACT.Copy).then_inc(xh_done[s], 1)
                    nc.scalar.activation(xT[s][:], ps[:, 2 + s, :], ACT.Copy).then_inc(xT_out[s], 1)
                for s in range(2):
                    act.wait_ge(logit_done[s], b + 2)
                    nc.scalar.activation(gates[:, bass.ds(TB * b + SC * s, SC), :], ps[:, 4 + s, 0:SC * NE].rearrange("p (t e) -> p t e", t=SC),
                                         ACT.Exp, scale=-1.0).then_inc(gate_exp[s], 1)

        @block.tensor
        def _(pe):
            for s in range(2):
                for free in (y_done, x1_done, xT_done, xl_done, logit_done):
                    pe.sem_inc(free[s], 1)
            with pe.Fori(0, B) as b:
                for s in range(2):
                    pe.wait_ge(o_done[s], b + 2)
                    pe.wait_ge(x1_done[s], b + 1)
                    for t in range(SC):
                        ins = nc.tensor.matmul(ps[:, s, P * t:P * t + P], oT[s][:, P * t:P * t + P], keep["woT"][:], start=True, stop=True)
                    ins.then_inc(y_done[s], 1)
            with pe.Fori(0, B) as b:
                for s in range(2):
                    pe.wait_ge(xn_done[s], b + 1)
                    pe.wait_ge(xl_done[s], b + 1)
                    pe.wait_ge(gate_exp[s], b + 1)
                    for t in range(SC):
                        ins = nc.tensor.transpose(ps[:, 2 + s, P * t:P * t + P], xn[s][:, t, :], ident[:])
                    ins.then_inc(xT_done[s], 1)
                for s in range(2):
                    pe.wait_ge(xT_out[s], b + 1)
                    for t in range(SC):
                        ins = nc.tensor.matmul(ps[:, 4 + s, NE * t:NE * t + NE], xT[s][:, P * t:P * t + P], keep["wg"][:], start=True, stop=True)
                    ins.then_inc(logit_done[s], 1)
            pe.wait_ge(member_done, 1)
            flat = member[:].rearrange("p e t -> p (e t)")
            nc.tensor.matmul(ps[:, 4, 0:NE * T], upper[:], flat, start=True, stop=True)
            nc.tensor.matmul(ps[:, 4, NE * T:2 * NE * T], ones[:], flat, start=True, stop=True)
            for h in range(2):
                nc.tensor.matmul(ps[:, 5, P * h:P * h + P], flat[:, P * h:P * h + P], ones[:], start=True, stop=True)
            for h in range(2):
                ins = nc.tensor.matmul(ps[:, 6, P * h:P * h + P], member_step[:, P * h:P * h + P], upper[:], start=True, stop=True)
            ins.then_inc(counted, 1)
            pe.wait_ge(counts_out, 1)
            for h in range(2):
                ins = nc.tensor.matmul(ps[:, 7, P * h:P * h + P], counts[:, h, :], same_expert[:], start=True, stop=True)
            ins.then_inc(scanned, 1)


def experts(nc, keep, ff, x_rows, y_rows):
    ident = keep["ident"]
    with ExitStack() as ctx:
        def sb(name, shape, dt=F32):
            return ctx.enter_context(nc.sbuf_tensor(name, shape, dt))

        def sem(name):
            return ctx.enter_context(nc.semaphore(name))

        def sems(name, n=2):
            return [sem(f"{name}{s}") for s in range(n)]

        RING = 2 * BATCH
        ITERS = SLOTS // RING
        run_reached = [sb(f"run_reached{i}", [P, 2, P], BF16) for i in range(BATCH)]
        placed, place_sum = sb("placed", [P, T, NE]), sb("place_sum", [P, T])
        within = sb("within", [P, BATCH])
        passed_by = sb("passed_by", [P, BATCH, P])
        n_passed = sb("n_passed", [P, BATCH])
        tokens = [[sb(f"tokens{g}_{i}", [P, 1], U32) for i in range(BATCH)] for g in range(2)]
        rows = sb("rows", [P, RING, ROW])
        row_weights = sb("row_weights", [P, BATCH, NE])
        wt = sb("wt", [P, 2, BATCH])
        xh = [sb(f"rows_hi{i}", [P, P], F32R) for i in range(2)]
        xl = [sb(f"rows_lo{i}", [P, P], F32R) for i in range(2)]
        act_out = [sb(f"act_out{i}", [P, FF]) for i in range(2)]
        hid = [sb(f"hid{i}", [P, FF]) for i in range(2)]
        hidT = [sb(f"hidT{i}", [P, FF]) for i in range(2)]
        y = [sb(f"y{g}", [P, BATCH, D]) for g in range(2)]
        ps_up = ctx.enter_context(nc.psum_tensor("ps_up", [P, 2, 512], F32))
        ps_hT = ctx.enter_context(nc.psum_tensor("ps_hT", [P, 2, 512], F32))
        ps_y = ctx.enter_context(nc.psum_tensor("ps_y", [P, 2, 512], F32))
        ps_xT = ctx.enter_context(nc.psum_tensor("ps_xT", [P, 512], F32))
        ps_run = ctx.enter_context(nc.psum_tensor("ps_run", [P, BATCH, P + 2], F32))

        reached, looked_up, ids_step, ids_done = sem("reached"), sem("looked_up"), sem("ids_step"), sem("ids_done")
        gathered, wt_step, wt_done = ff["row_gathers"], sem("wt_step"), sem("wt_done")
        xT_done, xh_done, xl_done = sem("xT_done3"), sem("xh_done3"), sem("xl_done3")
        up_done, act_done, hid_done = sem("up_done"), sem("act_done"), sem("hid_done")
        hT_done, hT_out, down_done, y_out = sem("hT_done"), sem("hT_out"), sem("down_done"), sem("y_out")
        y_free = sems("y_free")
        place_step = sem("place_step")
        passed = sem("passed3")
        block = ctx.enter_context(nc.Block())


        def steps(eng, body):
            for v in range(BATCH, RING):
                body(v - RING, -1, v)
            with eng.Fori(0, ITERS - 1) as it:
                for v in range(RING):
                    body(RING * it + v, it, v)
            for v in range(RING):
                body(RING * (ITERS - 1) + v, ITERS - 1, v)

        def there(t):
            return not isinstance(t, int) or 0 <= t < SLOTS

        def wait_free(eng, semaphore, count):
            if not isinstance(count, int) or count > 0:
                eng.wait_ge(semaphore, count)

        @block.sync
        def _(sp):
            for g in range(2):
                sp.sem_inc(y_free[g], 16)
            with sp.Fori(0, ITERS) as it:
                for g in range(2):
                    sp.wait_ge(y_out, RING * it + BATCH * g + BATCH)
                    sp.dma_start(y_rows[bass.ds((RING * it + BATCH * g) * P, BATCH * P), :].rearrange("(i p) d -> p i d", p=P), y[g][:]).then_inc(y_free[g], 16)
            for g in range(2):
                sp.wait_ge(y_free[g], 16 * (ITERS + 1))

        @block.gpsimd
        def _(pool):
            with pool.Fori(0, ITERS) as it:
                for g in range(2):
                    pool.wait_ge(ids_done, 2 * it + g + 1)
                    pool.wait_ge(xT_done, RING * it + BATCH * g + BATCH)
                    pool.wait_ge(wt_done, 2 * it + g + 1)
                    pool.sem_inc(passed, 1)
                    for i in range(BATCH):
                        nc.gpsimd.indirect_dma_start(rows[:, BATCH * g + i, :], None, x_rows,
                                                     bass.IndirectOffsetOnAxis(ap=tokens[g][i][:, 0:1], axis=0)).then_inc(gathered[g], 16)

        @block.vector
        def _(dve):
            def reach(q):
                for i in range(BATCH):
                    for h in range(2):
                        ins = nc.vector.tensor_scalar(run_reached[i][:, h, :], ff["iota"][:], ff["slot_start"][:, h, bass.ds(BATCH * q + i, 1)], None, ALU.is_ge)
                ins.then_inc(reached, 1)

            def find_tokens(q, g):
                dve.wait_ge(looked_up, q + 1)
                nc.vector.tensor_tensor(within[:], ff["slot_index"][:, bass.ds(BATCH * q, BATCH)], ps_run[:, :, P], ALU.subtract).then_inc(ids_step, 1)
                dve.wait_ge(ids_step, 3 * q + 1)
                nc.vector.tensor_tensor(passed_by[:], ps_run[:, :, 0:P],
                                        within[:].rearrange("p (j a) -> p j a", a=1).to_broadcast([P, BATCH, P]), ALU.is_le).then_inc(ids_step, 1)
                dve.wait_ge(ids_step, 3 * q + 2)
                nc.vector.reduce_sum(n_passed[:], passed_by[:], AX).then_inc(ids_step, 1)
                dve.wait_ge(ids_step, 3 * q + 3)
                for i in range(BATCH):
                    ins = nc.vector.tensor_tensor(tokens[g][i][:], n_passed[:, i:i + 1], ps_run[:, i, P + 1:P + 2], ALU.add)
                ins.then_inc(ids_done, 1)

            def take_weights(q, it, g):
                dve.wait_ge(gathered[g], 16 * BATCH * it + 16 * BATCH)
                nc.vector.tensor_tensor(row_weights[:], rows[:, BATCH * g:BATCH * g + BATCH, D:ROW],
                                        ff["slot_onehot"][:, bass.ds(BATCH * q, BATCH), :], ALU.mult).then_inc(wt_step, 1)
                dve.wait_ge(wt_step, q + 1)
                nc.vector.reduce_sum(wt[:, g, :], row_weights[:], AX).then_inc(wt_done, 1)
                dve.wait_ge(wt_done, q + 3)

            def body(j, it, v):
                batch = j // BATCH if isinstance(j, int) else 2 * it + v // BATCH
                g_next, q_next = (v // BATCH + 1) % 2, batch + 1
                if v % BATCH == 0 and there(j + 3):
                    take_weights(q_next, it + (v + BATCH) // RING, g_next)
                if there(j + 3):
                    dve.wait_ge(xh_done, j + 4)
                    nc.vector.tensor_tensor(xl[(v + 3) % 2][:], ps_xT[:, 0:P], xh[(v + 3) % 2][:].bitcast(F32), ALU.subtract).then_inc(xl_done, 1)
                if there(j + 2):
                    w = (v + 2) % RING
                    dve.wait_ge(act_done, j + 3)
                    nc.vector.scalar_tensor_tensor(out=hid[w % 2][:], in0=ps_up[:, w % 2, FF:2 * FF], scalar=wt[:, w // BATCH, w % BATCH:w % BATCH + 1],
                                                   in1=act_out[w % 2][:], op0=ALU.mult, op1=ALU.mult).then_inc(hid_done, 1)
                if there(j + 9):
                    if v % BATCH == 0:
                        reach(batch + 3)
                    if v % BATCH == 1:
                        find_tokens(batch + 3, g_next)

            dve.sem_inc(wt_done, 2)
            for q in range(2):
                reach(q)
                find_tokens(q, q)
            for k in range(TOP):
                nc.vector.tensor_tensor(placed[:], ff["place"][:].rearrange("p e t -> p t e"), ff["chosen"][k][:], ALU.mult).then_inc(place_step, 1)
                dve.wait_ge(place_step, 3 * k + 1)
                nc.vector.reduce_sum(place_sum[:], placed[:], AX).then_inc(place_step, 1)
                dve.wait_ge(place_step, 3 * k + 2)
                nc.vector.tensor_scalar(ff["position"][:, k, :], place_sum[:], -1.0, None, ALU.add).then_inc(place_step, 1)
                dve.wait_ge(place_step, 3 * k + 3)
            steps(dve, body)

        @block.scalar
        def _(act):
            def body(j, it, v):
                if there(j + 2):
                    a = (v + 2) % 2
                    act.wait_ge(up_done, j + 3)
                    nc.scalar.activation(act_out[a][:], ps_up[:, a, 0:FF], ACT.Silu).then_inc(act_done, 1)
                if there(j + 3):
                    act.wait_ge(xT_done, RING + j + 4)
                    nc.scalar.activation(xh[(v + 3) % 2][:], ps_xT[:, 0:P], ACT.Copy).then_inc(xh_done, 1)
                if there(j + 1):
                    a = (v + 1) % 2
                    act.wait_ge(hT_done, j + 2)
                    nc.scalar.activation(hidT[a][:], ps_hT[:, a, 0:FF], ACT.Copy).then_inc(hT_out, 1)
                if there(j):
                    act.wait_ge(down_done, j + 1)
                    if v % BATCH == 0:
                        act.wait_ge(y_free[v // BATCH], 16 * it + 16)
                    nc.scalar.activation(y[v // BATCH][:, v % BATCH, :], ps_y[:, v % 2, 0:D], ACT.Copy).then_inc(y_out, 1)

            steps(act, body)

        @block.tensor
        def _(pe):
            def look_up(q):
                pe.wait_ge(reached, q + 1)
                wait_free(pe, ids_done, q)
                for i in range(BATCH):
                    for h in range(2):
                        ins = nc.tensor.matmul(ps_run[:, i, :], run_reached[i][:, h, :], ff["table"][:, h, :], start=(h == 0), stop=(h == 1))
                ins.then_inc(looked_up, 1)

            here = {}

            def load_experts(j):
                values = nc.values_load_multi_w_load_instructions(
                    ff["slot_expert"][0:1, bass.ds(j, RING + 2)], engines=(mybir.EngineType.PE,), min_val=0, max_val=NE - 1,
                    skip_runtime_bounds_check_because="each is a sum of seven comparisons")[1]
                here.clear()
                here.update(enumerate(values))

            def body(j, it, v):
                if v == 0:
                    load_experts(j)
                if there(j + 2):
                    a = (v + 2) % 2
                    pe.wait_ge(xl_done, j + 3)
                    e = bass.ds(here[v + 2 if not isinstance(j, int) or j >= 0 else v + 2 - RING], 1)
                    hi, lo = (keep[name][:, e, :].rearrange("p a c -> p (a c)") for name in ("w13_hi", "w13_lo"))
                    nc.tensor.matmul(ps_up[:, a, :], xh[a][:], hi, start=True, stop=False)
                    nc.tensor.matmul(ps_up[:, a, :], xl[a][:], hi, start=False, stop=False)
                    nc.tensor.matmul(ps_up[:, a, :], xh[a][:], lo, start=False, stop=True).then_inc(up_done, 1)
                if there(j + 3):
                    w = (v + 3) % RING
                    if v % BATCH == 0:
                        pe.wait_ge(gathered[w // BATCH], 16 * BATCH * (it + (v + 3) // RING) + 16 * BATCH)
                    nc.tensor.transpose(ps_xT[:, 0:P], rows[:, w, 0:D], ident[:]).then_inc(xT_done, 1)
                if v % BATCH == 1 and there(j + 8):
                    look_up((j - 1) // BATCH + 3 if isinstance(j, int) else 2 * it + v // BATCH + 3)
                if there(j + 1):
                    a = (v + 1) % 2
                    pe.wait_ge(hid_done, j + 2)
                    for c in range(2):
                        ins = nc.tensor.transpose(ps_hT[:, a, P * c:P * c + P], hid[a][:, P * c:P * c + P], ident[:])
                    ins.then_inc(hT_done, 1)
                if there(j):
                    pe.wait_ge(hT_out, j + 1)
                    for c in range(2):
                        ins = nc.tensor.matmul(ps_y[:, v % 2, 0:D], hidT[v % 2][:, P * c:P * c + P],
                                               keep["w2"][:, bass.ds(here[v], 1), c, :].rearrange("p a d -> p (a d)"), start=(c == 0), stop=(c == 1))
                    ins.then_inc(down_done, 1)

            load_experts(0)
            pe.sem_inc(xT_done, RING)
            for q in range(2):
                look_up(q)
            steps(pe, body)


def combine(nc, keep, ff, y_rows, out_tiles):
    x_all = keep["x_all"]
    with ExitStack() as ctx:
        def sb(name, shape, dt=F32):
            return ctx.enter_context(nc.sbuf_tensor(name, shape, dt))

        def sem(name):
            return ctx.enter_context(nc.semaphore(name))

        def sems(name, n=2):
            return [sem(f"{name}{s}") for s in range(n)]

        GATHERS = TOP * SC
        CHUNKS_OUT = T // SC
        places = [[sb(f"places{s}_{i}", [P, 1], U32) for i in range(GATHERS)] for s in range(2)]
        routed = [sb(f"routed{s}", [P, GATHERS, D]) for s in range(2)]
        act_out = [sb(f"act_out_s{i}", [P, HALF]) for i in range(2)]
        hidT = [sb(f"hidT_s{i}", [P, HALF]) for i in range(2)]
        y = [sb(f"y_s{s}", [P, SC, D]) for s in range(2)]
        ps_up = ctx.enter_context(nc.psum_tensor("ps_up_s", [P, 2, 2, 512], F32))
        ps_y = ctx.enter_context(nc.psum_tensor("ps_y_s", [P, 2, 512], F32))

        places_ready, gathered, up_done, act_done, hid_done = sems("places_ready"), ff["output_gathers"], sems("up_done_s"), sems("act_done_s"), sems("hid_done_s")
        down_done, shared_added, first_added, y_out, y_free = sems("down_done_s"), sems("shared_added"), sems("first_added"), sems("y_out_s"), sems("y_free_s")
        passed = sem("passed4")
        block = ctx.enter_context(nc.Block())


        @block.sync
        def _(sp):
            for s in range(2):
                sp.sem_inc(y_free[s], 16)
            with sp.Fori(0, CHUNKS_OUT // 2) as it:
                for s in range(2):
                    sp.wait_ge(y_out[s], it + 2)
                    sp.dma_start(out_tiles[:, bass.ds(TB * it + SC * s, SC), :], y[s][:]).then_inc(y_free[s], 16)
            for s in range(2):
                sp.wait_ge(y_free[s], 16 * (CHUNKS_OUT // 2 + 1))

        @block.gpsimd
        def _(pool):
            with pool.Fori(0, CHUNKS_OUT // 2) as it:
                for s in range(2):
                    pool.wait_ge(places_ready[s], it + 1)
                    pool.wait_ge(y_out[s], it + 1)
                    pool.sem_inc(passed, 1)
                    for i in range(GATHERS):
                        nc.gpsimd.indirect_dma_start(routed[s][:, i, :], None, y_rows,
                                                     bass.IndirectOffsetOnAxis(ap=places[s][i][:, 0:1], axis=0)).then_inc(gathered[s], 16)

        @block.vector
        def _(dve):
            def put_places(it, s):
                for k in range(TOP):
                    for t in range(SC):
                        n = bass.ds(TB * it + SC * s + t, 1)
                        ins = nc.vector.tensor_copy(places[s][k * SC + t][:], ff["position"][:, k, n])
                ins.then_inc(places_ready[s], 1)

            def body(it, s, more):
                rows = x_all[:, bass.ds(TB * it + SC * s, SC), :]
                for c in range(2):
                    dve.wait_ge(act_done[c], 2 * it + s + 1)
                    dve.wait_ge(down_done[(s + 1) % 2], it + s + 0 + 1)
                    nc.vector.tensor_tensor(hidT[c][:], ps_up[:, c, 1, :], act_out[c][:], ALU.mult).then_inc(hid_done[c], 1)
                dve.wait_ge(down_done[s], it + 2)
                nc.vector.scalar_tensor_tensor(out=rows, in0=ps_y[:, s, :].rearrange("p (t d) -> p t d", t=SC), scalar=1.0 / (1 + TOP),
                                               in1=rows, op0=ALU.mult, op1=ALU.add).then_inc(shared_added[s], 1)
                dve.wait_ge(gathered[s], 16 * GATHERS * it + 16 * GATHERS)
                if more:
                    put_places(it + 1, s)
                dve.wait_ge(shared_added[s], it + 2)
                nc.vector.tensor_tensor(rows, rows, routed[s][:, 0:SC, :], ALU.add).then_inc(first_added[s], 1)
                dve.wait_ge(first_added[s], it + 1)
                dve.wait_ge(y_free[s], 16 * it + 16)
                nc.vector.tensor_tensor(y[s][:], rows, routed[s][:, SC:GATHERS, :], ALU.add).then_inc(y_out[s], 1)

            for s in range(2):
                dve.sem_inc(y_out[s], 1)
                put_places(0, s)
            with dve.Fori(0, CHUNKS_OUT // 2 - 1) as it:
                for s in range(2):
                    body(it, s, True)
            for s in range(2):
                body(CHUNKS_OUT // 2 - 1, s, False)

        @block.scalar
        def _(act):
            for c in range(2):
                act.sem_inc(hid_done[c], 1)
            with act.Fori(0, CHUNKS_OUT // 2) as it:
                for s in range(2):
                    for c in range(2):
                        act.wait_ge(up_done[c], 2 * it + s + 1)
                        act.wait_ge(hid_done[c], 2 * it + s + 1)
                        nc.scalar.activation(act_out[c][:], ps_up[:, c, 0, :], ACT.Silu).then_inc(act_done[c], 1)

        @block.tensor
        def _(pe):
            def up(it, s):
                for c in range(2):
                    pe.wait_ge(hid_done[c], 2 * it + s + 1)
                    for k in range(2):
                        col = FF * k + P * c
                        hi, lo = keep["w13_hi"][:, NE, col:col + P], keep["w13_lo"][:, NE, col:col + P]
                        xh, xl = (ff[n][:, bass.ds(it, 1), HALF * s:HALF * s + HALF].rearrange("p a c -> p (a c)") for n in ("x_hi", "x_lo"))
                        nc.tensor.matmul(ps_up[:, c, k, :], hi, xh, start=True, stop=False)
                        nc.tensor.matmul(ps_up[:, c, k, :], hi, xl, start=False, stop=False)
                        ins = nc.tensor.matmul(ps_up[:, c, k, :], lo, xh, start=False, stop=True)
                    ins.then_inc(up_done[c], 1)

            for s in range(2):
                pe.sem_inc(down_done[s], 1)
                pe.sem_inc(shared_added[s], 1)
            with pe.Fori(0, CHUNKS_OUT // 2) as it:
                for s in range(2):
                    up(it, s)
                    for c in range(2):
                        pe.wait_ge(hid_done[c], 2 * it + s + 2)
                    pe.wait_ge(shared_added[s], it + 1)
                    for t in range(SC):
                        for c in range(2):
                            ins = nc.tensor.matmul(ps_y[:, s, P * t:P * t + P], hidT[c][:, P * t:P * t + P],
                                                   keep["w2"][:, NE, c, :], start=(c == 0), stop=(c == 1))
                    ins.then_inc(down_done[s], 1)


_INS = ["L0_attn_x", "L0_attn_Wq", "L0_attn_bq", "L0_attn_Wk", "L0_attn_bk", "L0_attn_Wv", "L0_attn_bv", "L0_attn_Wo",
        "L0_attn_bo", "L0_ffn_Wg", "L0_ffn_Ws1", "L0_ffn_Ws3", "L0_ffn_Ws2", "L0_ffn_We1", "L0_ffn_We3", "L0_ffn_We2"]


def kernel(**inputs):
    import numpy as np
    import concourse.bacc as bacc
    from concourse.bass_utils import run_bass_kernel_spmd

    nc = bacc.Bacc("TRN2", target_bir_lowering=False, num_devices=1)
    arrays, args = {}, []
    for name in _INS:
        a = np.ascontiguousarray(inputs[name])
        arrays[f"in_{name}"] = a
        args.append(nc.dram_tensor(f"in_{name}", a.shape, mybir.dt.from_np(a.dtype), kind="ExternalInput").ap())
    out = nc.dram_tensor("out_x", (B, S, D), F32, kind="ExternalOutput").ap()
    layer_kernel(nc, *args, out)
    r = run_bass_kernel_spmd(nc, [arrays], core_ids=[0])
    return r.results[0]["out_x"]
```

```python
from contextlib import ExitStack

import concourse.bass as bass
from concourse import mybir

F32 = mybir.dt.float32
F32R = mybir.dt.float32r
BF16 = mybir.dt.bfloat16
U32 = mybir.dt.uint32
I32 = mybir.dt.int32
ACT = mybir.ActivationFunctionType
ALU = mybir.AluOpType
AX = mybir.AxisListType.X

P = 128
D = 128
B, S = 4, 1024
H, DH = 16, 8
GH = 4
GB = H // GH
NG = B * GB
ROWS = P // GH
PARTS = 3 * DH
T = B * S // P
TB = S // P
HALF = S // 2
SC = 4
FF = 256
NE = 8
UNITS = NE + 1
EPS = 1e-5
TOP = 2
SLOTS = 72
BATCH = 3
ROW = D + NE
MASKED = -1.0e30
SCALE = float(DH) ** -0.5

TILES = [
    [(0, 0, 512), (0, 512, 512)],
    [(7, 0, 128), (1, 128, 384), (1, 512, 512)],
    [(6, 0, 256), (2, 256, 256), (2, 512, 512)],
    [(5, 0, 384), (3, 384, 128), (3, 512, 512)],
]
DIAGONALS = [[0], [0, 128], [0, 256], [0, 384], [0, 512]]
NTYPE = 5
STEPS = 4 * GH + GH // 2
TYPE_END = [4, 8, 12, 16, 18]


def query_of(j, c):
    return c + (S - P * (8 - j) if j > 4 else 0)


def half_pieces(hs):
    st, half = divmod(hs, 2)
    if st < 16:
        t, h = divmod(st, GH)
        return [(h, j, c % HALF, w, query_of(j, c)) for j, c, w in TILES[t] if c // HALF == half]
    return [(2 * (st - 16) + 1 - half, 4, 0, 512, 512)]


def values_chunks():
    cuts = {512: (256, 256)}
    order = [[0, 1], [1, 0, 2], [1, 0, 2], [1, 0, 2]]
    out = []
    for t, pieces in enumerate(TILES):
        for j, c, w in [pieces[i] for i in order[t]]:
            for part in cuts.get(w, (w,)):
                out.append((t, j, c, part, query_of(j, c)))
                c += part
    return out + [(4, 4, c, 256, 512 + c) for c in (0, 256)]


def max_segments():
    out = []
    for i in range(S // ROWS):
        n = ROWS * (i + 1)
        if n <= 512:
            out.append((i, 0, n, i, True))
        else:
            out.append((i, 0, n // 2, i, False))
            out.append((i, n // 2, n // 2, i + 16, True))
    return out


SEGMENTS = max_segments()
NSEG = len(SEGMENTS)
CHUNKS = values_chunks()
LAG = 4
HALVES = 2 * STEPS
AHEAD = 3
MAX_AT = 7
LOWER_LAST = max(i for i, (t, j, c, w, q) in enumerate(CHUNKS) if q < HALF)


def segments_by_chunk():
    cost = [s[2] for s in SEGMENTS]
    total, at, out = sum(cost), 0.0, [[] for _ in range(STEPS)]
    for n, c in enumerate(cost):
        u = MAX_AT + min(int(at / total * STEPS), STEPS - 1)
        out[u % STEPS].append((2 if u < STEPS else 1, n))
        at += c
    return out


SEGS_BY_CHUNK = segments_by_chunk()


def layer_kernel(nc, x, Wq, bq, Wk, bk, Wv, bv, Wo, bo, Wg, Ws1, Ws3, Ws2, We1, We3, We2, out):
    q_parts = nc.dram_tensor("q_parts", (B, H, 2 * DH + 2, S), F32).ap()
    k_parts = nc.dram_tensor("k_parts", (B, H, 2 * DH, S), F32).ap()
    heads_out = nc.dram_tensor("heads_out", (B * H, DH + 1, S), F32).ap()
    inverse = nc.dram_tensor("inverse", (B * H, S), F32).ap()
    x_tiles = x.rearrange("b (n p) d -> p (b n) d", p=P)
    out_tiles = out.rearrange("b (n p) d -> p (b n) d", p=P)
    with ExitStack() as ctx:
        def sb(name, shape, dt=F32, where=ctx):
            return where.enter_context(nc.sbuf_tensor(name, shape, dt))

        ident = sb("ident", [P, P])
        x_all = sb("x_all", [P, T, D])
        woT = sb("woT", [P, D])
        row_consts = sb("row_consts", [P, 2, D])
        wg = sb("wg", [P, NE])
        neg_half = sb("neg_half", [P, TB])
        w13_hi = sb("w13_hi", [P, UNITS, 2 * FF], F32R)
        w13_lo = sb("w13_lo", [P, UNITS, 2 * FF], F32R)
        w2 = sb("w2", [P, UNITS, 2, D])
        with ExitStack() as attn:
            keep = dict(
                ident=ident, x_all=x_all, woT=woT, row_consts=row_consts, neg_half=neg_half, wg=wg,
                w13_hi=w13_hi, w13_lo=w13_lo, w2=w2,
                ident_bf=sb("ident_bf", [P, P], BF16, attn),
                mask_bf=sb("mask_bf", [P, ROWS], BF16, attn),
                v_all=sb("v_all", [P, NG, TB, GH * DH], F32, attn),
                q_diag=[sb(f"q_diag{i}", [P, S // ROWS, GH, ROWS], F32R, attn) for i in range(3)],
                k_rows=[sb(f"k_rows{i}", [P, S], F32R, attn) for i in range(3)],
                v_one=[sb(f"v_one{i}", [P, TB, GH, ROWS], F32, attn) for i in range(3)],
            )
            prepare(nc, keep, x_tiles, Wq, bq, Wk, bk, Wv, bv, Wo, bo, Wg, q_parts, k_parts)
            attention(nc, keep, q_parts, k_parts, heads_out, inverse, Ws1, Ws3, Ws2, We1, We3, We2)
        feed_forward(nc, keep, heads_out, inverse, out_tiles)


def prepare(nc, keep, x_tiles, Wq, bq, Wk, bk, Wv, bv, Wo, bo, Wg, q_parts, k_parts):
    ident, x_all = keep["ident"], keep["x_all"]
    semaphores = []
    with ExitStack() as ctx:
        def sb(name, shape, dt=F32):
            return ctx.enter_context(nc.sbuf_tensor(name, shape, dt))

        def pair(name, shape, dt=F32):
            return [sb(f"{name}{s}", shape, dt) for s in range(2)]

        def sem(name):
            semaphores.append(nc.alloc_semaphore(name))
            return semaphores[-1]

        def sems(name):
            return [sem(f"{name}{s}") for s in range(2)]

        w_raw = sb("w_raw", [P, 4, D])
        w_hi = sb("w_hi", [P, 3, D], F32R)
        w_lo = sb("w_lo", [P, 3, D], F32R)
        bias_cols = sb("bias_cols", [P, 2])
        zeros = sb("zeros", [P, S])
        stats = sb("stats", [P, T, 6])
        mean_var = sb("mean_var", [P, T, 2])
        var_eps = sb("var_eps", [P, T])
        rstd = sb("rstd", [P, T])
        xn = pair("xn", [P, SC, D])
        xh = pair("xh", [P, SC * P], F32R)
        xl = pair("xl", [P, SC * P], F32R)
        qf, kf = pair("qf", [P, HALF]), pair("kf", [P, HALF])
        qh, kh = pair("qh", [P, HALF], F32R), pair("kh", [P, HALF], F32R)
        ql, kl = pair("ql", [P, HALF], F32R), pair("kl", [P, HALF], F32R)
        ps = ctx.enter_context(nc.psum_tensor("ps_prep", [P, 8, 512], F32))

        x_in, w_in, b_in, mat_in = sem("x_in"), sem("w_in"), sem("b_in"), sem("mat_in")
        consts, ident_ready, wT_done, w_hi_done = sem("consts"), sem("ident_ready"), sem("wT_done"), sem("w_hi_done")
        w_ready, fills, pool_fills = sem("w_ready"), sem("fills"), sem("pool_fills")
        stats_step, mv_done, eps_done, rstd_done = sem("stats_step"), sem("mv_done"), sem("eps_done"), sem("rstd_done")
        xn_done, xT_done, xh_done, xl_done = sems("xn_done"), sems("xT_done"), sems("xh_done"), sems("xl_done")
        q_done, k_done, v_done = sems("q_done"), sems("k_done"), sems("v_done")
        qf_done, kf_done, qh_done, kh_done = sems("qf_done"), sems("kf_done"), sems("qh_done"), sems("kh_done")
        ql_done, kl_done, v_out = sems("ql_done"), sems("kl_done"), sems("v_out")
        stored, rows_out = sems("stored"), sem("rows_out")
        passed, passed_sync = sem("passed0"), sem("passed_sync")
        block = ctx.enter_context(nc.Block())
        FILLS = 11
        STORED = 16 * 4

        @block.sync
        def _(sp):
            sp.dma_start(x_all[:, 0:TB, :], x_tiles[:, 0:TB, :]).then_inc(x_in, 16)
            for n, w in enumerate((Wq, Wk, Wv, Wo)):
                sp.dma_start(w_raw[:, n, :], w).then_inc(w_in, 16)
            for n, b in enumerate((bq, bk)):
                sp.dma_start(bias_cols[:, n:n + 1], b.rearrange("(p a) -> p a", a=1)).then_inc(b_in, 16)
            for n, b in enumerate((bv, bo)):
                sp.dma_start(keep["row_consts"][:, n, :], b.rearrange("(a n) -> a n", a=1).to_broadcast([P, D])).then_inc(b_in, 16)
            sp.dma_start(keep["wg"][:], Wg).then_inc(b_in, 16)
            sp.wait_ge(x_in, 16)
            for b in range(1, B):
                sp.dma_start(x_all[:, TB * b:TB * b + TB, :], x_tiles[:, TB * b:TB * b + TB, :]).then_inc(x_in, 16)
                sp.wait_ge(x_in, 16 * (b + 1))
            for s in range(2):
                sp.sem_inc(stored[s], STORED)
            with sp.Fori(0, B) as b:
                for s in range(2):
                    cols = slice(HALF * s, HALF * s + HALF)
                    qd = q_parts[bass.ds(b, 1), :, :, cols].rearrange("b h r c -> (b h) r c")
                    kd = k_parts[bass.ds(b, 1), :, :, cols].rearrange("b h r c -> (b h) r c")
                    sp.wait_ge(qh_done[s], b + 1)
                    sp.sem_inc(passed_sync, 1)
                    sp.dma_start(qd[:, DH:2 * DH, :], qh[s][:].bitcast(F32)).then_inc(stored[s], 16)
                    sp.wait_ge(kh_done[s], b + 1)
                    sp.sem_inc(passed_sync, 1)
                    sp.dma_start(kd[:, 0:DH, :], kh[s][:].bitcast(F32)).then_inc(stored[s], 16)
                    sp.wait_ge(ql_done[s], b + 2)
                    sp.sem_inc(passed_sync, 1)
                    sp.dma_start(qd[:, 0:DH, :], ql[s][:].bitcast(F32)).then_inc(stored[s], 16)
                    sp.wait_ge(kl_done[s], b + 2)
                    sp.sem_inc(passed_sync, 1)
                    sp.dma_start(kd[:, DH:2 * DH, :], kl[s][:].bitcast(F32)).then_inc(stored[s], 16)
            for s in range(2):
                sp.wait_ge(stored[s], STORED * (B + 1))

        @block.gpsimd
        def _(pool):
            mask, identb = keep["mask_bf"], keep["ident_bf"]
            nc.gpsimd.memset(ident[:], 0.0).then_inc(consts, 1)
            nc.gpsimd.memset(identb[:], 0.0).then_inc(consts, 1)
            nc.gpsimd.memset(mask[:], 0.0).then_inc(consts, 1)
            pool.wait_ge(consts, 3)
            for m in (ident, identb):
                nc.gpsimd.affine_select(out=m[:], in_=m[:], compare_op=ALU.not_equal, fill=1.0, base=0,
                                        pattern=[[-1, P]], channel_multiplier=1).then_inc(ident_ready, 1)
            pool.wait_ge(ident_ready, 2)
            nc.gpsimd.memset(keep["neg_half"][:], -0.5).then_inc(consts, 1)
            pool.wait_ge(consts, 4)

            def fill(c):
                if c == 0:
                    for h in range(GH):
                        m = mask[ROWS * h:ROWS * h + ROWS, :]
                        nc.gpsimd.affine_select(out=m, in_=m, compare_op=ALU.is_ge, fill=MASKED, base=0,
                                                pattern=[[-1, ROWS]], channel_multiplier=1).then_inc(ident_ready, 1)
                        pool.wait_ge(ident_ready, 3 + h)
                    nc.gpsimd.memset(zeros[:], 0.0).then_inc(pool_fills, 1)
                if 1 <= c <= 3:
                    i = c - 1
                    nc.gpsimd.memset(keep["v_one"][i][:], 0.0).then_inc(pool_fills, 1)
                    nc.gpsimd.memset(keep["k_rows"][i][:].bitcast(F32), 1.0).then_inc(pool_fills, 1)
                    pool.wait_ge(pool_fills, 1 + 3 * i + 2)
                    nc.gpsimd.memset(keep["v_one"][i][:, :, :, DH:DH + 1], 1.0).then_inc(pool_fills, 1)
                if c == 4:
                    nc.gpsimd.memset(keep["q_diag"][2][:].bitcast(F32), 0.0).then_inc(pool_fills, 1)

            def root(c):
                t = slice(SC * c, SC * c + SC)
                pool.wait_ge(mv_done, c + 1)
                nc.gpsimd.tensor_scalar(var_eps[:, t], mean_var[:, t, 1], EPS, 0.0, ALU.add, ALU.add).then_inc(eps_done, 1)
                pool.wait_ge(eps_done, c + 1)
                nc.gpsimd.tensor_tensor(rstd[:, t], var_eps[:, t], keep["neg_half"][:, 0:SC], ALU.pow).then_inc(rstd_done, 1)

            def low_parts(c):
                b, s = divmod(c, 2)
                pool.wait_ge(stored[s], STORED * b + STORED)
                for full, high, low, h_done, l_done in ((qf, qh, ql, qh_done, ql_done), (kf, kh, kl, kh_done, kl_done)):
                    pool.wait_ge(h_done[s], b + 1)
                    nc.gpsimd.tensor_tensor(low[s][:], full[s][:], high[s][:].bitcast(F32), ALU.subtract).then_inc(l_done[s], 1)

            for s in range(2):
                pool.sem_inc(ql_done[s], 1)
                pool.sem_inc(kl_done[s], 1)
            for c in range(2 * B + 2):
                if c < 2 * B:
                    root(c)
                    fill(c)
                if c > 1:
                    low_parts(c - 2)

        @block.vector
        def _(dve):
            w_psum = ps[:, 7, :].rearrange("p (n d) -> p n d", n=4)
            def statistics(c):
                dve.wait_ge(x_in, 16 * (c // 2) + 16)
                for t in range(SC * c, SC * c + SC):
                    nc.vector.bn_stats(stats[:, t, :], x_all[:, t, :]).then_inc(stats_step, 1)
                dve.wait_ge(stats_step, SC * c + SC)
                for t in range(SC * c, SC * c + SC):
                    ins = nc.vector.bn_aggr(mean_var[:, t, :], stats[:, t, :])
                ins.then_inc(mv_done, 1)

            def normalise(c):
                b, s = divmod(c, 2)
                dve.wait_ge(rstd_done, c + 1)
                dve.wait_ge(xT_done[s], b + 1)
                for t in range(SC):
                    n = SC * c + t
                    ins = nc.vector.tensor_scalar(xn[s][:, t, :], x_all[:, n, :], mean_var[:, n, 0:1], rstd[:, n:n + 1], ALU.subtract, ALU.mult)
                ins.then_inc(xn_done[s], 1)

            def low_part(c):
                b, s = divmod(c, 2)
                dve.wait_ge(xh_done[s], b + 1)
                nc.vector.tensor_tensor(xl[s][:], ps[:, s, :], xh[s][:].bitcast(F32), ALU.subtract).then_inc(xl_done[s], 1)

            def keep_values(c):
                b, s = divmod(c, 2)
                dve.wait_ge(v_done[s], b + 2)
                src = ps[:, 6 + s, :].rearrange("p (j g c) -> p j g c", j=SC, g=GB)
                bias = keep["row_consts"][:, 0:1, :].rearrange("p a (g c) -> p a g c", g=GB).to_broadcast([P, SC, GB, GH * DH])
                dst = keep["v_all"][:, GB * b:GB * b + GB, SC * s:SC * s + SC, :].rearrange("p g j c -> p j g c")
                nc.vector.tensor_tensor(dst, src, bias, ALU.add).then_inc(v_out[s], 1)

            for s in range(2):
                dve.sem_inc(xl_done[s], 1)
                dve.sem_inc(v_out[s], 1)
            statistics(0)
            for c in range(2 * B + 2):
                if c < 2 * B:
                    normalise(c)
                if c == 0:
                    dve.wait_ge(w_hi_done, 2)
                    nc.vector.tensor_tensor(w_lo[:], w_psum[:, 0:3, :], w_hi[:].bitcast(F32), ALU.subtract).then_inc(w_ready, 1)
                if c == 2:
                    dve.wait_ge(b_in, 16 * 5)
                if c > 1:
                    keep_values(c - 2)
                if c + 1 < 2 * B:
                    statistics(c + 1)
                if c < 2 * B:
                    low_part(c)
                if c in (1, 2):
                    nc.vector.memset(keep["q_diag"][c - 1][:].bitcast(F32), 0.0).then_inc(fills, 1)

        @block.scalar
        def _(act):
            w_psum = ps[:, 7, :].rearrange("p (n d) -> p n d", n=4)
            act.wait_ge(wT_done, 1)
            nc.scalar.activation(w_hi[:], w_psum[:, 0:3, :], ACT.Copy).then_inc(w_hi_done, 1)
            nc.scalar.activation(keep["woT"][:], w_psum[:, 3, :], ACT.Copy).then_inc(w_hi_done, 1)
            act.wait_ge(b_in, 16 * 5)

            def high_part(b, s):
                act.wait_ge(xT_done[s], b + 2)
                act.wait_ge(v_done[s], b + 1)
                nc.scalar.activation(xh[s][:], ps[:, s, :], ACT.Copy).then_inc(xh_done[s], 1)

            def q_and_k(b, s):
                for full, high, f_done, h_done, mm_done, l_done, col in (
                        (qf, qh, qf_done, qh_done, q_done, ql_done, 0), (kf, kh, kf_done, kh_done, k_done, kl_done, 1)):
                    act.wait_ge(mm_done[s], b + 1)
                    act.wait_ge(l_done[s], b + 1)
                    nc.scalar.activation(full[s][:], ps[:, 2 + 2 * col + s, :], ACT.Identity,
                                         bias=bias_cols[:, col:col + 1]).then_inc(f_done[s], 1)
                    act.wait_ge(f_done[s], b + 2)
                    act.wait_ge(stored[s], STORED * b + STORED)
                    nc.scalar.activation(high[s][:], full[s][:], ACT.Copy).then_inc(h_done[s], 1)

            def batch(b, more):
                high_part(b, 1)
                q_and_k(b, 0)
                if more:
                    high_part(b + 1, 0)
                q_and_k(b, 1)

            for s in range(2):
                act.sem_inc(qf_done[s], 1)
                act.sem_inc(kf_done[s], 1)
            high_part(0, 0)
            with act.Fori(0, B - 1) as b:
                batch(b, True)
            batch(B - 1, False)
            act.wait_ge(pool_fills, FILLS)
            act.dma_start(q_parts.rearrange("b h r c -> (b h) r c")[:, 2 * DH:2 * DH + 2, :], zeros[:]).then_inc(rows_out, 16)
            act.wait_ge(rows_out, 16)

        @block.tensor
        def _(pe):
            pe.wait_ge(w_in, 64)
            pe.wait_ge(ident_ready, 1)
            for n in range(4):
                ins = nc.tensor.transpose(ps[:, 7, D * n:D * n + D], w_raw[:, n, :], ident[:])
            ins.then_inc(wT_done, 1)
            def transpose_rows(b, s):
                pe.wait_ge(xn_done[s], b + 1)
                pe.wait_ge(xl_done[s], b + 1)
                for t in range(SC):
                    ins = nc.tensor.transpose(ps[:, s, P * t:P * t + P], xn[s][:, t, :], ident[:])
                ins.then_inc(xT_done[s], 1)

            def project(b, s):
                pe.wait_ge(xl_done[s], b + 2)
                for col, mm_done, f_done in ((0, q_done, qf_done), (1, k_done, kf_done)):
                    pe.wait_ge(f_done[s], b + 1)
                    o = ps[:, 2 + 2 * col + s, :]
                    nc.tensor.matmul(o, w_hi[:, col, :], xh[s][:], start=True, stop=False)
                    nc.tensor.matmul(o, w_hi[:, col, :], xl[s][:], start=False, stop=False)
                    nc.tensor.matmul(o, w_lo[:, col, :], xh[s][:], start=False, stop=True).then_inc(mm_done[s], 1)
                pe.wait_ge(v_out[s], b + 1)
                for t in range(SC):
                    o, c = ps[:, 6 + s, P * t:P * t + P], slice(P * t, P * t + P)
                    nc.tensor.matmul(o, xh[s][:, c], w_hi[:, 2, :], start=True, stop=False)
                    nc.tensor.matmul(o, xl[s][:, c], w_hi[:, 2, :], start=False, stop=False)
                    ins = nc.tensor.matmul(o, xh[s][:, c], w_lo[:, 2, :], start=False, stop=True)
                ins.then_inc(v_done[s], 1)

            def batch(b, more):
                transpose_rows(b, 1)
                project(b, 0)
                if more:
                    transpose_rows(b + 1, 0)
                project(b, 1)

            for s in range(2):
                pe.sem_inc(xT_done[s], 1)
                pe.sem_inc(v_done[s], 1)
            transpose_rows(0, 0)
            pe.wait_ge(w_ready, 1)
            with pe.Fori(0, B - 1) as b:
                batch(b, True)
            batch(B - 1, False)
    nc.clear_and_free_semaphores(semaphores)
    nc.all_engine_barrier()


def attention(nc, keep, q_parts, k_parts, heads_out, inverse, Ws1, Ws3, Ws2, We1, We3, We2):
    q_diag, k_rows, v_one = keep["q_diag"], keep["k_rows"], keep["v_one"]
    q_flat = q_parts.rearrange("b h r c -> (b h) r c")
    k_flat = k_parts.rearrange("b h r c -> (b h) r c")
    with ExitStack() as ctx:
        def sb(name, shape, dt=F32):
            return ctx.enter_context(nc.sbuf_tensor(name, shape, dt))

        def sem(name):
            return ctx.enter_context(nc.semaphore(name))

        def sems(name):
            return [sem(f"{name}{s}") for s in range(3)]

        probs = [sb(f"probs{i}", [P, GH, S]) for i in range(3)]
        heads = sb("heads", [P, S])
        sums = sb("sums", [P, B - 1, P])
        partial = sb("partial", [P, 48])
        row_max = sb("row_max", [P, 32])
        neg_max = sb("neg_max", [32, 2, P], F32R)
        neg_full = sb("neg_full", [32, P])
        def raw_up(u):
            return probs[2][:, u // 2, HALF * (u % 2):HALF * (u % 2) + 2 * FF] if u < NE else probs[1][:, 0, 0:2 * FF]

        ps_scores = ctx.enter_context(nc.psum_tensor("ps_scores", [P, 3, 512], F32))
        ps_max = ctx.enter_context(nc.psum_tensor("ps_max", [P, 3, 512], F32))
        ps_out = ctx.enter_context(nc.psum_tensor("ps_out", [P, 2, 512], F32))

        qk_in, max_in, heads_free = sems("qk_in"), sems("max_in"), sem("heads_free")
        scores_done, exp_done, mask_done = sem("scores_done"), sem("exp_done"), sem("mask_done")
        seg_done, seg_read, max_done, maxT_done = sem("seg_done"), sem("seg_read"), sem("max_done"), sem("maxT_done")
        neg_step, neg_done, v_ready = sem("neg_step"), sem("neg_done"), sem("v_ready")
        lower_done = sem("lower_done")
        lower_free, upper_free = sem("lower_free"), sem("upper_free")
        probs_free = sems("probs_free")
        sums_in, sums_done = sem("sums_in"), sem("sums_done")
        w2_in = sem("w2_in")
        bias_added, passed_load = sem("bias_added"), sem("passed_load")
        passed, ffw_hi, ffw_lo, ffw_in = sem("passed1"), sem("ffw_hi"), sem("ffw_lo"), sem("ffw_in")
        block = ctx.enter_context(nc.Block())
        FIRST = 2 * LAG + AHEAD
        QK_IN, MAX_IN = 16 * 4 * GH, 16 * 2 * GH
        ITERS = (NG - 4) // 3
        PEELED = range(3 * ITERS, NG)


        def load_queries(eng, n, slot):
            for h in range(GH):
                r = ROWS * h
                rows = q_flat[bass.ds(n * GH + h, 1), :, :].rearrange("a r (i c) -> (a r) i c", c=ROWS)
                eng.dma_start(q_diag[slot][r + DH:r + PARTS + 2, :, h, :].bitcast(F32), rows).then_inc(qk_in[slot], 16)
                eng.dma_start(q_diag[slot][r:r + DH, :, h, :].bitcast(F32), rows[DH:2 * DH, :, :]).then_inc(qk_in[slot], 16)

        def load_keys(eng, n, slot):
            for h in range(GH):
                r = ROWS * h
                rows = k_flat[bass.ds(n * GH + h, 1), :, :].rearrange("a r c -> (a r) c")
                eng.dma_start(k_rows[slot][r + DH:r + PARTS, :].bitcast(F32), rows).then_inc(qk_in[slot], 16)
                eng.dma_start(k_rows[slot][r:r + DH, :].bitcast(F32), rows[0:DH, :]).then_inc(qk_in[slot], 16)

        @block.sync
        def _(sp):
            def load(n, slot):
                load_queries(sp, n, slot)
                load_keys(sp, n, slot)

            def put_max(m, slot):
                sp.wait_ge(neg_done, m + 1)
                for h in range(GH):
                    for part in range(2):
                        r = ROWS * h + PARTS + part
                        sp.dma_start(q_diag[slot][r:r + 1, :, h, :].bitcast(F32),
                                     neg_max[:, part, ROWS * h:ROWS * h + ROWS].bitcast(F32)).then_inc(max_in[slot], 16)

            def group(n, k, loads, following):
                if following:
                    put_max(n + 1, (k + 1) % 3)
                if loads:
                    sp.wait_ge(scores_done, HALVES * (n + 1) + 1)
                    sp.sem_inc(passed_load, 1)
                    load(n + 3, k)
                sp.wait_ge(lower_free, n + 2)
                sp.wait_ge(upper_free, n + 2)
                for h in range(GH):
                    sp.dma_start(heads_out[bass.ds(GH * n + h, 1), :, :].rearrange("a r c -> (a r) c"),
                                 heads[ROWS * h:ROWS * h + DH + 1, :]).then_inc(heads_free, 16)

            sp.sem_inc(heads_free, 16 * GH)
            load_queries(sp, 0, 0)
            load(1, 1)
            put_max(0, 0)
            load(2, 2)
            with sp.Fori(0, ITERS) as it:
                for k in range(3):
                    group(3 * it + k, k, True, True)
            for n in PEELED:
                if n == NG - 3:
                    sp.wait_ge(heads_free, 16 * GH * n)
                    for b in range(B - 1):
                        sp.dma_start(sums[:, b, :], sums_of(heads_out, b)).then_inc(sums_in, 16)
                if n == NG - 1:
                    sp.wait_ge(sums_done, 1)
                    for b in range(B - 1):
                        sp.dma_start(inverse_of(inverse, b), sums[:, b, :]).then_inc(sums_in, 16)
                group(n, n % 3, n + 3 < NG, n + 1 < NG)
            sp.wait_ge(heads_free, 16 * GH * (NG + 1))
            sp.wait_ge(sums_in, 16 * 2 * (B - 1))

        @block.gpsimd
        def _(pool):
            def group(n, k):
                for st in range(STEPS):
                    t = st // GH
                    buf = probs[(5 * k + t) % 3]
                    slot = st % GH if t < 4 else st - 16
                    pool.wait_ge(exp_done, HALVES * n + 2 * st + 2)
                    pool.sem_inc(passed, 1)
                    gap, count = max(DIAGONALS[t][-1], P), len(DIAGONALS[t])
                    view = buf[:, slot, 0:gap * count].rearrange("p (a c) -> p a c", a=count)[:, :, 0:P]
                    nc.gpsimd.affine_select(out=view, in_=view, compare_op=ALU.is_ge, fill=0.0, base=0,
                                            pattern=[[0, count], [1, P]], channel_multiplier=-1).then_inc(mask_done, 1)
                    if st == 1:
                        src = keep["v_all"][:, bass.ds(n, 1), :, :].rearrange("p a j (h d) -> p (a j) h d", h=GH)
                        nc.gpsimd.tensor_copy(v_one[k][:, :, :, 0:DH], src).then_inc(v_ready, 1)

            for b in range(B):
                rows = keep["x_all"][:, TB * b:TB * b + TB, :]
                nc.gpsimd.tensor_tensor(rows, rows, keep["row_consts"][:, 1:2, :].to_broadcast([P, TB, D]), ALU.add).then_inc(bias_added, 1)
            for u in range(UNITS):
                pool.wait_ge(ffw_hi, u + 1)
                nc.gpsimd.tensor_tensor(keep["w13_lo"][:, u, :], raw_up(u), keep["w13_hi"][:, u, :].bitcast(F32), ALU.subtract).then_inc(ffw_lo, 1)
            with pool.Fori(0, ITERS) as it:
                for k in range(3):
                    group(3 * it + k, k)
            for n in PEELED:
                group(n, n % 3)

        @block.scalar
        def _(act):
            def exp_half(n, it, k, hs):
                st, half = divmod(hs, 2)
                t = st // GH
                tau = 5 * k + t
                slot = st % GH if t < 4 else st - 16
                if hs % (2 * GH) == 0:
                    act.wait_ge(probs_free[tau % 3], 5 * it + tau // 3 + 1)
                act.wait_ge(scores_done, HALVES * n + hs + 1)
                nc.scalar.activation(probs[tau % 3][:, slot, HALF * half:HALF * half + HALF], ps_scores[:, hs % 3, :],
                                     ACT.Exp, scale=SCALE).then_inc(exp_done, 1)

            def copy_out(n, it, k, half, free):
                if half == 1:
                    tau = 5 * k + 4
                    act.wait_ge(probs_free[tau % 3], 5 * it + tau // 3 + 2)
                if half == 0:
                    act.wait_ge(lower_done, n + 1)
                    act.wait_ge(heads_free, 16 * GH * (n + 1))
                nc.scalar.activation(heads[:, HALF * half:HALF * half + HALF], ps_out[:, half, :], ACT.Copy).then_inc(free, 1)

            def group(n, it, k, following):
                for hs in range(FIRST, HALVES + FIRST):
                    if hs < HALVES:
                        exp_half(n, it, k, hs)
                    elif following:
                        exp_half(n + 1, it + (k == 2), (k + 1) % 3, hs - HALVES)
                    if hs == HALVES + 5:
                        copy_out(n, it, k, 0, lower_free)
                    if hs == HALVES + 2 * LAG + 1:
                        copy_out(n, it, k, 1, upper_free)

            act.sem_inc(lower_free, 1)
            act.sem_inc(upper_free, 1)

            load_keys(act, 0, 0)
            for u in range(UNITS):
                for n, w in enumerate((We1[u], We3[u]) if u < NE else (Ws1, Ws3)):
                    act.dma_start(raw_up(u)[:, FF * n:FF * n + FF], w).then_inc(ffw_in, 16)
            for u in range(UNITS):
                w2 = We2[u] if u < NE else Ws2
                act.dma_start(keep["w2"][:, u, :, :], w2.rearrange("(c p) d -> p c d", p=P)).then_inc(w2_in, 16)
            act.wait_ge(ffw_in, 32 * UNITS)
            for u in range(UNITS):
                nc.scalar.activation(keep["w13_hi"][:, u, :], raw_up(u), ACT.Copy).then_inc(ffw_hi, 1)
            act.wait_ge(ffw_lo, UNITS)
            for hs in range(FIRST):
                exp_half(0, 0, 0, hs)
            with act.Fori(0, ITERS) as it:
                for k in range(3):
                    group(3 * it + k, it, k, True)
            for n in PEELED:
                group(n, n // 3, n % 3, n + 1 < NG)
            act.wait_ge(w2_in, 16 * UNITS)

        @block.vector
        def _(dve):
            def reduce_segment(m, s):
                _, _, n, col, _ = SEGMENTS[s]
                dve.wait_ge(seg_done, NSEG * m + s + 1)
                dst = row_max[:, col:col + 1] if col < 16 else partial[:, col:col + 1]
                nc.vector.reduce_max(dst, ps_max[:, s % 3, 0:n], AX).then_inc(seg_read, 1)
                if s == NSEG - 1:
                    dve.wait_ge(seg_read, NSEG * m + NSEG)
                    nc.vector.tensor_tensor(row_max[:, 16:32], partial[:, 16:32], partial[:, 32:48], ALU.max).then_inc(max_done, 1)

            def negate(m, put_before):
                if put_before is not None:
                    dve.wait_ge(*put_before)
                dve.wait_ge(maxT_done, m + 1)
                nc.vector.tensor_scalar(neg_full[:], ps_max[0:32, 2, 0:P], -1.0, None, ALU.mult).then_inc(neg_step, 1)
                dve.wait_ge(neg_step, 2 * m + 1)
                nc.vector.tensor_copy(neg_max[:, 0, :], neg_full[:]).then_inc(neg_step, 1)
                dve.wait_ge(neg_step, 2 * m + 2)
                nc.vector.tensor_tensor(neg_max[:, 1, :], neg_full[:], neg_max[:, 0, :].bitcast(F32), ALU.subtract).then_inc(neg_done, 1)

            def group(n, it, k, last):
                for u in range(STEPS):
                    if u == MAX_AT:
                        negate(n + 1, (max_in[k], MAX_IN * (it + 1)))
                    for dm, s in SEGS_BY_CHUNK[u]:
                        if dm <= last:
                            reduce_segment(n + dm, s)

            for s in range(NSEG):
                reduce_segment(0, s)
            negate(0, None)
            for u in range(MAX_AT, STEPS):
                for _, s in SEGS_BY_CHUNK[u]:
                    reduce_segment(1, s)
            with dve.Fori(0, ITERS) as it:
                for k in range(3):
                    group(3 * it + k, it, k, 2)
            for n in PEELED:
                if n + 1 < NG:
                    group(n, n // 3, n % 3, NG - 1 - n)
            dve.wait_ge(sums_in, 16 * (B - 1))
            nc.vector.reciprocal(sums[:], sums[:]).then_inc(sums_done, 1)

        @block.tensor
        def _(pe):
            def scores(hs, slot):
                for h, j, c, w, q in half_pieces(hs):
                    ins = nc.tensor.matmul(ps_scores[:, hs % 3, c:c + w], k_rows[slot][:, P * j:P * j + P],
                                           q_diag[slot][:, q // ROWS:(q + w) // ROWS, h, :], start=True, stop=True)
                ins.then_inc(scores_done, 1)

            def segment(m, s, slot, first=False):
                i, k0, n, _, diagonal = SEGMENTS[s]
                if s == 2 and not first:
                    pe.wait_ge(neg_step, 2 * m - 1)
                if not (first and s < 3):
                    pe.wait_ge(seg_read, NSEG * m + s - 2)
                o = ps_max[:, s % 3, 0:n]
                ins = nc.tensor.matmul(o, q_diag[slot][:, i, :, :].rearrange("p h r -> p (h r)"), k_rows[slot][:, k0:k0 + n],
                                       start=True, stop=not diagonal)
                if diagonal:
                    ins = nc.tensor.matmul(ps_max[:, s % 3, n - ROWS:n], keep["ident_bf"][:], keep["mask_bf"][:],
                                           start=False, stop=True)
                ins.then_inc(seg_done, 1)

            def transpose_max(m):
                pe.wait_ge(max_done, m + 1)
                nc.tensor.transpose(ps_max[0:32, 2, 0:P], row_max[:], keep["ident"][:]).then_inc(maxT_done, 1)

            def values(n, k, u):
                t, j, c, w, q = CHUNKS[u]
                tau = 5 * k + t
                if u == 0:
                    pe.wait_ge(v_ready, n + 1)
                    pe.wait_ge(lower_free, n + 1)
                if u == 2:
                    pe.wait_ge(upper_free, n + 1)
                if u == 0 or CHUNKS[u - 1][0] != t:
                    pe.wait_ge(mask_done, STEPS * n + TYPE_END[t])
                for h in range(GH):
                    slot, c0 = (h, c) if t < 4 else (h // 2, c + HALF * (1 - h % 2))
                    ins = nc.tensor.matmul(ps_out[ROWS * h:ROWS * h + ROWS, q // HALF, q % HALF:q % HALF + w], v_one[k][:, j, h, :],
                                           probs[tau % 3][:, slot, c0:c0 + w], start=(u in (0, 2)), stop=(u in (LOWER_LAST, STEPS - 1)))
                if u == STEPS - 1 or CHUNKS[u + 1][0] != t:
                    ins.then_inc(probs_free[tau % 3], 1)
                elif u == LOWER_LAST:
                    ins.then_inc(lower_done, 1)

            def group(n, it, k, last):
                for u in range(STEPS):
                    st = u + LAG
                    segs = [(dm, s) for dm, s in SEGS_BY_CHUNK[u] if dm <= last]
                    if u == MAX_AT and last > 1:
                        pe.wait_ge(qk_in[(k + 2) % 3], QK_IN * (it + 1 + (k > 0)))
                    middle = max([0] + [i + 1 for i in range((len(segs) + 1) // 2) if i < len(segs) and SEGMENTS[segs[i][1]][4]])
                    cut = [0, middle // 2, middle, (middle + len(segs) + 1) // 2, len(segs)]
                    if u == MAX_AT and last > 0:
                        cut[1] = 0
                        transpose_max(n + 1)
                    for part in range(4):
                        for dm, s in segs[cut[part]:cut[part + 1]]:
                            segment(n + dm, s, (k + dm) % 3)
                        if part == 1:
                            values(n, k, u)
                        if part in (0, 2):
                            hs = 2 * st + part // 2
                            if hs + AHEAD < HALVES or last > 0:
                                pe.wait_ge(exp_done, HALVES * n + hs + 1)
                                if hs + AHEAD == HALVES:
                                    pe.wait_ge(max_in[(k + 1) % 3], MAX_IN * (it + 1 + (k == 2)))
                                scores((hs + AHEAD) % HALVES, (k + (hs + AHEAD >= HALVES)) % 3)

            for k in range(3):
                pe.sem_inc(probs_free[k], 1)
            pe.wait_ge(qk_in[0], QK_IN)
            for s in range(NSEG):
                segment(0, s, 0, True)
            transpose_max(0)
            pe.wait_ge(qk_in[1], QK_IN)
            early = [s for u in range(MAX_AT, STEPS) for _, s in SEGS_BY_CHUNK[u]]
            cut = len(early) // 2
            for s in early[:cut]:
                segment(1, s, 1)
            pe.wait_ge(max_in[0], MAX_IN)
            for hs in range(AHEAD):
                scores(hs, 0)
            for hs in range(2 * LAG):
                for s in early[cut + hs * (len(early) - cut) // (2 * LAG):cut + (hs + 1) * (len(early) - cut) // (2 * LAG)]:
                    segment(1, s, 1)
                pe.wait_ge(exp_done, hs + 1)
                scores(hs + AHEAD, 0)
            with pe.Fori(0, ITERS) as it:
                for k in range(3):
                    group(3 * it + k, it, k, 2)
            for n in PEELED:
                group(n, n // 3, n % 3, NG - 1 - n)


def feed_forward(nc, keep, heads_out, inverse, out_tiles):
    x_rows = nc.dram_tensor("x_rows", (B * S + 1, ROW), F32).ap()
    y_rows = nc.dram_tensor("y_rows", (SLOTS * P, D), F32).ap()
    with ExitStack() as ctx:
        def sb(name, shape, dt=F32):
            return ctx.enter_context(nc.sbuf_tensor(name, shape, dt))

        gathers = [ctx.enter_context(nc.semaphore(f"gathered{i}")) for i in range(4)]
        ff = dict(
            row_gathers=gathers[:2], output_gathers=gathers[2:],
            x_hi=sb("x_hi_all", [P, B, S], F32R),
            x_lo=sb("x_lo_all", [P, B, S], F32R),
            position=sb("position", [P, TOP, T], U32),
            place=sb("place", [P, NE, T]),
            chosen=[sb(f"chosen{k}", [P, T, NE]) for k in range(TOP)],
            slot_expert=sb("slot_expert", [P, SLOTS + BATCH], I32),
            slot_onehot=sb("slot_onehot", [P, SLOTS, NE]),
            slot_start=sb("slot_start", [P, 2, SLOTS + BATCH]),
            table=sb("table", [P, 2, P + 2], BF16),
            iota=sb("iota_tokens", [P, P], BF16),
            slot_index=sb("slot_index", [P, SLOTS + BATCH]),
        )
        route(nc, keep, ff, heads_out, inverse, x_rows)
        experts(nc, keep, ff, x_rows, y_rows)
        combine(nc, keep, ff, y_rows, out_tiles)


def sums_of(heads_out, b):
    return heads_out[H * b:H * b + H, DH:DH + 1, :].rearrange("h a (q c) -> h (a q) c", c=P)


def inverse_of(inverse, b):
    return inverse[H * b:H * b + H, :].rearrange("h (q c) -> (h q) c", c=P)


def route(nc, keep, ff, heads_out, inverse, x_rows):
    ident, x_all = keep["ident"], keep["x_all"]
    with ExitStack() as ctx:
        def sb(name, shape, dt=F32):
            return ctx.enter_context(nc.sbuf_tensor(name, shape, dt))

        def pair(name, shape, dt=F32):
            return [sb(f"{name}{s}", shape, dt) for s in range(2)]

        def sem(name):
            return ctx.enter_context(nc.semaphore(name))

        def sems(name):
            return [sem(f"{name}{s}") for s in range(2)]

        o_raw = pair("o_raw", [P, HALF])
        over_sums = pair("over_sums", [P, HALF])
        last_sums = sb("last_sums", [P, P])
        oT = pair("oT", [P, HALF])
        stats = sb("stats2", [P, T, 6])
        mean_var = sb("mean_var2", [P, T, 2])
        var_eps = sb("var_eps2", [P, T])
        rstd = sb("rstd2", [P, T])
        xn = pair("xn2", [P, SC, D])
        xT = pair("xT2", [P, HALF])
        gates = sb("gates", [P, T, NE])
        zero_row = sb("zero_row", [1, ROW])
        upper = sb("upper", [P, P], BF16)
        ones = sb("ones_bf", [P, P], BF16)
        same_expert = sb("same_expert", [P, P], BF16)
        descending = sb("descending", [P, NE])
        numbers = sb("numbers", [P, NE])
        earlier = sb("earlier", [P, NE, NE])
        tile_counts = sb("tile_counts", [P, T])
        run_tokens = sb("run_tokens", [P, NE, T])
        slot_numbers = sb("slot_numbers", [P, SLOTS + BATCH])
        best, second, total = sb("best", [P, T]), sb("second", [P, T]), sb("total", [P, T])
        pick = sb("pick", [P, T])
        equal = sb("equal", [P, T, NE])
        chosen = ff["chosen"]
        rest = sb("rest", [P, T, NE])
        both = sb("both", [P, T, NE])
        weights = sb("weights", [P, T, NE])
        member = sb("member", [P, NE, T], BF16)
        member_step = sb("member_step", [P, NE * T], BF16)
        counts = sb("counts", [P, 2, P], BF16)
        n_expert = sb("n_expert", [P, NE])
        over = sb("over", [P, NE, T])
        n_tiles = sb("n_tiles", [P, NE])
        before = sb("before", [P, NE, NE])
        base, end = sb("base", [P, NE]), sb("end", [P, NE])
        starts = sb("starts", [P, 2, NE * T])
        starts_step = sb("starts_step", [P, 2, NE * T])
        diagonal = sb("diagonal", [P, 2, P])
        steps_diagonal = sb("steps_diagonal", [P, 2, 2, P])
        start_column = sb("start_column", [P, 2])
        step_columns = sb("step_columns", [P, 2, 2])
        past = sb("past", [P, SLOTS + BATCH, NE - 1])
        expert_f = sb("expert_f", [P, SLOTS + BATCH])
        ps = ctx.enter_context(nc.psum_tensor("ps_route", [P, 8, 512], F32))

        o_in, o_done, y_done, x1_done = sems("o_in"), sems("o_done"), sems("y_done"), sems("x1_done")
        stats_step, mv_done, eps_done, rstd_done = sem("stats_step2"), sem("mv_done2"), sem("eps_done2"), sem("rstd_done2")
        xn_done, xT_done, xT_out, logit_done, gate_exp = sems("xn_done2"), sems("xT_done2"), sems("xT_out2"), sems("logit_done"), sems("gate_exp")
        sums_in, sums_done = sem("sums_in"), sem("sums_done")
        xh_done, xl_done, xn_free = sems("xh_done2"), sems("xl_done2"), sems("xn_free2")
        const_step, chain, row_zero, rows_out, weights_done = sem("const_step"), sem("chain"), sem("row_zero"), sem("rows_out2"), sem("weights_done")
        member_done, counted, counts_out, scanned = sem("member_done"), sem("counted"), sem("counts_out"), sem("scanned")
        block = ctx.enter_context(nc.Block())
        CONSTS = 16

        @block.sync
        def _(sp):
            def load_heads(c):
                b, s = divmod(c, 2)
                rows, cols = slice(H * b, H * b + H), slice(HALF * s, HALF * s + HALF)
                sp.wait_ge(o_done[s], b + 1)
                sp.dma_start(o_raw[s][:], heads_out[rows, 0:DH, cols]).then_inc(o_in[s], 16)
                sp.dma_start(over_sums[s][:], inverse[rows, cols].rearrange("h (a c) -> h a c", a=1).to_broadcast([H, DH, HALF])).then_inc(o_in[s], 16)

            def store_rows(c):
                b, s = divmod(c, 2)
                sp.wait_ge(xn_done[s], b + 1)
                sp.dma_start(x_rows[S * b + HALF * s:S * b + HALF * s + HALF, 0:D].rearrange("(t p) d -> p t d", p=P), xn[s][:]).then_inc(xn_free[s], 16)

            for s in range(2):
                sp.sem_inc(xn_free[s], 16)
            sp.dma_start(last_sums[:], sums_of(heads_out, B - 1)).then_inc(sums_in, 16)
            for c in range(2):
                load_heads(c)
            sp.wait_ge(sums_done, 1)
            sp.dma_start(inverse_of(inverse, B - 1), last_sums[:]).then_inc(sums_in, 16)
            sp.wait_ge(row_zero, 1)
            sp.dma_start(x_rows[B * S:B * S + 1, :], zero_row[:]).then_inc(rows_out, 16)
            load_heads(2)
            sp.wait_ge(sums_in, 32)
            for c in range(2 * B):
                if c + 3 < 2 * B:
                    load_heads(c + 3)
                store_rows(c)
            sp.wait_ge(weights_done, 1)
            sp.dma_start(x_rows[0:B * S, D:ROW].rearrange("(t p) e -> p t e", p=P), weights[:]).then_inc(rows_out, 16)
            sp.wait_ge(rows_out, 32)
            for s in range(2):
                sp.wait_ge(xn_free[s], 16 * (B + 1))

        @block.gpsimd
        def _(pool):
            nc.gpsimd.memset(zero_row[:], 0.0).then_inc(row_zero, 1)
            for m in (upper, ones, same_expert, earlier):
                nc.gpsimd.memset(m[:], 1.0).then_inc(const_step, 1)
            for m, pattern, p_step in ((descending, [[-1, NE]], 0), (numbers, [[1, NE]], 0), (tile_counts, [[P, T]], 0),
                                       (run_tokens, [[0, NE], [P, T]], 0), (slot_numbers, [[1, SLOTS + BATCH]], 0),
                                       (ff["iota"], [[1, P]], 0), (ff["slot_index"], [[P, SLOTS + BATCH]], 1)):
                nc.gpsimd.iota(m[:], pattern=pattern, base=NE if m is descending else 0, channel_multiplier=p_step,
                               allow_small_or_imprecise_dtypes=True).then_inc(const_step, 1)
            pool.wait_ge(const_step, 11)
            nc.gpsimd.affine_select(out=upper[:], in_=upper[:], compare_op=ALU.is_ge, fill=0.0, base=0,
                                    pattern=[[1, P]], channel_multiplier=-1).then_inc(const_step, 1)
            nc.gpsimd.affine_select(out=earlier[:], in_=earlier[:], compare_op=ALU.is_gt, fill=0.0, base=0,
                                    pattern=[[1, NE], [-1, NE]], channel_multiplier=0).then_inc(const_step, 1)
            nc.gpsimd.affine_select(out=same_expert[:], in_=same_expert[:], compare_op=ALU.is_gt, fill=0.0, base=0,
                                    pattern=[[1, P]], channel_multiplier=-1).then_inc(const_step, 1)
            pool.wait_ge(const_step, 14)
            nc.gpsimd.affine_select(out=same_expert[:], in_=same_expert[:], compare_op=ALU.is_ge, fill=0.0, base=0,
                                    pattern=[[-T, P // T], [0, T]], channel_multiplier=1).then_inc(const_step, 1)
            nc.gpsimd.tensor_copy(starts[:, 1, :], run_tokens[:].rearrange("p e t -> p (e t)")).then_inc(const_step, 1)
            for c in range(2 * B):
                pool.wait_ge(mv_done, c + 1)
                nc.gpsimd.tensor_scalar(var_eps[:, SC * c:SC * c + SC], mean_var[:, SC * c:SC * c + SC, 1], EPS, 0.0, ALU.add, ALU.add).then_inc(eps_done, 1)
                pool.wait_ge(eps_done, c + 1)
                nc.gpsimd.tensor_tensor(rstd[:, SC * c:SC * c + SC], var_eps[:, SC * c:SC * c + SC], keep["neg_half"][:, 0:SC], ALU.pow).then_inc(rstd_done, 1)

        @block.vector
        def _(dve):
            def tokens_of(c):
                return x_all[:, SC * c:SC * c + SC, :]

            def divide(c):
                b, s = divmod(c, 2)
                dve.wait_ge(o_in[s], 32 * b + 32)
                dve.wait_ge(y_done[s], b + 1)
                nc.vector.tensor_tensor(oT[s][:], o_raw[s][:], over_sums[s][:], ALU.mult).then_inc(o_done[s], 1)

            def statistics(c):
                b, s = divmod(c, 2)
                dve.wait_ge(y_done[s], b + 2)
                nc.vector.tensor_tensor(tokens_of(c), ps[:, s, :].rearrange("p (t d) -> p t d", t=SC), tokens_of(c), ALU.add).then_inc(x1_done[s], 1)
                dve.wait_ge(x1_done[s], b + 2)
                for t in range(SC):
                    nc.vector.bn_stats(stats[:, SC * c + t, :], x_all[:, SC * c + t, :]).then_inc(stats_step, 1)
                dve.wait_ge(stats_step, SC * c + SC)
                for t in range(SC):
                    ins = nc.vector.bn_aggr(mean_var[:, SC * c + t, :], stats[:, SC * c + t, :])
                ins.then_inc(mv_done, 1)

            def normalise(c):
                b, s = divmod(c, 2)
                dve.wait_ge(rstd_done, c + 1)
                dve.wait_ge(xn_free[s], 16 * b + 16)
                dve.wait_ge(xT_done[s], b + 1)
                for t in range(SC):
                    n = SC * c + t
                    ins = nc.vector.tensor_scalar(xn[s][:, t, :], x_all[:, n, :], mean_var[:, n, 0:1], rstd[:, n:n + 1], ALU.subtract, ALU.mult)
                ins.then_inc(xn_done[s], 1)

            def low_part(c):
                b, s = divmod(c, 2)
                dve.wait_ge(xT_out[s], b + 1)
                nc.vector.tensor_tensor(ff["x_lo"][:, b, HALF * s:HALF * s + HALF], ps[:, 2 + s, :],
                                        ff["x_hi"][:, b, HALF * s:HALF * s + HALF].bitcast(F32), ALU.subtract).then_inc(xl_done[s], 1)

            for s in range(2):
                dve.sem_inc(o_done[s], 1)
            dve.wait_ge(sums_in, 16)
            nc.vector.reciprocal(last_sums[:], last_sums[:]).then_inc(sums_done, 1)
            divide(0)
            for c in range(2 * B + 2):
                if c + 1 < 2 * B:
                    divide(c + 1)
                if c < 2 * B:
                    statistics(c)
                if 0 < c <= 2 * B:
                    normalise(c - 1)
                if c > 1:
                    low_part(c - 2)

            done = [0]

            def then(ins):
                ins.then_inc(chain, 1)
                done[0] += 1
                dve.wait_ge(chain, done[0])

            def over_experts(ap):
                return ap.rearrange("p (t a) -> p t a", a=1).to_broadcast([P, T, NE])

            def over_tiles(ap):
                return ap.rearrange("p (a e) -> p a e", a=1).to_broadcast([P, T, NE])

            for s in range(2):
                dve.wait_ge(gate_exp[s], B + 1)
            dve.wait_ge(const_step, CONSTS)
            then(nc.vector.tensor_scalar(gates[:], gates[:], 1.0, None, ALU.add))
            then(nc.vector.reciprocal(gates[:], gates[:]))
            for k, (source, greatest) in enumerate(((gates, best), (rest, second))):
                then(nc.vector.reduce_max(greatest[:], source[:], AX))
                then(nc.vector.tensor_tensor(equal[:], source[:], over_experts(greatest[:]), ALU.is_equal))
                then(nc.vector.tensor_tensor(equal[:], equal[:], over_tiles(descending[:]), ALU.mult))
                then(nc.vector.reduce_max(pick[:], equal[:], AX))
                then(nc.vector.tensor_tensor(chosen[k][:], over_tiles(descending[:]), over_experts(pick[:]), ALU.is_equal))
                if k == 0:
                    then(nc.vector.scalar_tensor_tensor(out=rest[:], in0=chosen[0][:], scalar=-4.0, in1=gates[:], op0=ALU.mult, op1=ALU.add))
            then(nc.vector.tensor_tensor(both[:], chosen[0][:], chosen[1][:], ALU.add))
            then(nc.vector.tensor_copy(member[:], both[:].rearrange("p t e -> p e t")))
            flat = member[:].rearrange("p e t -> p (e t)")
            nc.vector.tensor_copy(member_step[:, 0:1], flat[:, 0:1])
            then(nc.vector.tensor_tensor(member_step[:, 1:NE * T], flat[:, 1:NE * T], flat[:, 0:NE * T - 1], ALU.subtract))
            nc.vector.sem_inc(member_done, 1)
            then(nc.vector.tensor_tensor(total[:], best[:], second[:], ALU.add))
            then(nc.vector.tensor_scalar(total[:], total[:], float(1 + TOP), None, ALU.mult))
            then(nc.vector.reciprocal(total[:], total[:]))
            then(nc.vector.tensor_tensor(weights[:], gates[:], both[:], ALU.mult))
            then(nc.vector.tensor_tensor(weights[:], weights[:], over_experts(total[:]), ALU.mult))
            nc.vector.sem_inc(weights_done, 1)
            inclusive = ps[:, 4, 0:NE * T]
            run_counts = ps[:, 4, NE * T:2 * NE * T].rearrange("p (e t) -> p e t", e=NE)
            dve.wait_ge(counted, 1)
            then(nc.vector.tensor_copy(counts[:], ps[:, 5, 0:2 * P].rearrange("p (h r) -> p h r", h=2)))
            nc.vector.sem_inc(counts_out, 1)
            then(nc.vector.tensor_copy(ff["table"][:, :, 0:P], ps[:, 6, 0:2 * P].rearrange("p (h r) -> p h r", h=2)))
            then(nc.vector.reduce_sum(n_expert[:], run_counts, AX))
            then(nc.vector.tensor_tensor(over[:], n_expert[:].rearrange("p (e a) -> p e a", a=1).to_broadcast([P, NE, T]),
                                         tile_counts[:].rearrange("p (a t) -> p a t", a=1).to_broadcast([P, NE, T]), ALU.is_gt))
            then(nc.vector.reduce_sum(n_tiles[:], over[:], AX))
            then(nc.vector.tensor_tensor(before[:], earlier[:], n_tiles[:].rearrange("p (a e) -> p a e", a=1).to_broadcast([P, NE, NE]), ALU.mult))
            then(nc.vector.reduce_sum(base[:], before[:], AX))
            then(nc.vector.tensor_tensor(end[:], base[:], n_tiles[:], ALU.add))
            dve.wait_ge(scanned, 1)
            then(nc.vector.scalar_tensor_tensor(out=starts[:, 0, :].rearrange("p (e t) -> p e t", e=NE),
                                                in0=base[:].rearrange("p (e a) -> p e a", a=1).to_broadcast([P, NE, T]), scalar=float(P),
                                                in1=ps[:, 7, 0:NE * T].rearrange("p (e t) -> p e t", e=NE), op0=ALU.mult, op1=ALU.add))
            eye2 = ident[:].rearrange("p (a c) -> p a c", a=1).to_broadcast([P, 2, P])
            eye4 = ident[:].rearrange("p (a b c) -> p a b c", a=1, b=1).to_broadcast([P, 2, 2, P])
            then(nc.vector.tensor_tensor(diagonal[:], starts[:, 0, :].rearrange("p (h r) -> p h r", h=2), eye2, ALU.mult))
            then(nc.vector.reduce_sum(start_column[:], diagonal[:], AX))
            nc.vector.tensor_copy(starts_step[:, :, 0:1], starts[:, :, 0:1])
            then(nc.vector.tensor_tensor(starts_step[:, :, 1:NE * T], starts[:, :, 1:NE * T], starts[:, :, 0:NE * T - 1], ALU.subtract))
            then(nc.vector.tensor_tensor(steps_diagonal[:], starts_step[:].rearrange("p k (h r) -> p k h r", h=2), eye4, ALU.mult))
            then(nc.vector.reduce_sum(step_columns[:], steps_diagonal[:], AX))
            then(nc.vector.tensor_copy(ff["table"][:, :, P:P + 2], step_columns[:].rearrange("p k h -> p h k")))
            then(nc.vector.tensor_tensor(ff["place"][:].rearrange("p e t -> p (e t)"), inclusive, starts[:, 0, :], ALU.add))
            then(nc.vector.scalar_tensor_tensor(out=ff["slot_start"][:],
                                                in0=slot_numbers[:].rearrange("p (a j) -> p a j", a=1).to_broadcast([P, 2, SLOTS + BATCH]), scalar=-float(P),
                                                in1=start_column[:].rearrange("p (h a) -> p h a", a=1).to_broadcast([P, 2, SLOTS + BATCH]),
                                                op0=ALU.mult, op1=ALU.add))
            then(nc.vector.tensor_tensor(past[:], end[:, 0:NE - 1].rearrange("p (a e) -> p a e", a=1).to_broadcast([P, SLOTS + BATCH, NE - 1]),
                                         slot_numbers[:].rearrange("p (j a) -> p j a", a=1).to_broadcast([P, SLOTS + BATCH, NE - 1]), ALU.is_le))
            then(nc.vector.reduce_sum(expert_f[:], past[:], AX))
            then(nc.vector.tensor_copy(ff["slot_expert"][:], expert_f[:]))
            then(nc.vector.tensor_tensor(ff["slot_onehot"][:], expert_f[:, 0:SLOTS].rearrange("p (j a) -> p j a", a=1).to_broadcast([P, SLOTS, NE]),
                                         numbers[:].rearrange("p (a e) -> p a e", a=1).to_broadcast([P, SLOTS, NE]), ALU.is_equal))

        @block.scalar
        def _(act):
            for s in range(2):
                act.sem_inc(gate_exp[s], 1)

            def copy_rows(c):
                b, s = divmod(c, 2)
                act.wait_ge(xT_done[s], b + 2)
                act.wait_ge(logit_done[s], b + 1)
                nc.scalar.activation(ff["x_hi"][:, b, HALF * s:HALF * s + HALF], ps[:, 2 + s, :], ACT.Copy).then_inc(xh_done[s], 1)
                nc.scalar.activation(xT[s][:], ps[:, 2 + s, :], ACT.Copy).then_inc(xT_out[s], 1)

            def gate(c):
                b, s = divmod(c, 2)
                act.wait_ge(logit_done[s], b + 2)
                nc.scalar.activation(gates[:, SC * c:SC * c + SC, :], ps[:, 4 + s, 0:SC * NE].rearrange("p (t e) -> p t e", t=SC),
                                     ACT.Exp, scale=-1.0).then_inc(gate_exp[s], 1)

            for c in range(2 * B + 1):
                if c < 2 * B:
                    copy_rows(c)
                if c > 0:
                    gate(c - 1)

        @block.tensor
        def _(pe):
            for s in range(2):
                for free in (y_done, x1_done, xT_done, xl_done, logit_done):
                    pe.sem_inc(free[s], 1)

            def project(c):
                b, s = divmod(c, 2)
                pe.wait_ge(o_done[s], b + 2)
                pe.wait_ge(x1_done[s], b + 1)
                for t in range(SC):
                    ins = nc.tensor.matmul(ps[:, s, P * t:P * t + P], oT[s][:, P * t:P * t + P], keep["woT"][:], start=True, stop=True)
                ins.then_inc(y_done[s], 1)

            def transpose_rows(c):
                b, s = divmod(c, 2)
                pe.wait_ge(xn_done[s], b + 1)
                pe.wait_ge(xl_done[s], b + 1)
                for t in range(SC):
                    ins = nc.tensor.transpose(ps[:, 2 + s, P * t:P * t + P], xn[s][:, t, :], ident[:])
                ins.then_inc(xT_done[s], 1)

            def logits(c):
                b, s = divmod(c, 2)
                pe.wait_ge(xT_out[s], b + 1)
                pe.wait_ge(gate_exp[s], b + 1)
                for t in range(SC):
                    ins = nc.tensor.matmul(ps[:, 4 + s, NE * t:NE * t + NE], xT[s][:, P * t:P * t + P], keep["wg"][:], start=True, stop=True)
                ins.then_inc(logit_done[s], 1)

            for c in range(2 * B + 3):
                if c < 2 * B:
                    project(c)
                if 1 < c < 2 * B + 2:
                    transpose_rows(c - 2)
                if c > 2:
                    logits(c - 3)
            pe.wait_ge(member_done, 1)
            flat = member[:].rearrange("p e t -> p (e t)")
            nc.tensor.matmul(ps[:, 4, 0:NE * T], upper[:], flat, start=True, stop=True)
            nc.tensor.matmul(ps[:, 4, NE * T:2 * NE * T], ones[:], flat, start=True, stop=True)
            for h in range(2):
                nc.tensor.matmul(ps[:, 5, P * h:P * h + P], flat[:, P * h:P * h + P], ones[:], start=True, stop=True)
            for h in range(2):
                ins = nc.tensor.matmul(ps[:, 6, P * h:P * h + P], member_step[:, P * h:P * h + P], upper[:], start=True, stop=True)
            ins.then_inc(counted, 1)
            pe.wait_ge(counts_out, 1)
            for h in range(2):
                ins = nc.tensor.matmul(ps[:, 7, P * h:P * h + P], counts[:, h, :], same_expert[:], start=True, stop=True)
            ins.then_inc(scanned, 1)


def experts(nc, keep, ff, x_rows, y_rows):
    ident = keep["ident"]
    with ExitStack() as ctx:
        def sb(name, shape, dt=F32):
            return ctx.enter_context(nc.sbuf_tensor(name, shape, dt))

        def sem(name):
            return ctx.enter_context(nc.semaphore(name))

        def sems(name, n=2):
            return [sem(f"{name}{s}") for s in range(n)]

        RING = 2 * BATCH
        ITERS = SLOTS // RING
        run_reached = [sb(f"run_reached{i}", [P, 2, P], BF16) for i in range(BATCH)]
        placed, place_sum = sb("placed", [P, T, NE]), sb("place_sum", [P, T])
        within = sb("within", [P, BATCH])
        passed_by = sb("passed_by", [P, BATCH, P])
        n_passed = sb("n_passed", [P, BATCH])
        tokens = [[sb(f"tokens{g}_{i}", [P, 1], U32) for i in range(BATCH)] for g in range(2)]
        rows = sb("rows", [P, RING, ROW])
        row_weights = sb("row_weights", [P, BATCH, NE])
        wt = sb("wt", [P, 2, BATCH])
        xh = [sb(f"rows_hi{i}", [P, P], F32R) for i in range(2)]
        xl = [sb(f"rows_lo{i}", [P, P], F32R) for i in range(2)]
        act_out = [sb(f"act_out{i}", [P, FF]) for i in range(2)]
        hid = [sb(f"hid{i}", [P, FF]) for i in range(2)]
        hidT = [sb(f"hidT{i}", [P, FF]) for i in range(2)]
        y = [sb(f"y{g}", [P, BATCH, D]) for g in range(2)]
        ps_up = ctx.enter_context(nc.psum_tensor("ps_up", [P, 2, 512], F32))
        ps_hT = ctx.enter_context(nc.psum_tensor("ps_hT", [P, 2, 512], F32))
        ps_y = ctx.enter_context(nc.psum_tensor("ps_y", [P, 2, 512], F32))
        ps_xT = ctx.enter_context(nc.psum_tensor("ps_xT", [P, 512], F32))
        ps_run = ctx.enter_context(nc.psum_tensor("ps_run", [P, BATCH, P + 2], F32))

        reached, looked_up, ids_step, ids_done = sem("reached"), sem("looked_up"), sem("ids_step"), sem("ids_done")
        gathered, wt_step, wt_done = ff["row_gathers"], sem("wt_step"), sem("wt_done")
        xT_done, xh_done, xl_done = sem("xT_done3"), sem("xh_done3"), sem("xl_done3")
        up_done, act_done, hid_done = sem("up_done"), sem("act_done"), sem("hid_done")
        hT_done, hT_out, down_done, y_out = sem("hT_done"), sem("hT_out"), sem("down_done"), sem("y_out")
        y_free = sems("y_free")
        place_step = sem("place_step")
        passed = sem("passed3")
        block = ctx.enter_context(nc.Block())


        def steps(eng, body):
            for v in range(BATCH, RING):
                body(v - RING, -1, v)
            with eng.Fori(0, ITERS - 1) as it:
                for v in range(RING):
                    body(RING * it + v, it, v)
            for v in range(RING):
                body(RING * (ITERS - 1) + v, ITERS - 1, v)

        def there(t):
            return not isinstance(t, int) or 0 <= t < SLOTS

        def wait_free(eng, semaphore, count):
            if not isinstance(count, int) or count > 0:
                eng.wait_ge(semaphore, count)

        @block.sync
        def _(sp):
            for g in range(2):
                sp.sem_inc(y_free[g], 16)
            with sp.Fori(0, ITERS) as it:
                for g in range(2):
                    sp.wait_ge(y_out, RING * it + BATCH * g + BATCH)
                    sp.dma_start(y_rows[bass.ds((RING * it + BATCH * g) * P, BATCH * P), :].rearrange("(i p) d -> p i d", p=P), y[g][:]).then_inc(y_free[g], 16)
            for g in range(2):
                sp.wait_ge(y_free[g], 16 * (ITERS + 1))

        @block.gpsimd
        def _(pool):
            with pool.Fori(0, ITERS) as it:
                for g in range(2):
                    pool.wait_ge(ids_done, 2 * it + g + 1)
                    pool.wait_ge(xT_done, RING * it + BATCH * g + BATCH)
                    pool.wait_ge(wt_done, 2 * it + g + 1)
                    pool.sem_inc(passed, 1)
                    for i in range(BATCH):
                        nc.gpsimd.indirect_dma_start(rows[:, BATCH * g + i, :], None, x_rows,
                                                     bass.IndirectOffsetOnAxis(ap=tokens[g][i][:, 0:1], axis=0)).then_inc(gathered[g], 16)

        @block.vector
        def _(dve):
            def reach(q):
                for i in range(BATCH):
                    for h in range(2):
                        ins = nc.vector.tensor_scalar(run_reached[i][:, h, :], ff["iota"][:], ff["slot_start"][:, h, bass.ds(BATCH * q + i, 1)], None, ALU.is_ge)
                ins.then_inc(reached, 1)

            def find_tokens(q, g):
                dve.wait_ge(looked_up, q + 1)
                nc.vector.tensor_tensor(within[:], ff["slot_index"][:, bass.ds(BATCH * q, BATCH)], ps_run[:, :, P], ALU.subtract).then_inc(ids_step, 1)
                dve.wait_ge(ids_step, 3 * q + 1)
                nc.vector.tensor_tensor(passed_by[:], ps_run[:, :, 0:P],
                                        within[:].rearrange("p (j a) -> p j a", a=1).to_broadcast([P, BATCH, P]), ALU.is_le).then_inc(ids_step, 1)
                dve.wait_ge(ids_step, 3 * q + 2)
                nc.vector.reduce_sum(n_passed[:], passed_by[:], AX).then_inc(ids_step, 1)
                dve.wait_ge(ids_step, 3 * q + 3)
                for i in range(BATCH):
                    ins = nc.vector.tensor_tensor(tokens[g][i][:], n_passed[:, i:i + 1], ps_run[:, i, P + 1:P + 2], ALU.add)
                ins.then_inc(ids_done, 1)

            def take_weights(q, it, g):
                dve.wait_ge(gathered[g], 16 * BATCH * it + 16 * BATCH)
                nc.vector.tensor_tensor(row_weights[:], rows[:, BATCH * g:BATCH * g + BATCH, D:ROW],
                                        ff["slot_onehot"][:, bass.ds(BATCH * q, BATCH), :], ALU.mult).then_inc(wt_step, 1)
                dve.wait_ge(wt_step, q + 1)
                nc.vector.reduce_sum(wt[:, g, :], row_weights[:], AX).then_inc(wt_done, 1)
                dve.wait_ge(wt_done, q + 3)

            def body(j, it, v):
                batch = j // BATCH if isinstance(j, int) else 2 * it + v // BATCH
                g_next, q_next = (v // BATCH + 1) % 2, batch + 1
                if v % BATCH == 0 and there(j + 3):
                    take_weights(q_next, it + (v + BATCH) // RING, g_next)
                if there(j + 3):
                    dve.wait_ge(xh_done, j + 4)
                    nc.vector.tensor_tensor(xl[(v + 3) % 2][:], ps_xT[:, 0:P], xh[(v + 3) % 2][:].bitcast(F32), ALU.subtract).then_inc(xl_done, 1)
                if there(j + 2):
                    w = (v + 2) % RING
                    dve.wait_ge(act_done, j + 3)
                    nc.vector.scalar_tensor_tensor(out=hid[w % 2][:], in0=ps_up[:, w % 2, FF:2 * FF], scalar=wt[:, w // BATCH, w % BATCH:w % BATCH + 1],
                                                   in1=act_out[w % 2][:], op0=ALU.mult, op1=ALU.mult).then_inc(hid_done, 1)
                if there(j + 9):
                    if v % BATCH == 0:
                        reach(batch + 3)
                    if v % BATCH == 1:
                        find_tokens(batch + 3, g_next)

            dve.sem_inc(wt_done, 2)
            for q in range(2):
                reach(q)
                find_tokens(q, q)
            for k in range(TOP):
                nc.vector.tensor_tensor(placed[:], ff["place"][:].rearrange("p e t -> p t e"), ff["chosen"][k][:], ALU.mult).then_inc(place_step, 1)
                dve.wait_ge(place_step, 3 * k + 1)
                nc.vector.reduce_sum(place_sum[:], placed[:], AX).then_inc(place_step, 1)
                dve.wait_ge(place_step, 3 * k + 2)
                nc.vector.tensor_scalar(ff["position"][:, k, :], place_sum[:], -1.0, None, ALU.add).then_inc(place_step, 1)
                dve.wait_ge(place_step, 3 * k + 3)
            steps(dve, body)

        @block.scalar
        def _(act):
            def body(j, it, v):
                if there(j + 3):
                    act.wait_ge(xT_done, RING + j + 4)
                    nc.scalar.activation(xh[(v + 3) % 2][:], ps_xT[:, 0:P], ACT.Copy).then_inc(xh_done, 1)
                if there(j + 2):
                    a = (v + 2) % 2
                    act.wait_ge(up_done, j + 3)
                    nc.scalar.activation(act_out[a][:], ps_up[:, a, 0:FF], ACT.Silu).then_inc(act_done, 1)
                if there(j + 1):
                    a = (v + 1) % 2
                    act.wait_ge(hT_done, j + 2)
                    nc.scalar.activation(hidT[a][:], ps_hT[:, a, 0:FF], ACT.Copy).then_inc(hT_out, 1)
                if there(j):
                    act.wait_ge(down_done, j + 1)
                    if v % BATCH == 0:
                        act.wait_ge(y_free[v // BATCH], 16 * it + 16)
                    nc.scalar.activation(y[v // BATCH][:, v % BATCH, :], ps_y[:, v % 2, 0:D], ACT.Copy).then_inc(y_out, 1)

            steps(act, body)

        @block.tensor
        def _(pe):
            def look_up(q):
                pe.wait_ge(reached, q + 1)
                wait_free(pe, ids_done, q)
                for i in range(BATCH):
                    for h in range(2):
                        ins = nc.tensor.matmul(ps_run[:, i, :], run_reached[i][:, h, :], ff["table"][:, h, :], start=(h == 0), stop=(h == 1))
                ins.then_inc(looked_up, 1)

            here = {}

            def load_experts(j):
                values = nc.values_load_multi_w_load_instructions(
                    ff["slot_expert"][0:1, bass.ds(j, RING + 2)], engines=(mybir.EngineType.PE,), min_val=0, max_val=NE - 1,
                    skip_runtime_bounds_check_because="each is a sum of seven comparisons")[1]
                here.clear()
                here.update(enumerate(values))

            def body(j, it, v):
                if v == 0:
                    load_experts(j)
                wait_free(pe, xl_done, min(j + 3, SLOTS) if isinstance(j, int) else j + 3)
                if there(j + 3):
                    w = (v + 3) % RING
                    if v % BATCH == 0:
                        pe.wait_ge(gathered[w // BATCH], 16 * BATCH * (it + (v + 3) // RING) + 16 * BATCH)
                    nc.tensor.transpose(ps_xT[:, 0:P], rows[:, w, 0:D], ident[:]).then_inc(xT_done, 1)
                if there(j + 2):
                    a = (v + 2) % 2
                    e = bass.ds(here[v + 2 if not isinstance(j, int) or j >= 0 else v + 2 - RING], 1)
                    hi, lo = (keep[name][:, e, :].rearrange("p a c -> p (a c)") for name in ("w13_hi", "w13_lo"))
                    nc.tensor.matmul(ps_up[:, a, :], xh[a][:], hi, start=True, stop=False)
                    nc.tensor.matmul(ps_up[:, a, :], xl[a][:], hi, start=False, stop=False)
                    nc.tensor.matmul(ps_up[:, a, :], xh[a][:], lo, start=False, stop=True).then_inc(up_done, 1)
                if there(j + 1):
                    a = (v + 1) % 2
                    pe.wait_ge(hid_done, j + 2)
                    for c in range(2):
                        ins = nc.tensor.transpose(ps_hT[:, a, P * c:P * c + P], hid[a][:, P * c:P * c + P], ident[:])
                    ins.then_inc(hT_done, 1)
                if v % BATCH == 1 and there(j + 8):
                    look_up((j - 1) // BATCH + 3 if isinstance(j, int) else 2 * it + v // BATCH + 3)
                if there(j):
                    pe.wait_ge(hT_out, j + 1)
                    for c in range(2):
                        ins = nc.tensor.matmul(ps_y[:, v % 2, 0:D], hidT[v % 2][:, P * c:P * c + P],
                                               keep["w2"][:, bass.ds(here[v], 1), c, :].rearrange("p a d -> p (a d)"), start=(c == 0), stop=(c == 1))
                    ins.then_inc(down_done, 1)

            load_experts(0)
            pe.sem_inc(xT_done, RING)
            for q in range(2):
                look_up(q)
            steps(pe, body)


def combine(nc, keep, ff, y_rows, out_tiles):
    x_all = keep["x_all"]
    with ExitStack() as ctx:
        def sb(name, shape, dt=F32):
            return ctx.enter_context(nc.sbuf_tensor(name, shape, dt))

        def sem(name):
            return ctx.enter_context(nc.semaphore(name))

        def sems(name, n=2):
            return [sem(f"{name}{s}") for s in range(n)]

        GATHERS = TOP * SC
        CHUNKS_OUT = T // SC
        places = [[sb(f"places{s}_{i}", [P, 1], U32) for i in range(GATHERS)] for s in range(2)]
        routed = [sb(f"routed{s}", [P, GATHERS, D]) for s in range(2)]
        act_out = [sb(f"act_out_s{i}", [P, HALF]) for i in range(2)]
        hidT = [sb(f"hidT_s{i}", [P, HALF]) for i in range(2)]
        y = [sb(f"y_s{s}", [P, SC, D]) for s in range(2)]
        ps_up = ctx.enter_context(nc.psum_tensor("ps_up_s", [P, 2, 2, 512], F32))
        ps_y = ctx.enter_context(nc.psum_tensor("ps_y_s", [P, 2, 512], F32))

        places_ready, gathered, up_done, act_done, hid_done = sems("places_ready"), ff["output_gathers"], sems("up_done_s"), sems("act_done_s"), sems("hid_done_s")
        down_done, shared_added, first_added, y_out, y_free = sems("down_done_s"), sems("shared_added"), sems("first_added"), sems("y_out_s"), sems("y_free_s")
        passed = sem("passed4")
        block = ctx.enter_context(nc.Block())


        @block.sync
        def _(sp):
            for s in range(2):
                sp.sem_inc(y_free[s], 16)
            with sp.Fori(0, CHUNKS_OUT // 2) as it:
                for s in range(2):
                    sp.wait_ge(y_out[s], it + 2)
                    sp.dma_start(out_tiles[:, bass.ds(TB * it + SC * s, SC), :], y[s][:]).then_inc(y_free[s], 16)
            for s in range(2):
                sp.wait_ge(y_free[s], 16 * (CHUNKS_OUT // 2 + 1))

        @block.gpsimd
        def _(pool):
            with pool.Fori(0, CHUNKS_OUT // 2) as it:
                for s in range(2):
                    pool.wait_ge(places_ready[s], it + 1)
                    pool.wait_ge(y_out[s], it + 1)
                    pool.sem_inc(passed, 1)
                    for i in range(GATHERS):
                        nc.gpsimd.indirect_dma_start(routed[s][:, i, :], None, y_rows,
                                                     bass.IndirectOffsetOnAxis(ap=places[s][i][:, 0:1], axis=0)).then_inc(gathered[s], 16)

        @block.vector
        def _(dve):
            def put_places(it, s):
                for k in range(TOP):
                    for t in range(SC):
                        n = bass.ds(TB * it + SC * s + t, 1)
                        ins = nc.vector.tensor_copy(places[s][k * SC + t][:], ff["position"][:, k, n])
                ins.then_inc(places_ready[s], 1)

            def body(it, s, more):
                rows = x_all[:, bass.ds(TB * it + SC * s, SC), :]
                for c in range(2):
                    dve.wait_ge(act_done[c], 2 * it + s + 1)
                    dve.wait_ge(down_done[(s + 1) % 2], it + s + 0 + 1)
                    nc.vector.tensor_tensor(hidT[c][:], ps_up[:, c, 1, :], act_out[c][:], ALU.mult).then_inc(hid_done[c], 1)
                dve.wait_ge(down_done[s], it + 2)
                nc.vector.scalar_tensor_tensor(out=rows, in0=ps_y[:, s, :].rearrange("p (t d) -> p t d", t=SC), scalar=1.0 / (1 + TOP),
                                               in1=rows, op0=ALU.mult, op1=ALU.add).then_inc(shared_added[s], 1)
                dve.wait_ge(gathered[s], 16 * GATHERS * it + 16 * GATHERS)
                if more:
                    put_places(it + 1, s)
                dve.wait_ge(shared_added[s], it + 2)
                nc.vector.tensor_tensor(rows, rows, routed[s][:, 0:SC, :], ALU.add).then_inc(first_added[s], 1)
                dve.wait_ge(first_added[s], it + 1)
                dve.wait_ge(y_free[s], 16 * it + 16)
                nc.vector.tensor_tensor(y[s][:], rows, routed[s][:, SC:GATHERS, :], ALU.add).then_inc(y_out[s], 1)

            for s in range(2):
                dve.sem_inc(y_out[s], 1)
                put_places(0, s)
            with dve.Fori(0, CHUNKS_OUT // 2 - 1) as it:
                for s in range(2):
                    body(it, s, True)
            for s in range(2):
                body(CHUNKS_OUT // 2 - 1, s, False)

        @block.scalar
        def _(act):
            for c in range(2):
                act.sem_inc(hid_done[c], 1)
            with act.Fori(0, CHUNKS_OUT // 2) as it:
                for s in range(2):
                    for c in range(2):
                        act.wait_ge(up_done[c], 2 * it + s + 1)
                        act.wait_ge(hid_done[c], 2 * it + s + 1)
                        nc.scalar.activation(act_out[c][:], ps_up[:, c, 0, :], ACT.Silu).then_inc(act_done[c], 1)

        @block.tensor
        def _(pe):
            def up(it, s):
                for c in range(2):
                    pe.wait_ge(hid_done[c], 2 * it + s + 1)
                    for k in range(2):
                        col = FF * k + P * c
                        hi, lo = keep["w13_hi"][:, NE, col:col + P], keep["w13_lo"][:, NE, col:col + P]
                        xh, xl = (ff[n][:, bass.ds(it, 1), HALF * s:HALF * s + HALF].rearrange("p a c -> p (a c)") for n in ("x_hi", "x_lo"))
                        nc.tensor.matmul(ps_up[:, c, k, :], hi, xh, start=True, stop=False)
                        nc.tensor.matmul(ps_up[:, c, k, :], hi, xl, start=False, stop=False)
                        ins = nc.tensor.matmul(ps_up[:, c, k, :], lo, xh, start=False, stop=True)
                    ins.then_inc(up_done[c], 1)

            for s in range(2):
                pe.sem_inc(down_done[s], 1)
                pe.sem_inc(shared_added[s], 1)
            with pe.Fori(0, CHUNKS_OUT // 2) as it:
                for s in range(2):
                    up(it, s)
                    for c in range(2):
                        pe.wait_ge(hid_done[c], 2 * it + s + 2)
                    pe.wait_ge(shared_added[s], it + 1)
                    for t in range(SC):
                        for c in range(2):
                            ins = nc.tensor.matmul(ps_y[:, s, P * t:P * t + P], hidT[c][:, P * t:P * t + P],
                                                   keep["w2"][:, NE, c, :], start=(c == 0), stop=(c == 1))
                    ins.then_inc(down_done[s], 1)


_INS = ["L0_attn_x", "L0_attn_Wq", "L0_attn_bq", "L0_attn_Wk", "L0_attn_bk", "L0_attn_Wv", "L0_attn_bv", "L0_attn_Wo",
        "L0_attn_bo", "L0_ffn_Wg", "L0_ffn_Ws1", "L0_ffn_Ws3", "L0_ffn_Ws2", "L0_ffn_We1", "L0_ffn_We3", "L0_ffn_We2"]


def kernel(**inputs):
    import numpy as np
    import concourse.bacc as bacc
    from concourse.bass_utils import run_bass_kernel_spmd

    nc = bacc.Bacc("TRN2", target_bir_lowering=False, num_devices=1)
    arrays, args = {}, []
    for name in _INS:
        a = np.ascontiguousarray(inputs[name])
        arrays[f"in_{name}"] = a
        args.append(nc.dram_tensor(f"in_{name}", a.shape, mybir.dt.from_np(a.dtype), kind="ExternalInput").ap())
    out = nc.dram_tensor("out_x", (B, S, D), F32, kind="ExternalOutput").ap()
    layer_kernel(nc, *args, out)
    r = run_bass_kernel_spmd(nc, [arrays], core_ids=[0])
    return r.results[0]["out_x"]
```
